# Optimizing a Trainium2 kernel written in Bass

```python
import numpy as np
import jax
import jax.numpy as jnp

def _softmax(x, axis=-1):
    return jax.nn.softmax(x, axis=axis)

def _gelu(x):
    return jax.nn.gelu(x, approximate=True)

def _silu(x):
    return jax.nn.silu(x)

def _sigmoid(x):
    return jax.nn.sigmoid(x)

def _layernorm(x, axis=-1, eps=1e-05):
    m = jnp.mean(x, axis=axis, keepdims=True)
    v = jnp.var(x, axis=axis, keepdims=True)
    return (x - m) / jnp.sqrt(v + eps)

def _scatter_add(tgt, idx, src, axis=0):
    return tgt.at[idx].add(src)

def _segment_sum(src, seg, n):
    return jax.ops.segment_sum(src, seg, n)
kernel_name = 'mk_xattn_ffn_d2_seqx_r4_d41930'

def setup_inputs(seed: int=0):
    np.random.seed(seed)
    _w = jnp.asarray

    def _rec_inputs():
        import jax
        import jax.numpy as jnp
        _rk = jax.random.key(seed)
        x = -0.0002928 + 1 * jax.random.normal(jax.random.fold_in(_rk, 1), (8, 256, 256), jnp.float32)
        _lenS = 256 - jax.random.randint(jax.random.fold_in(_rk, 7), (8,), 0, max(1, 256 // 4) + 1, jnp.int32)
        _lenS2 = 256 - jax.random.randint(jax.random.fold_in(_rk, 8), (8,), 0, max(1, 256 // 4) + 1, jnp.int32)
        _ctx_1024P = jax.random.normal(jax.random.fold_in(_rk, 11), (8, 16, 256), jnp.float32)
        _ctx_1024c = jax.random.dirichlet(jax.random.fold_in(_rk, 511), 0.3 * jnp.ones((16,), jnp.float32), (8, 256))
        _ctx_1024t = jnp.einsum('bsk,bkd->bsd', _ctx_1024c, _ctx_1024P)
        _ctx_1024t = _ctx_1024t * jax.lax.rsqrt(jnp.mean(jnp.square(_ctx_1024t)) + 1e-12) * 0.953939
        ctx_1024 = -1.39393e-06 + 0.999914 * (_ctx_1024t + 0.3 * jax.random.normal(jax.random.fold_in(_rk, 611), (8, 256, 256), jnp.float32))
        return (x, ctx_1024)
    x, ctx_1024 = _rec_inputs()

    def _L0_xattn_setup():
        import jax, jax.numpy as jnp
        import numpy as np
        D_MODEL = 256
        N_HEADS = 16
        HEAD = D_MODEL // N_HEADS
        D_FF = 1024
        LN_EPS = 1e-05

        def _layernorm(x, g, b):
            mu = jnp.mean(x, axis=-1, keepdims=True)
            var = jnp.mean(jnp.square(x - mu), axis=-1, keepdims=True)
            return (x - mu) * jax.lax.rsqrt(var + LN_EPS) * g + b

        def _mha(q_in, k_in, v_in, Wq, Wk, Wv, bv, causal):
            q = jnp.einsum('bsd,hde->bhse', q_in, Wq)
            k = jnp.einsum('btd,hde->bhte', k_in, Wk)
            v = jnp.einsum('btd,hde->bhte', v_in, Wv) + bv[None, :, None, :]
            scale = HEAD ** (-0.5)
            scores = jnp.einsum('bhse,bhte->bhst', q, k) * scale
            if causal:
                S, T = (scores.shape[-2], scores.shape[-1])
                mask = jnp.tril(jnp.ones((S, T), dtype=bool))
                scores = jnp.where(mask, scores, -jnp.inf)
            p = jax.nn.softmax(scores, axis=-1)
            o = jnp.einsum('bhst,bhte->bhse', p, v)
            B, H, S, E = o.shape
            return o.transpose(0, 2, 1, 3).reshape(B, S, H * E)
        key = jax.random.key(seed)
        ks = jax.random.split(key, 20)
        B, S, T = (2, 512, 512)
        sd = D_MODEL ** (-0.5)
        inp = {'input_tensor': jax.random.normal(ks[0], (B, S, D_MODEL), jnp.float32), 'encoder_output': jax.random.normal(ks[1], (B, T, D_MODEL), jnp.float32), 'Wq1': jax.random.normal(ks[2], (N_HEADS, D_MODEL, HEAD), jnp.float32) * sd, 'Wk1': jax.random.normal(ks[3], (N_HEADS, D_MODEL, HEAD), jnp.float32) * sd, 'Wv1': jax.random.normal(ks[4], (N_HEADS, D_MODEL, HEAD), jnp.float32) * sd, 'bv1': jnp.zeros((N_HEADS, HEAD), jnp.float32), 'Wq2': jax.random.normal(ks[5], (N_HEADS, D_MODEL, HEAD), jnp.float32) * sd, 'Wk2': jax.random.normal(ks[6], (N_HEADS, D_MODEL, HEAD), jnp.float32) * sd, 'Wv2': jax.random.normal(ks[7], (N_HEADS, D_MODEL, HEAD), jnp.float32) * sd, 'bv2': jnp.zeros((N_HEADS, HEAD), jnp.float32), 'g1': jnp.ones((D_MODEL,), jnp.float32), 'be1': jnp.zeros((D_MODEL,), jnp.float32), 'g2': jnp.ones((D_MODEL,), jnp.float32), 'be2': jnp.zeros((D_MODEL,), jnp.float32), 'g3': jnp.ones((D_MODEL,), jnp.float32), 'be3': jnp.zeros((D_MODEL,), jnp.float32), 'Wf1': jax.random.normal(ks[8], (D_MODEL, D_FF), jnp.float32) * sd, 'bf1': jnp.zeros((D_FF,), jnp.float32), 'Wf2': jax.random.normal(ks[9], (D_FF, D_MODEL), jnp.float32) * D_FF ** (-0.5), 'bf2': jnp.zeros((D_MODEL,), jnp.float32)}
        return inp
    _L0_xattn_all = _L0_xattn_setup()
    _L0_xattn_in = {k: v for k, v in _L0_xattn_all.items() if k in ('Wq1', 'Wk1', 'Wv1', 'bv1', 'Wq2', 'Wk2', 'Wv2', 'bv2', 'g1', 'be1', 'g2', 'be2', 'g3', 'be3', 'Wf1', 'bf1', 'Wf2', 'bf2')}
    del _L0_xattn_all

    def _L0_ffn_setup():
        import jax, jax.numpy as jnp
        import numpy as np
        TOP_K = 2
        key = jax.random.key(seed)
        ks = jax.random.split(key, 5)
        B, S, D, H, E = (1, 512, 256, 896, 8)
        sd = 1.0 / np.sqrt(D)
        sh = 1.0 / np.sqrt(H)
        return {'x': jax.random.normal(ks[0], (B, S, D), dtype=jnp.float32), 'gate_w': jax.random.normal(ks[1], (E, D), dtype=jnp.float32) * sd, 'W1': jax.random.normal(ks[2], (E, H, D), dtype=jnp.float32) * sd, 'W2': jax.random.normal(ks[3], (E, D, H), dtype=jnp.float32) * sh, 'W3': jax.random.normal(ks[4], (E, H, D), dtype=jnp.float32) * sd}
    _L0_ffn_all = _L0_ffn_setup()
    _L0_ffn_in = {k: v for k, v in _L0_ffn_all.items() if k in ('gate_w', 'W1', 'W2', 'W3')}
    del _L0_ffn_all

    def _L1_xattn_setup():
        import jax, jax.numpy as jnp
        import numpy as np
        N_HEAD = 16
        key = jax.random.key(seed)
        ks = jax.random.split(key, 5)
        b, l, d = (4, 512, 256)
        dh = d // N_HEAD
        return {'q': jax.random.normal(ks[0], (b, l, d), dtype=jnp.float32), 'kv': jax.random.normal(ks[1], (b, l, d), dtype=jnp.float32), 'Wq': jax.random.normal(ks[2], (d, d), dtype=jnp.float32) * 0.02, 'Wkv': jax.random.normal(ks[3], (2 * dh, d), dtype=jnp.float32) * 0.02, 'Wc': jax.random.normal(ks[4], (d, d), dtype=jnp.float32) * 0.02}
    _L1_xattn_all = _L1_xattn_setup()
    _L1_xattn_in = {k: v for k, v in _L1_xattn_all.items() if k in ('Wq', 'Wkv', 'Wc')}
    del _L1_xattn_all

    def _L1_ffn_setup():
        import jax, jax.numpy as jnp
        import numpy as np
        TOP_K = 2
        key = jax.random.key(seed)
        ks = jax.random.split(key, 8)
        B, S, D = (2, 512, 256)
        N_r, N_s = (16, 2)
        u = jax.random.normal(ks[0], (B, S, D), dtype=jnp.float32)
        centroids = jax.random.normal(ks[1], (N_r, D), dtype=jnp.float32)
        expert_biases = jnp.zeros((N_r,), dtype=jnp.float32)
        Wr = jax.random.normal(ks[2], (N_r, D, D), dtype=jnp.float32) * (1.0 / np.sqrt(D))
        br = jax.random.normal(ks[3], (N_r, D), dtype=jnp.float32) * 0.01
        Ws = jax.random.normal(ks[4], (N_s, D, D), dtype=jnp.float32) * (1.0 / np.sqrt(D))
        bs = jax.random.normal(ks[5], (N_s, D), dtype=jnp.float32) * 0.01
        return {'u': u, 'centroids': centroids, 'expert_biases': expert_biases, 'Wr': Wr, 'br': br, 'Ws': Ws, 'bs': bs}
    _L1_ffn_all = _L1_ffn_setup()
    _L1_ffn_in = {k: v for k, v in _L1_ffn_all.items() if k in ('centroids', 'expert_biases', 'Wr', 'br', 'Ws', 'bs')}
    del _L1_ffn_all
    return {'x': x, 'ctx_1024': ctx_1024, 'L0_xattn_Wq1': _L0_xattn_in['Wq1'], 'L0_xattn_Wk1': _L0_xattn_in['Wk1'], 'L0_xattn_Wv1': _L0_xattn_in['Wv1'], 'L0_xattn_bv1': _L0_xattn_in['bv1'], 'L0_xattn_Wq2': _L0_xattn_in['Wq2'], 'L0_xattn_Wk2': _L0_xattn_in['Wk2'], 'L0_xattn_Wv2': _L0_xattn_in['Wv2'], 'L0_xattn_bv2': _L0_xattn_in['bv2'], 'L0_xattn_g1': _L0_xattn_in['g1'], 'L0_xattn_be1': _L0_xattn_in['be1'], 'L0_xattn_g2': _L0_xattn_in['g2'], 'L0_xattn_be2': _L0_xattn_in['be2'], 'L0_xattn_g3': _L0_xattn_in['g3'], 'L0_xattn_be3': _L0_xattn_in['be3'], 'L0_xattn_Wf1': _L0_xattn_in['Wf1'], 'L0_xattn_bf1': _L0_xattn_in['bf1'], 'L0_xattn_Wf2': _L0_xattn_in['Wf2'], 'L0_xattn_bf2': _L0_xattn_in['bf2'], 'L0_ffn_gate_w': _L0_ffn_in['gate_w'], 'L0_ffn_W1': _L0_ffn_in['W1'], 'L0_ffn_W2': _L0_ffn_in['W2'], 'L0_ffn_W3': _L0_ffn_in['W3'], 'L1_xattn_Wq': _L1_xattn_in['Wq'], 'L1_xattn_Wkv': _L1_xattn_in['Wkv'], 'L1_xattn_Wc': _L1_xattn_in['Wc'], 'L1_ffn_centroids': _L1_ffn_in['centroids'], 'L1_ffn_expert_biases': _L1_ffn_in['expert_biases'], 'L1_ffn_Wr': _L1_ffn_in['Wr'], 'L1_ffn_br': _L1_ffn_in['br'], 'L1_ffn_Ws': _L1_ffn_in['Ws'], 'L1_ffn_bs': _L1_ffn_in['bs']}

def reference(x, ctx_1024, L0_xattn_Wq1, L0_xattn_Wk1, L0_xattn_Wv1, L0_xattn_bv1, L0_xattn_Wq2, L0_xattn_Wk2, L0_xattn_Wv2, L0_xattn_bv2, L0_xattn_g1, L0_xattn_be1, L0_xattn_g2, L0_xattn_be2, L0_xattn_g3, L0_xattn_be3, L0_xattn_Wf1, L0_xattn_bf1, L0_xattn_Wf2, L0_xattn_bf2, L0_ffn_gate_w, L0_ffn_W1, L0_ffn_W2, L0_ffn_W3, L1_xattn_Wq, L1_xattn_Wkv, L1_xattn_Wc, L1_ffn_centroids, L1_ffn_expert_biases, L1_ffn_Wr, L1_ffn_br, L1_ffn_Ws, L1_ffn_bs):
    import jax
    import jax.numpy as jnp

    def _L0_xattn_ref(input_tensor, encoder_output, Wq1, Wk1, Wv1, bv1, Wq2, Wk2, Wv2, bv2, g1, be1, g2, be2, g3, be3, Wf1, bf1, Wf2, bf2):
        import jax, jax.numpy as jnp
        import numpy as np
        D_MODEL = 256
        N_HEADS = 16
        HEAD = D_MODEL // N_HEADS
        D_FF = 1024
        LN_EPS = 1e-05

        def _layernorm(x, g, b):
            mu = jnp.mean(x, axis=-1, keepdims=True)
            var = jnp.mean(jnp.square(x - mu), axis=-1, keepdims=True)
            return (x - mu) * jax.lax.rsqrt(var + LN_EPS) * g + b

        def _mha(q_in, k_in, v_in, Wq, Wk, Wv, bv, causal):
            q = jnp.einsum('bsd,hde->bhse', q_in, Wq)
            k = jnp.einsum('btd,hde->bhte', k_in, Wk)
            v = jnp.einsum('btd,hde->bhte', v_in, Wv) + bv[None, :, None, :]
            scale = HEAD ** (-0.5)
            scores = jnp.einsum('bhse,bhte->bhst', q, k) * scale
            if causal:
                S, T = (scores.shape[-2], scores.shape[-1])
                mask = jnp.tril(jnp.ones((S, T), dtype=bool))
                scores = jnp.where(mask, scores, -jnp.inf)
            p = jax.nn.softmax(scores, axis=-1)
            o = jnp.einsum('bhst,bhte->bhse', p, v)
            B, H, S, E = o.shape
            return o.transpose(0, 2, 1, 3).reshape(B, S, H * E)
        x = input_tensor
        sa = _mha(x, x, x, Wq1, Wk1, Wv1, bv1, causal=True)
        x = _layernorm(sa + input_tensor, g1, be1)
        ca = _mha(x, encoder_output, encoder_output, Wq2, Wk2, Wv2, bv2, causal=False)
        x = _layernorm(x + ca, g2, be2)
        ffn = jax.nn.relu(x @ Wf1 + bf1) @ Wf2 + bf2
        x = _layernorm(x + ffn, g3, be3)
        return x

    def _L0_ffn_ref(x, gate_w, W1, W2, W3):
        import jax, jax.numpy as jnp
        import numpy as np
        TOP_K = 2
        orig_shape = x.shape
        D = x.shape[-1]
        xf = x.reshape(-1, D)
        scores = xf @ gate_w.T
        expert_weights, expert_indices = jax.lax.top_k(scores, TOP_K)
        expert_weights = jax.nn.softmax(expert_weights, axis=-1)
        h1 = jnp.einsum('td,ehd->teh', xf, W1)
        h3 = jnp.einsum('td,ehd->teh', xf, W3)
        mid = jax.nn.silu(h1) * h3
        out_all = jnp.einsum('teh,edh->ted', mid, W2)
        sel = jnp.take_along_axis(out_all, expert_indices[:, :, None], axis=1)
        y = jnp.sum(sel * expert_weights[:, :, None], axis=1)
        return y.reshape(orig_shape)

    def _L1_xattn_ref(q, kv, Wq, Wkv, Wc):
        import jax, jax.numpy as jnp
        import numpy as np
        N_HEAD = 16
        b, l, d = q.shape
        h = N_HEAD
        dh = d // h
        qp = jnp.einsum('bld,ed->ble', q, Wq)
        scores = jnp.einsum('bld,bmd->blm', qp, kv)
        idx = jnp.argmax(scores, axis=-1)
        mem = jnp.take_along_axis(kv, idx[..., None], axis=1)
        mkv = jnp.einsum('bld,ed->ble', mem, Wkv)
        mk, mv = jnp.split(mkv, 2, axis=-1)
        qh = qp.reshape(b, l, h, dh).transpose(0, 2, 1, 3)
        scale = 1.0 / np.sqrt(dh).astype(np.float32)
        logits = jnp.einsum('bhld,bmd->bhlm', qh, mk) * scale
        attn = jax.nn.softmax(logits, axis=-1)
        out = jnp.einsum('bhlm,bmd->bhld', attn, mv)
        out = out.transpose(0, 2, 1, 3).reshape(b, l, d)
        return jnp.einsum('bld,ed->ble', out, Wc)

    def _L1_ffn_ref(u, centroids, expert_biases, Wr, br, Ws, bs):
        import jax, jax.numpy as jnp
        import numpy as np
        TOP_K = 2
        N_r = centroids.shape[0]
        N_s = Ws.shape[0]
        raw_scores = jnp.einsum('bsd,ed->bse', u, centroids)
        s = jax.nn.softmax(raw_scores + expert_biases, axis=-1)
        topk_vals, topk_idx = jax.lax.top_k(s, TOP_K)
        g_topk = jnp.sum(jax.nn.one_hot(topk_idx, N_r, dtype=s.dtype) * topk_vals[..., None], axis=-2)
        xe = jnp.einsum('bsd,eod->bseo', u, Wr) + br
        routed = jnp.einsum('bse,bseo->bso', g_topk, xe)
        shared = (jnp.einsum('bsd,eod->bso', u, Ws) + jnp.sum(bs, axis=0)) / N_s
        return u + routed + shared
    x = x + _L0_xattn_ref(_layernorm(x, axis=-1), ctx_1024, L0_xattn_Wq1, L0_xattn_Wk1, L0_xattn_Wv1, L0_xattn_bv1, L0_xattn_Wq2, L0_xattn_Wk2, L0_xattn_Wv2, L0_xattn_bv2, L0_xattn_g1, L0_xattn_be1, L0_xattn_g2, L0_xattn_be2, L0_xattn_g3, L0_xattn_be3, L0_xattn_Wf1, L0_xattn_bf1, L0_xattn_Wf2, L0_xattn_bf2)
    x = x + _L0_ffn_ref(_layernorm(x, axis=-1), L0_ffn_gate_w, L0_ffn_W1, L0_ffn_W2, L0_ffn_W3)
    x = x + _L1_xattn_ref(_layernorm(x, axis=-1), ctx_1024, L1_xattn_Wq, L1_xattn_Wkv, L1_xattn_Wc)
    x = x + _L1_ffn_ref(_layernorm(x, axis=-1), L1_ffn_centroids, L1_ffn_expert_biases, L1_ffn_Wr, L1_ffn_br, L1_ffn_Ws, L1_ffn_bs)
    return x

_drawn_inputs = setup_inputs


def setup_inputs(seed=0):
    import zlib

    import numpy as np

    out = dict(_drawn_inputs(seed))
    spreads = {'L0_xattn_bv1': (0.0, 0.1),
     'L0_xattn_bv2': (0.0, 0.1),
     'L0_xattn_g1': (1.0, 0.2),
     'L0_xattn_be1': (0.0, 0.1),
     'L0_xattn_g2': (1.0, 0.2),
     'L0_xattn_be2': (0.0, 0.1),
     'L0_xattn_g3': (1.0, 0.2),
     'L0_xattn_be3': (0.0, 0.1),
     'L0_xattn_bf1': (0.0, 0.1),
     'L0_xattn_bf2': (0.0, 0.1),
     'L1_ffn_expert_biases': (0.0, 0.8)}
    factors = {'L1_xattn_Wq': 12.707, 'L1_ffn_br': 8.0, 'L1_ffn_bs': 26.908}
    for name, (base, spread) in spreads.items():
        noise = np.random.default_rng([zlib.crc32(name.encode()), seed]).standard_normal(out[name].shape)
        drawn = base * np.exp(spread * noise) if base else spread * noise
        out[name] = jnp.asarray(drawn.astype(out[name].dtype))
    for name, factor in factors.items():
        out[name] = (out[name] * factor).astype(out[name].dtype)
    return out
```

```python
import concourse.bass as bass
from concourse import mybir
from contextlib import ExitStack

F32 = mybir.dt.float32
F16 = mybir.dt.float16
BF16 = mybir.dt.bfloat16
U32 = mybir.dt.uint32
I32 = mybir.dt.int32
ALU = mybir.AluOpType
ACT = mybir.ActivationFunctionType
AX = mybir.AxisListType

P = 128
BATCHES = 8
SEQ = 256
TOKENS = BATCHES * SEQ
D = 256
TT = SEQ // P
DC = D // P
HEADS = 16
HD = D // HEADS
VW = 32
PAIRS = HEADS // 2
GROUP = P // VW
GROUPS = HEADS // GROUP
KEY_WORDS = 32
MEM_WORDS = KEY_WORDS + VW
SCALE = HD ** -0.5
EPS = 1e-5
MASKED = -1e30
BANK = 512
STACK = 3 * HD
ROWS = STACK + 1


class Turn:

    def __init__(self, pairs, offset, count=BATCHES):
        self.pairs, self.offset, self.count = pairs, offset, count
        self.n = pairs * 2 + offset
        self.slot = offset % 2
        self.turn = pairs + offset // 2

    def plus(self, k):
        return Turn(self.pairs, self.offset + k, self.count)

    def within(self):
        return not isinstance(self.n, int) or 0 <= self.n < self.count

    def before(self, k):
        return not isinstance(self.n, int) or self.n >= k


def pipeline(eng, step, lead, tail, count=BATCHES):
    first, last = max((tail + 1) // 2, 1), (count - lead) // 2
    if last - first < 2:
        last = first
    for n in range(-lead, 2 * first):
        step(Turn(0, n, count))
    if last > first:
        with eng.Fori(first, last) as pairs:
            for k in range(2):
                step(Turn(pairs, k, count))
    for n in range(2 * last, count + tail):
        step(Turn(last, n - 2 * last, count))


class Constants:

    def __init__(self, sb):
        self.ident, self.ident_bf, self.ident_h = sb("ident", [P, P]), sb("ident_bf", [P, P], BF16), sb("ident_h", [P, P], F16)
        self.mask_st, self.mask_ts = sb("mask_st", [P, P], BF16), sb("mask_ts", [P, P], BF16)
        self.minus_half, self.eps = sb("minus_half", [P, TT]), sb("eps", [P, TT])
        self.zeros = sb("zeros", [P, D])
        self.counted = []


def semaphore(nc, c, ctx, name):
    sem = ctx.enter_context(nc.semaphore(name))
    c.counted.append(sem.num)
    return sem


def clear_counted(nc, c):
    with nc.Block() as block:
        @block.gpsimd
        def _(pool):
            for num in c.counted:
                pool.sem_clear(range(num, num + 1))
    c.counted.clear()


def constants(nc, c, done, xs, zeroed):
    with nc.Block() as block:
        @block.sync
        def _(sp):
            sp.wait_ge(done, 8)
            sp.dma_start(xs.rearrange("(n p) d -> p n d", p=P), c.zeros[:, :].unsqueeze(1).to_broadcast(
                [P, xs.shape[0] // P, D])).then_inc(zeroed, 16)

        @block.gpsimd
        def _(pool):
            nc.gpsimd.memset(c.ident[:, :], 0.0).then_inc(done, 1)
            nc.gpsimd.memset(c.ident_bf[:, :], 0.0).then_inc(done, 1)
            nc.gpsimd.memset(c.mask_st[:, :], 0.0).then_inc(done, 1)
            nc.gpsimd.memset(c.mask_ts[:, :], 0.0).then_inc(done, 1)
            nc.gpsimd.memset(c.minus_half[:, :], -0.5).then_inc(done, 1)
            nc.gpsimd.memset(c.eps[:, :], EPS).then_inc(done, 1)
            nc.gpsimd.memset(c.zeros[:, :], 0.0).then_inc(done, 1)
            nc.gpsimd.memset(c.ident_h[:, :], 0.0).then_inc(done, 1)
            pool.wait_ge(done, 8)
            for m in (c.ident, c.ident_bf, c.ident_h):
                nc.gpsimd.affine_select(out=m[:, :], in_=m[:, :], compare_op=ALU.not_equal, fill=1.0, base=0,
                                        pattern=[[-1, P]], channel_multiplier=1).then_inc(done, 1)
            nc.gpsimd.affine_select(out=c.mask_st[:, :], in_=c.mask_st[:, :], compare_op=ALU.is_ge, fill=MASKED,
                                    base=0, pattern=[[-1, P]], channel_multiplier=1).then_inc(done, 1)
            nc.gpsimd.affine_select(out=c.mask_ts[:, :], in_=c.mask_ts[:, :], compare_op=ALU.is_ge, fill=MASKED,
                                    base=0, pattern=[[1, P]], channel_multiplier=-1).then_inc(done, 1)
            pool.wait_ge(done, 13)


def normalize_input(nc, c, x, out):
    with ExitStack() as ctx:
        def sb(name, shape, dt=F32):
            return ctx.enter_context(nc.sbuf_tensor(name, shape, dt))

        def sem(name):
            return semaphore(nc, c, ctx, name)

        xt = [sb(f"ln_x{k}", [P, TT, D]) for k in range(2)]
        yt = [sb(f"ln_y{k}", [P, TT, D]) for k in range(2)]
        stats = [sb(f"ln_stats{k}", [P, TT, 6]) for k in range(2)]
        mv = [sb(f"ln_mv{k}", [P, TT, 2]) for k in range(2)]
        var = [sb(f"ln_var{k}", [P, TT]) for k in range(2)]
        rstd = [sb(f"ln_rstd{k}", [P, TT]) for k in range(2)]
        loaded = [sem(f"ln_loaded{k}") for k in range(2)]
        stored = [sem(f"ln_stored{k}") for k in range(2)]
        stats_done, aggregated, var_done = sem("ln_stats_done"), sem("ln_aggregated"), sem("ln_var_done")
        rstd_done, applied = sem("ln_rstd_done"), sem("ln_applied")
        src = x.rearrange("(b t p) d -> b p t d", b=BATCHES, p=P)

        with nc.Block() as block:
            @block.sync
            def _(sp):
                def step(t):
                    if t.within():
                        if t.before(2):
                            sp.wait_ge(applied, TT * (t.n - 1))
                        sp.dma_start(xt[t.slot][:, :, :], src[t.n]).then_inc(loaded[t.slot], 16)
                    u = t.plus(-2)
                    if u.within():
                        sp.wait_ge(applied, TT * (u.n + 1))
                        sp.dma_start(out[u.n], yt[u.slot][:, :, :]).then_inc(stored[u.slot], 16)
                for n in range(BATCHES + 2):
                    step(Turn(0, n))
                for k in range(2):
                    sp.wait_ge(stored[k], 16 * (BATCHES // 2))

            @block.vector
            def _(dve):
                def step(t):
                    if t.within():
                        dve.wait_ge(loaded[t.slot], 16 * (t.turn + 1))
                        for k in range(TT):
                            nc.vector.bn_stats(stats[t.slot][:, k, :], xt[t.slot][:, k, :]).then_inc(stats_done, 1)
                        dve.wait_ge(stats_done, TT * (t.n + 1))
                        for k in range(TT):
                            nc.vector.bn_aggr(mv[t.slot][:, k, :], stats[t.slot][:, k, :]).then_inc(aggregated, 1)
                    u = t.plus(-1)
                    if u.within():
                        dve.wait_ge(rstd_done, u.n + 1)
                        if u.before(2):
                            dve.wait_ge(stored[u.slot], 16 * u.turn)
                        for k in range(TT):
                            nc.vector.tensor_scalar(yt[u.slot][:, k, :], xt[u.slot][:, k, :], mv[u.slot][:, k, 0:1],
                                                    rstd[u.slot][:, k:k + 1], ALU.subtract, ALU.mult).then_inc(applied, 1)
                for n in range(BATCHES + 1):
                    step(Turn(0, n))

            @block.gpsimd
            def _(pool):
                for n in range(BATCHES):
                    t = Turn(0, n)
                    pool.wait_ge(aggregated, TT * (n + 1))
                    nc.gpsimd.tensor_scalar(var[t.slot][:, :], mv[t.slot][:, :, 1], EPS, None, ALU.add).then_inc(var_done, 1)
                    pool.wait_ge(var_done, n + 1)
                    nc.gpsimd.tensor_tensor(rstd[t.slot][:, :], var[t.slot][:, :], c.minus_half[:, :],
                                            ALU.pow).then_inc(rstd_done, 1)


def attention(nc, c, name, causal, hin, weights, out, ctx_t=None, bias_v=None, gain=None, shift=None, memory=None):
    with ExitStack() as ctx:
        def sb(nm, shape, dt=F32):
            return ctx.enter_context(nc.sbuf_tensor(f"{name}_{nm}", shape, dt))

        def ps(nm, shape, dt=F32):
            return ctx.enter_context(nc.psum_tensor(f"{name}_{nm}", shape, dt))

        def sem(nm):
            return semaphore(nc, c, ctx, f"{name}_{nm}")

        def ring(make, nm, *args, n=2):
            return [make(f"{nm}{k}", *args) for k in range(n)]

        def dram(nm, shape, dt):
            return nc.dram_tensor(f"{name}_{nm}", shape, dt, kind="Internal").ap()

        mem = memory is not None
        cross = ctx_t is not None and not mem
        normed_out = gain is not None
        kv_heads = 1 if mem else HEADS
        keys_of = [P, SEQ] if causal else [SEQ, SEQ]
        width = sum(keys_of)
        q_of = [(0, SEQ), (P if causal else 0, SEQ)]

        w = [sb(f"w{k}", [P, DC, D]) for k in range(len(weights))]
        h_in = ring(sb, "h_in", [P, TT, D])
        h_t = ring(sb, "h_t", [P, DC, SEQ])
        src_t = ring(sb, "src_t", [P, DC, SEQ]) if ctx_t is not None else h_t
        q_hl = ring(sb, "q_hl", [P, 2, DC, SEQ], F16)
        q_st = ring(sb, "q_st", [64, HEADS, SEQ], F16)
        k_st = ring(sb, "k_st", [64, kv_heads, SEQ], F16)
        if mem:
            q_t = ring(sb, "q_t", [P, DC, SEQ])
            best = sb("best", [P, TT, 8])
            best_at = sb("best_at", [P, TT, 8], U32)
            best_row = ring(sb, "best_row", [P, TT], I32)
            first_row = sb("first_row", [P, TT])
            rows = ring(sb, "rows", [P, TT, MEM_WORDS])
        else:
            k_hl = ring(sb, "k_hl", [P, 2, DC, SEQ], F16)
            v = ring(sb, "v", [P, TT, HEADS, VW])
            bv = sb("bv", [P, D])
        if normed_out:
            g, be = sb("gain", [P, D]), sb("shift", [P, D])
            h_res = ring(sb, "h_res", [P, TT, D])
            total = sb("total", [P, TT, D])
            stats, mv = sb("stats", [P, TT, 6]), sb("mv", [P, TT, 2])
            var, rstd = sb("var", [P, TT]), sb("rstd", [P, TT])
            normed = sb("normed", [P, TT, D])
        neg_m = ring(sb, "neg_m", [P, TT, HEADS])
        m_row = ring(sb, "m_row", [HEADS, SEQ], F16)
        probs = ring(sb, "probs", [P, 2, width], n=4)
        o_t = sb("o_t", [P, GROUPS, SEQ])
        recip = sb("recip", [P, HEADS])
        att = ring(sb, "att", [P, TT, HEADS, HD])
        result = ring(sb, "result", [P, TT, D]) if normed_out else [x[:, :, :, :].rearrange("p t h e -> p t (h e)") for x in att]

        ps_s = ring(ps, "ps_s", [P, TT, SEQ])
        ps_t = ps("ps_t", [P, 2, BANK])
        ps_o = ring(ps, "ps_o", [P, BANK])
        ps_f = ps("ps_f", [P, 2, SEQ])
        ps_x = ps("ps_x", [P, HEADS, VW])

        q_dram = dram("q_dram", [BATCHES, 2, D, SEQ], F16)
        k_dram = None if mem else dram("k_dram", [BATCHES, 2, D, SEQ], F16)

        params_loaded, ones_set = sem("params_loaded"), sem("ones_set")
        h_in_loaded, src_loaded = ring(sem, "h_in_loaded"), ring(sem, "src_loaded")
        f_filled, f_emptied = sem("f_filled"), sem("f_emptied")
        x_filled, x_emptied = sem("x_filled"), sem("x_emptied")
        hi_done, lo_done = sem("hi_done"), sem("lo_done")
        q_stored, k_stored = ring(sem, "q_stored"), ring(sem, "k_stored")
        stack_loaded, m_loaded = ring(sem, "stack_loaded"), ring(sem, "m_loaded")
        s_filled, s_emptied = sem("s_filled"), sem("s_emptied")
        m_row_done = sem("m_row_done")
        t_filled, t_emptied = sem("t_filled"), sem("t_emptied")
        v_done, pv_done, o_copied = sem("v_done"), sem("pv_done"), sem("o_copied")
        recip_done, divided = sem("recip_done"), sem("divided")
        h_res_loaded, h_res_free = ring(sem, "h_res_loaded"), sem("h_res_free")
        tail_step, var_done, rstd_done = sem("tail_step"), sem("var_done"), sem("rstd_done")
        normed_free, affine_done = sem("normed_free"), sem("affine_done")
        result_stored = ring(sem, "result_stored")
        best_step, row_done, rows_loaded = sem("best_step"), sem("row_done"), ring(sem, "rows_loaded")
        ordered, gathering, turning = sem("ordered"), sem("gathering"), sem("turning")
        KV = 1 if mem else 2
        STACK_DMAS, TAIL_STEPS, BEST_STEPS = 3 * KV, 6, 3
        params = len(weights) + (0 if mem else 1) + (2 if normed_out else 0)

        F_FILLS = (2, 2, 2) if mem else (2, 2, 2, 1)
        F_TURN, F_Q, F_K, F_V = range(4)
        F_BEST = F_K
        X_FILLS = (-1, -1, 1, 1) if mem else (-1, -1, 1)
        X_OUT, X_KEYS, X_MAX = 0, 2, len(X_FILLS) - 1

        def fills(kinds, t, k):
            n = 0
            for j, off in enumerate(kinds):
                m = t.n + off + (1 if j < k else 0)
                n += min(max(m, 0), BATCHES) if isinstance(m, int) else m
            return n

        with nc.Block() as block:
            @block.sync
            def _(sp):
                for dst, src in zip(w, weights):
                    sp.dma_start(dst[:, :, :], src.rearrange("(c p) f -> p c f", p=P)).then_inc(params_loaded, 16)
                for dst, src in (() if mem else ((bv, bias_v),)) + (((g, gain), (be, shift)) if normed_out else ()):
                    sp.dma_start(dst[:, :], src.partition_broadcast(P)).then_inc(params_loaded, 16)

                def load_h(t):
                    if t.before(2):
                        sp.wait_ge(f_filled, fills(F_FILLS, t.plus(-4), F_TURN) + 1)
                    sp.dma_start(h_in[t.slot][:, :, :], hin[t.n]).then_inc(h_in_loaded[t.slot], 16)

                def load_src(t):
                    if t.before(2):
                        sp.wait_ge(f_filled, fills(F_FILLS, t.plus(-4 if mem else -3), F_BEST if mem else F_V) + 1)
                    sp.dma_start(src_t[t.slot][:, :, :], ctx_t[:, bass.ds(t.n * SEQ, SEQ)].rearrange(
                        "(c p) s -> p c s", p=P)).then_inc(src_loaded[t.slot], 16)

                def store(t, hl, to, stored, k):
                    sp.wait_ge(lo_done, KV * t.n + k + 1)
                    sp.dma_start(to[t.n].rearrange("l (c p) s -> p (l c) s", p=P),
                                 hl[t.slot][:, :, :, :].rearrange("p l c s -> p (l c) s")).then_inc(stored[t.slot], 16)

                def load_stacks(t):
                    if t.before(2):
                        sp.wait_ge(t_filled, PAIRS * (t.n - 1))
                    if not mem and isinstance(t.n, int) and t.n < 2:
                        sp.wait_ge(ones_set, t.n + 1)
                    for frm, stored, to, parts in ((q_dram, q_stored, q_st, (0, 1, 0)), (k_dram, k_stored, k_st, (0, 0, 1)))[:KV]:
                        sp.wait_ge(stored[t.slot], 16 * (t.turn + 1))
                        for row, part in enumerate(parts):
                            sp.dma_start(to[t.slot][row * HD:(row + 1) * HD, :, :],
                                         frm[t.n, part].rearrange("(h e) s -> e h s", e=HD)).then_inc(stack_loaded[t.slot], 16)

                def load_m(t):
                    sp.wait_ge(m_row_done, t.n + 1)
                    sp.dma_start(q_st[t.slot][STACK:ROWS, :, :], m_row[t.slot][:, :]).then_inc(m_loaded[t.slot], 16)

                def step(t):
                    nxt, new, ahead, old = t.plus(1), t.plus(2), t.plus(3), t.plus(-1)
                    if nxt.within():
                        load_stacks(nxt)
                    if ahead.within():
                        load_h(ahead)
                    if normed_out and t.within():
                        if t.before(2):
                            sp.wait_ge(h_res_free, t.n - 1)
                        sp.dma_start(h_res[t.slot][:, :, :], hin[t.n]).then_inc(h_res_loaded[t.slot], 16)
                    if new.within():
                        store(new, q_hl, q_dram, q_stored, 0)
                        if not mem:
                            store(new, k_hl, k_dram, k_stored, 1)
                    if old.within():
                        if normed_out:
                            sp.wait_ge(affine_done, 2 * (old.n + 1))
                        else:
                            sp.wait_ge(divided, TT * (old.n + 1))
                        sp.dma_start(out[old.n], result[old.slot][:, :, :] if normed_out else result[old.slot]).then_inc(result_stored[old.slot], 16)
                    if ctx_t is not None and ahead.within():
                        load_src(ahead)
                    if nxt.within():
                        load_m(nxt)

                pipeline(sp, step, 3, 1)
                for k in range(2):
                    sp.wait_ge(result_stored[k], 16 * (BATCHES // 2))

            @block.tensor
            def _(pe):
                pe.sem_inc(pv_done, 2)
                pe.wait_ge(params_loaded, 16 * params)

                def turn_rows(t, new):
                    pe.wait_ge(f_emptied, fills(F_FILLS, t, F_TURN))
                    pe.wait_ge(h_in_loaded[new.slot], 16 * (new.turn + 1))
                    for k in range(TT):
                        for dc in range(DC):
                            mm = nc.tensor.transpose(ps_f[:, dc, k * P:(k + 1) * P],
                                                     h_in[new.slot][:, k, dc * P:(dc + 1) * P], c.ident[:, :])
                    mm.then_inc(f_filled, 1)

                def project(t, k, src, wt):
                    pe.wait_ge(f_emptied, fills(F_FILLS, t, k))
                    for fc in range(DC):
                        for dc in range(DC):
                            mm = nc.tensor.matmul(ps_f[:, fc, :], wt[:, dc, fc * P:(fc + 1) * P], src[:, dc, :],
                                                  start=(dc == 0), stop=(dc == DC - 1))
                    mm.then_inc(f_filled, 1)

                def project_values(t, nxt):
                    pe.wait_ge(f_emptied, fills(F_FILLS, t, F_V))
                    for k in range(TT):
                        for dc in range(DC):
                            mm = nc.tensor.matmul(ps_f[:, k, :], src_t[nxt.slot][:, dc, k * P:(k + 1) * P], w[2][:, dc, :],
                                                  start=(dc == 0), stop=(dc == DC - 1))
                    mm.then_inc(f_filled, 1)

                def score_rows(t, new):
                    pe.wait_ge(f_emptied, fills(F_FILLS, t, F_BEST))
                    pe.wait_ge(src_loaded[new.slot], 16 * (new.turn + 1))
                    for k in range(TT):
                        for dc in range(DC):
                            mm = nc.tensor.matmul(ps_f[:, k, :], q_t[new.slot][:, dc, k * P:(k + 1) * P], src_t[new.slot][:, dc, :],
                                                  start=(dc == 0), stop=(dc == DC - 1))
                    mm.then_inc(f_filled, 1)

                def turn_keys(t, nxt):
                    pe.wait_ge(x_emptied, fills(X_FILLS, t, X_KEYS))
                    pe.wait_ge(rows_loaded[nxt.slot], 16 * TT * (nxt.turn + 1))
                    pe.sem_inc(turning, 1)
                    to = ps_x[0:64, 0:8, :].rearrange("p a b -> p (a b)").bitcast(F16)
                    for k in range(TT):
                        mm = nc.tensor.transpose(to[:, k * P:(k + 1) * P], rows[nxt.slot][:, k, 0:KEY_WORDS].bitcast(F16), c.ident_h[:, :])
                    mm.then_inc(x_filled, 1)

                def scores(nxt, h):
                    pe.wait_ge(s_emptied, HEADS * nxt.n + h + 1)
                    q, kk, to = q_st[nxt.slot], k_st[nxt.slot][:, h % kv_heads, :], ps_s[h % 2]
                    for k in range(TT):
                        mm = nc.tensor.matmul(to[:, k, 0:keys_of[k]], q[0:STACK, h, k * P:(k + 1) * P],
                                              kk[0:STACK, 0:keys_of[k]], start=True, stop=not causal)
                        if causal:
                            mm = nc.tensor.matmul(to[:, k, k * P:(k + 1) * P], c.ident_bf[:, :], c.mask_st[:, :],
                                                  start=False, stop=True)
                    mm.then_inc(s_filled, 1)

                def turn_maxima(t, nxt):
                    pe.wait_ge(x_emptied, fills(X_FILLS, t, X_MAX))
                    pe.wait_ge(s_emptied, 2 + HEADS * (nxt.n + 1))
                    to = ps_x[0:HEADS, 0:8, :].rearrange("p a b -> p (a b)")
                    for k in range(TT):
                        mm = nc.tensor.transpose(to[:, k * P:(k + 1) * P], neg_m[nxt.slot][:, k, :], c.ident[:, :])
                    mm.then_inc(x_filled, 1)

                def shifted_scores(t, p):
                    if p == 0:
                        pe.wait_ge(m_loaded[t.slot], 16 * (t.turn + 1))
                    pe.wait_ge(t_emptied, PAIRS * t.n + p + 1)
                    for j in range(2):
                        h, at = 2 * p + j, 0
                        for k in range(TT):
                            a, b = q_of[k]
                            mm = nc.tensor.matmul(ps_t[:, j, at:at + b - a], k_st[t.slot][0:ROWS, h % kv_heads, k * P:(k + 1) * P],
                                                  q_st[t.slot][0:ROWS, h, a:b], start=True, stop=not causal)
                            if causal:
                                mm = nc.tensor.matmul(ps_t[:, j, at:at + P], c.ident_bf[:, :], c.mask_ts[:, :],
                                                      start=False, stop=True)
                            at += b - a
                    mm.then_inc(t_filled, 1)

                def values(t, gr):
                    pe.wait_ge(t_emptied, 1 + PAIRS * t.n + 2 * gr + 2)
                    if gr == 0 and not mem:
                        pe.wait_ge(v_done, t.n + 1)
                    pe.wait_ge(o_copied, GROUPS * t.n + gr + 1)
                    at = 0
                    for k in range(TT):
                        a, b = q_of[k]
                        for j in range(GROUP):
                            h = GROUP * gr + j
                            vals = rows[t.slot][:, k, KEY_WORDS:MEM_WORDS] if mem else v[t.slot][:, k, h, :]
                            mm = nc.tensor.matmul(ps_o[gr % 2][j * VW:(j + 1) * VW, a:b], vals,
                                                  probs[h // 2 % 4][:, h % 2, at:at + b - a], start=(k == 0), stop=(k == TT - 1),
                                                  tile_position=(0, j * VW))
                        at += b - a
                    mm.then_inc(pv_done, 1)

                def turn_outputs(t, old, k):
                    pe.wait_ge(x_emptied, fills(X_FILLS, t, X_OUT + k))
                    if k == 0:
                        pe.wait_ge(o_copied, 2 + GROUPS * (old.n + 1))
                    to = ps_x[:, :, :].rearrange("p (g h) e -> p g (h e)", g=GROUPS)
                    for gr in range(GROUPS):
                        mm = nc.tensor.transpose(to[:, gr, :], o_t[:, gr, k * P:(k + 1) * P], c.ident[:, :])
                    mm.then_inc(x_filled, 1)

                def step(t):
                    nxt, new, old = t.plus(1), t.plus(2), t.plus(-1)
                    for p in range(PAIRS):
                        if t.within():
                            shifted_scores(t, p)
                        if p in (1, 2) and old.within():
                            turn_outputs(t, old, p - 1)
                        if t.within() and p in (2, 4, 6):
                            values(t, p // 2 - 1)
                        if p == 0 and new.within():
                            turn_rows(t, new)
                        if p == 1 and new.within():
                            project(t, F_Q, h_t[new.slot], w[0])
                        if p == 2 and new.within() and not mem:
                            if cross:
                                pe.wait_ge(src_loaded[new.slot], 16 * (new.turn + 1))
                            project(t, F_K, src_t[new.slot], w[1])
                        if p == 2 and nxt.within() and mem:
                            turn_keys(t, nxt)
                        if p == 2 and nxt.within():
                            pe.wait_ge(stack_loaded[nxt.slot], 16 * STACK_DMAS * (nxt.turn + 1))
                            if mem:
                                pe.wait_ge(v_done, nxt.n + 1)
                        if p == 3 and new.within() and mem:
                            score_rows(t, new)
                        if 2 <= p < 7 and nxt.within():
                            for h in range(3 * (p - 2), HEADS if p == 6 else 3 * (p - 1)):
                                scores(nxt, h)
                        if p == 7 and nxt.within():
                            if not mem:
                                project_values(t, nxt)
                            turn_maxima(t, nxt)
                    if t.within():
                        values(t, GROUPS - 1)

                pipeline(pe, step, 2, 1)

            @block.scalar
            def _(act):
                act.sem_inc(t_emptied, 1)
                act.sem_inc(o_copied, 2)

                def copy_outputs(t, gr):
                    act.wait_ge(pv_done, 2 + GROUPS * t.n + gr + 1)
                    if gr == 0 and t.before(1):
                        act.wait_ge(x_filled, fills(X_FILLS, t, X_OUT + 1) + 1)
                    nc.scalar.copy(o_t[:, gr, :], ps_o[gr % 2][:, 0:SEQ]).then_inc(o_copied, 1)

                def step(t):
                    nxt, new, old = t.plus(1), t.plus(2), t.plus(-1)
                    for p in range(PAIRS):
                        if t.within():
                            act.wait_ge(t_filled, PAIRS * t.n + p + 1)
                            act.wait_ge(pv_done, GROUPS * t.n + p // 2 + 1)
                            nc.scalar.activation(probs[p % 4][:, :, :], ps_t[:, :, 0:width], ACT.Exp,
                                                 scale=SCALE).then_inc(t_emptied, 1)
                        if p == 0 and old.within():
                            copy_outputs(old, GROUPS - 1)
                        if p in (2, 4, 6) and t.within():
                            copy_outputs(t, p // 2 - 1)
                        if p == 0 and new.within():
                            act.wait_ge(f_filled, fills(F_FILLS, t, F_TURN) + 1)
                            nc.scalar.copy(h_t[new.slot][:, :, :], ps_f[:, :, :]).then_inc(f_emptied, 1)
                        if p in (1, 2)[:KV] and new.within():
                            hl, stored = (q_hl, q_stored) if p == 1 else (k_hl, k_stored)
                            act.wait_ge(f_filled, fills(F_FILLS, t, p) + 1)
                            if new.before(2):
                                act.wait_ge(stored[new.slot], 16 * new.turn)
                            if mem:
                                nc.scalar.copy(q_t[new.slot][:, :, :], ps_f[:, :, :])
                            nc.scalar.copy(hl[new.slot][:, 0, :, :], ps_f[:, :, :]).then_inc(hi_done, 1)
                        if p == 2 and nxt.within() and mem:
                            act.wait_ge(x_filled, fills(X_FILLS, t, X_KEYS) + 1)
                            nc.scalar.copy(k_st[nxt.slot][:, 0, :],
                                           ps_x[0:64, 0:8, :].rearrange("p a b -> p (a b)").bitcast(F16)[:, 0:SEQ]).then_inc(x_emptied, 1)
                            act.wait_ge(x_emptied, fills(X_FILLS, t, X_KEYS) + 1)
                            act.sem_inc(v_done, 1)
                        if p == 7 and nxt.within():
                            act.wait_ge(x_filled, fills(X_FILLS, t, X_MAX) + 1)
                            if nxt.before(2):
                                act.wait_ge(m_loaded[nxt.slot], 16 * nxt.turn)
                            nc.scalar.copy(m_row[nxt.slot][:, :],
                                           ps_x[0:HEADS, 0:8, :].rearrange("p a b -> p (a b)")).then_inc(x_emptied, 1)
                            act.wait_ge(x_emptied, fills(X_FILLS, t, X_MAX) + 1)
                            act.sem_inc(m_row_done, 1)

                pipeline(act, step, 2, 1)

            @block.vector
            def _(dve):
                dve.sem_inc(s_emptied, 2)
                if mem:
                    nc.vector.memset(first_row[:, :], 0.0).then_inc(row_done, 1)
                else:
                    for k in range(2):
                        nc.vector.memset(v[k][:, :, :, HD:VW], 0.0).then_inc(ones_set, 1)
                    dve.wait_ge(ones_set, 2)
                    for k in range(2):
                        nc.vector.memset(v[k][:, :, :, HD:HD + 1], 1.0)
                        nc.vector.memset(k_st[k][32:64, :, :], 1.0).then_inc(ones_set, 1)
                dve.wait_ge(params_loaded, 16 * params)

                def low_part(t, new, k, hl):
                    dve.wait_ge(hi_done, KV * new.n + k)
                    nc.vector.tensor_tensor(hl[new.slot][:, 1, :, :], ps_f[:, :, :], hl[new.slot][:, 0, :, :],
                                            ALU.subtract).then_inc(f_emptied, 1)
                    dve.wait_ge(f_emptied, fills(F_FILLS, t, k) + 1)
                    dve.sem_inc(lo_done, 1)

                def copy_values(t, nxt):
                    dve.wait_ge(f_filled, fills(F_FILLS, t, F_V) + 1)
                    if nxt.before(1):
                        dve.wait_ge(pv_done, 2 + GROUPS * (nxt.n - 1))
                    nc.vector.tensor_tensor(
                        v[nxt.slot][:, :, :, 0:HD], ps_f[:, :, :].rearrange("p t (h e) -> p t h e", e=HD),
                        bv[:, :].rearrange("p (h e) -> p h e", e=HD).unsqueeze(1).to_broadcast([P, TT, HEADS, HD]),
                        ALU.add).then_inc(f_emptied, 1)
                    dve.wait_ge(f_emptied, fills(F_FILLS, t, F_V) + 1)
                    dve.sem_inc(v_done, 1)

                def find_best(t, new):
                    dve.wait_ge(f_filled, fills(F_FILLS, t, F_BEST) + 1)
                    dve.sem_inc(ordered, 1)
                    for k in range(TT):
                        ins = nc.vector.max(best[:, k, :], ps_f[:, k, :])
                    ins.then_inc(best_step, 1)
                    dve.wait_ge(best_step, BEST_STEPS * new.n + 1)
                    dve.sem_inc(ordered, 1)
                    for k in range(TT):
                        ins = nc.vector.max_index(best_at[:, k, :], best[:, k, :], ps_f[:, k, :])
                    ins.then_inc(f_emptied, 1)
                    dve.wait_ge(f_emptied, fills(F_FILLS, t, F_BEST) + 1)
                    nc.vector.tensor_copy(best[:, :, 0], best_at[:, :, 0]).then_inc(best_step, 1)
                    dve.wait_ge(best_step, BEST_STEPS * new.n + 2)
                    dve.wait_ge(row_done, new.n + 1)
                    if new.before(2):
                        dve.wait_ge(rows_loaded[new.slot], 16 * TT * new.turn)
                    nc.vector.tensor_tensor(best_row[new.slot][:, :], best[:, :, 0], first_row[:, :], ALU.add).then_inc(best_step, 1)
                    dve.wait_ge(best_step, BEST_STEPS * new.n + 3)
                    nc.vector.tensor_scalar(first_row[:, :], first_row[:, :], float(SEQ), None, ALU.add).then_inc(row_done, 1)

                def maximum(nxt, h):
                    dve.wait_ge(s_filled, HEADS * nxt.n + h + 1)
                    if causal:
                        nc.vector.tensor_reduce(neg_m[nxt.slot][:, 0, h:h + 1], ps_s[h % 2][:, 0, 0:P], AX.X, ALU.max, negate=True)
                        nc.vector.tensor_reduce(neg_m[nxt.slot][:, 1, h:h + 1], ps_s[h % 2][:, 1, :], AX.X, ALU.max,
                                                negate=True).then_inc(s_emptied, 1)
                    else:
                        nc.vector.tensor_reduce(neg_m[nxt.slot][:, :, h:h + 1], ps_s[h % 2][:, :, :], AX.X, ALU.max,
                                                negate=True).then_inc(s_emptied, 1)

                def divide(t, old, k):
                    dve.wait_ge(x_filled, fills(X_FILLS, t, X_OUT + k) + 1)
                    if k == 0 and not normed_out and old.before(2):
                        dve.wait_ge(result_stored[old.slot], 16 * old.turn)
                    nc.vector.reciprocal(recip[:, :], ps_x[:, :, HD]).then_inc(recip_done, 1)
                    dve.wait_ge(recip_done, TT * old.n + k + 1)
                    nc.vector.tensor_tensor(att[old.slot][:, k, :, :], ps_x[:, :, 0:HD],
                                            recip[:, :].unsqueeze(2).to_broadcast([P, HEADS, HD]),
                                            ALU.mult).then_inc(x_emptied, 1)
                    dve.wait_ge(x_emptied, fills(X_FILLS, t, X_OUT + k) + 1)
                    dve.sem_inc(divided, 1)

                def sum_and_stats(t):
                    dve.wait_ge(h_res_loaded[t.slot], 16 * (t.turn + 1))
                    nc.vector.tensor_tensor(total[:, :, :], att[t.slot][:, :, :, :].rearrange("p t h e -> p t (h e)"),
                                            h_res[t.slot][:, :, :], ALU.add).then_inc(tail_step, 1)
                    dve.wait_ge(tail_step, TAIL_STEPS * t.n + 1)
                    for k in range(TT):
                        ins = nc.vector.bn_stats(stats[:, k, :], total[:, k, :])
                    ins.then_inc(tail_step, 1)
                    dve.wait_ge(tail_step, TAIL_STEPS * t.n + 2)
                    dve.sem_inc(h_res_free, 1)
                    for k in range(TT):
                        nc.vector.bn_aggr(mv[:, k, :], stats[:, k, :]).then_inc(tail_step, 1)

                def apply(t):
                    dve.wait_ge(rstd_done, t.n + 1)
                    if t.before(1):
                        dve.wait_ge(normed_free, t.n)
                    for k in range(TT):
                        nc.vector.tensor_scalar(normed[:, k, :], total[:, k, :], mv[:, k, 0:1], rstd[:, k:k + 1],
                                                ALU.subtract, ALU.mult).then_inc(tail_step, 1)

                def step(t):
                    nxt, new, old = t.plus(1), t.plus(2), t.plus(-1)
                    for p in range(PAIRS):
                        if p in (1, 2) and old.within():
                            divide(t, old, p - 1)
                        if p in (1, 2)[:KV] and new.within():
                            low_part(t, new, p, q_hl if p == 1 else k_hl)
                        if p == 2 and old.within() and normed_out:
                            sum_and_stats(old)
                        if p == 4 and old.within() and normed_out:
                            apply(old)
                        if 2 <= p < 7 and nxt.within():
                            for h in range(3 * (p - 2), HEADS if p == 6 else 3 * (p - 1)):
                                maximum(nxt, h)
                        if p == 3 and new.within() and mem:
                            find_best(t, new)
                        if p == 7 and nxt.within() and not mem:
                            copy_values(t, nxt)

                pipeline(dve, step, 2, 1)

            @block.gpsimd
            def _(pool):
                pool.wait_ge(params_loaded, 16 * params)

                def gather(t):
                    if t.before(2):
                        pool.wait_ge(pv_done, 2 + GROUPS * (t.n - 1))
                    pool.wait_ge(row_done, t.n + 2)
                    pool.sem_inc(gathering, 1)
                    for k in range(TT):
                        nc.gpsimd.indirect_dma_start(rows[t.slot][:, k, :], None, memory[:, :], bass.IndirectOffsetOnAxis(
                            ap=best_row[t.slot][:, k:k + 1], axis=0)).then_inc(rows_loaded[t.slot], 16)

                def step(t):
                    nxt, t = t.plus(1), t.plus(-1)
                    if mem and nxt.within():
                        gather(nxt)
                    if not t.within() or not normed_out:
                        return
                    pool.wait_ge(tail_step, TAIL_STEPS * t.n + 4)
                    nc.gpsimd.tensor_tensor(var[:, :], mv[:, :, 1], c.eps[:, :], ALU.add).then_inc(var_done, 1)
                    pool.wait_ge(var_done, t.n + 1)
                    nc.gpsimd.tensor_tensor(rstd[:, :], var[:, :], c.minus_half[:, :], ALU.pow).then_inc(rstd_done, 1)
                    pool.wait_ge(tail_step, TAIL_STEPS * (t.n + 1))
                    if t.before(2):
                        pool.wait_ge(result_stored[t.slot], 16 * t.turn)
                    nc.gpsimd.tensor_tensor(result[t.slot][:, :, :], normed[:, :, :],
                                            g[:, :].unsqueeze(1).to_broadcast([P, TT, D]), ALU.mult).then_inc(affine_done, 1)
                    pool.wait_ge(affine_done, 2 * t.n + 1)
                    pool.sem_inc(normed_free, 1)
                    nc.gpsimd.tensor_tensor(result[t.slot][:, :, :], result[t.slot][:, :, :],
                                            be[:, :].unsqueeze(1).to_broadcast([P, TT, D]), ALU.add).then_inc(affine_done, 1)

                pipeline(pool, step, 2, 1)


def feed_forward(nc, c, x2, x, w1, b1, w2, b2, gain, shift, gate, out, out_normed, logits):
    with ExitStack() as ctx:
        def sb(nm, shape, dt=F32):
            return ctx.enter_context(nc.sbuf_tensor(f"ff_{nm}", shape, dt))

        def ps(nm, shape, dt=F32):
            return ctx.enter_context(nc.psum_tensor(f"ff_{nm}", shape, dt))

        def sem(nm):
            return semaphore(nc, c, ctx, f"ff_{nm}")

        def ring(make, nm, *args, n=2):
            return [make(f"{nm}{k}", *args) for k in range(n)]

        FC = w1.shape[1] // P
        E = gate.shape[1]
        w1_sb, w2_sb = sb("w1", [P, DC, FC * P]), sb("w2", [P, FC, D])
        b1_sb, b2_sb = sb("b1", [P, FC]), sb("b2", [P, D])
        g, be, gate_sb = sb("gain", [P, D]), sb("shift", [P, D]), sb("gate", [P, DC, E])
        x2_in = ring(sb, "x2_in", [P, TT, D])
        x2_t = ring(sb, "x2_t", [P, DC, SEQ])
        hidden = ring(sb, "hidden", [P, FC, SEQ])
        biased = ring(sb, "biased", [P, TT, D])
        total = ring(sb, "total", [P, TT, D])
        stats, mv = ring(sb, "stats", [P, TT, 6]), ring(sb, "mv", [P, TT, 2])
        stats_o, mv_o = ring(sb, "stats_o", [P, TT, 6]), ring(sb, "mv_o", [P, TT, 2])
        var, rstd = sb("var", [P, TT]), ring(sb, "rstd", [P, TT])
        var_o, rstd_o = sb("var_o", [P, TT]), ring(sb, "rstd_o", [P, TT])
        normed = ring(sb, "normed", [P, TT, D])
        x_in = ring(sb, "x_in", [P, TT, D])
        res = ring(sb, "res", [P, TT, D])
        res_n = ring(sb, "res_n", [P, TT, D])
        res_t = sb("res_t", [P, DC, SEQ])

        ps_x = ps("ps_x", [P, DC, SEQ])
        ps_h = ring(ps, "ps_h", [P, 2, SEQ])
        ps_o = ps("ps_o", [P, TT, D])
        ps_r = ps("ps_r", [P, DC, SEQ])
        ps_g = ps("ps_g", [P, BANK])
        ps_ge = ps_g[:, 0:TT * E].rearrange("p (t e) -> p t e", t=TT)

        params_loaded = sem("params_loaded")
        x2_loaded, x_loaded = ring(sem, "x2_loaded"), ring(sem, "x_loaded")
        x_turned, x_copied, h_filled, h_done = sem("x_turned"), sem("x_copied"), sem("h_filled"), sem("h_done")
        o_filled, o_read, bias_added = sem("o_filled"), sem("o_read"), sem("bias_added")
        step1, step2 = sem("step1"), sem("step2")
        var_done, rstd_done, rstd_o_done = sem("var_done"), sem("rstd_done"), sem("rstd_o_done")
        normed_done, affine = sem("normed_done"), sem("affine")
        res_n_done = sem("res_n_done")
        r_turned, r_copied, g_filled, g_copied = sem("r_turned"), sem("r_copied"), sem("g_filled"), sem("g_copied")
        res_stored, res_n_stored = ring(sem, "res_stored"), ring(sem, "res_n_stored")
        AFFINE_STEPS, LN_STEPS = 3, 3
        x_rows = x.rearrange("(b t p) d -> b p t d", b=BATCHES, p=P)

        with nc.Block() as block:
            @block.sync
            def _(sp):
                for dst, src in ((w1_sb, w1.rearrange("(c p) f -> p c f", p=P)), (w2_sb, w2.rearrange("(c p) f -> p c f", p=P)),
                                 (gate_sb, gate.rearrange("(c p) f -> p c f", p=P))):
                    sp.dma_start(dst[:, :, :], src).then_inc(params_loaded, 16)
                sp.dma_start(b1_sb[:, :], b1).then_inc(params_loaded, 16)
                for dst, src in ((b2_sb, b2), (g, gain), (be, shift)):
                    sp.dma_start(dst[:, :], src.partition_broadcast(P)).then_inc(params_loaded, 16)

                def step(t):
                    new, old, older = t.plus(2), t.plus(-2), t.plus(-4)
                    if new.within():
                        if new.before(2):
                            sp.wait_ge(x_turned, new.n - 1)
                            sp.wait_ge(bias_added, new.n - 1)
                        sp.dma_start(x2_in[new.slot][:, :, :], x2[new.n]).then_inc(x2_loaded[new.slot], 16)
                    if t.within():
                        if t.before(2):
                            sp.wait_ge(affine, AFFINE_STEPS * (t.n - 1))
                        sp.dma_start(x_in[t.slot][:, :, :], x_rows[t.n]).then_inc(x_loaded[t.slot], 16)
                    if old.within():
                        sp.wait_ge(affine, AFFINE_STEPS * (old.n + 1))
                        sp.dma_start(out[old.n], res[old.slot][:, :, :]).then_inc(res_stored[old.slot], 16)
                    if older.within():
                        sp.wait_ge(res_n_done, TT * (older.n + 1))
                        sp.dma_start(out_normed[older.n], res_n[older.slot][:, :, :]).then_inc(res_n_stored[older.slot], 16)

                pipeline(sp, step, 2, 4)
                for k in range(2):
                    sp.wait_ge(res_stored[k], 16 * (BATCHES // 2))
                    sp.wait_ge(res_n_stored[k], 16 * (BATCHES // 2))

            @block.tensor
            def _(pe):
                pe.wait_ge(params_loaded, 16 * 7)

                def first_layer(t):
                    pe.wait_ge(x2_loaded[t.slot], 16 * (t.turn + 1))
                    if t.before(1):
                        pe.wait_ge(x_copied, t.n)
                    for k in range(TT):
                        for dc in range(DC):
                            mm = nc.tensor.transpose(ps_x[:, dc, k * P:(k + 1) * P], x2_in[t.slot][:, k, dc * P:(dc + 1) * P], c.ident[:, :])
                    mm.then_inc(x_turned, 1)
                    pe.wait_ge(x_copied, t.n + 1)
                    for f in range(0, FC, 2):
                        if f >= 4 or t.before(1):
                            pe.wait_ge(h_done, FC * t.n + f - 2)
                        for j in range(2):
                            for dc in range(DC):
                                mm = nc.tensor.matmul(ps_h[f // 2 % 2][:, j, :], w1_sb[:, dc, (f + j) * P:(f + j + 1) * P],
                                                      x2_t[t.slot][:, dc, :], start=(dc == 0), stop=(dc == DC - 1))
                        mm.then_inc(h_filled, 1)

                def second_layer(t):
                    pe.wait_ge(h_done, FC * (t.n + 1))
                    if t.before(1):
                        pe.wait_ge(o_read, t.n)
                    for k in range(TT):
                        for f in range(FC):
                            mm = nc.tensor.matmul(ps_o[:, k, :], hidden[t.slot][:, f, k * P:(k + 1) * P], w2_sb[:, f, :],
                                                  start=(f == 0), stop=(f == FC - 1))
                    mm.then_inc(o_filled, 1)

                def turn_result(t):
                    pe.wait_ge(res_n_done, TT * (t.n + 1))
                    if t.before(1):
                        pe.wait_ge(r_copied, t.n)
                    for k in range(TT):
                        for dc in range(DC):
                            mm = nc.tensor.transpose(ps_r[:, dc, k * P:(k + 1) * P], res_n[t.slot][:, k, dc * P:(dc + 1) * P], c.ident[:, :])
                    mm.then_inc(r_turned, 1)

                def gates(t):
                    pe.wait_ge(r_copied, t.n + 1)
                    if t.before(1):
                        pe.wait_ge(g_copied, t.n)
                    for k in range(TT):
                        for dc in range(DC):
                            mm = nc.tensor.matmul(ps_ge[:, k, :], res_t[:, dc, k * P:(k + 1) * P], gate_sb[:, dc, :],
                                                  start=(dc == 0), stop=(dc == DC - 1))
                    mm.then_inc(g_filled, 1)

                def step(t):
                    new, old = t.plus(1), t.plus(-4)
                    if old.within():
                        turn_result(old)
                    if new.within():
                        first_layer(new)
                    if old.within():
                        gates(old)
                    if t.within():
                        second_layer(t)

                pipeline(pe, step, 1, 4)

            @block.scalar
            def _(act):
                act.wait_ge(params_loaded, 16 * 7)

                def step(t):
                    new, old = t.plus(1), t.plus(-4)
                    if old.within():
                        act.wait_ge(r_turned, old.n + 1)
                        if old.before(1):
                            act.wait_ge(g_filled, old.n)
                        nc.scalar.copy(res_t[:, :, :], ps_r[:, :, :]).then_inc(r_copied, 1)
                    if new.within():
                        act.wait_ge(x_turned, new.n + 1)
                        nc.scalar.copy(x2_t[new.slot][:, :, :], ps_x[:, :, :]).then_inc(x_copied, 1)
                        for f in range(FC):
                            if f % 2 == 0:
                                act.wait_ge(h_filled, FC // 2 * new.n + f // 2 + 1)
                            if f == 0 and new.before(2):
                                act.wait_ge(o_filled, new.n - 1)
                            nc.scalar.activation(hidden[new.slot][:, f, :], ps_h[f // 2 % 2][:, f % 2, :], ACT.Relu,
                                                 bias=b1_sb[:, f:f + 1]).then_inc(h_done, 1)

                pipeline(act, step, 1, 4)

            @block.vector
            def _(dve):
                def statistics(src, st, to, n, sm, base):
                    for k in range(TT):
                        ins = nc.vector.bn_stats(st[:, k, :], src[:, k, :])
                    ins.then_inc(sm, 1)
                    dve.wait_ge(sm, LN_STEPS * n + base + 1)
                    dve.sem_inc(sm, 1)
                    for k in range(TT):
                        ins = nc.vector.bn_aggr(to[:, k, :], st[:, k, :])
                    ins.then_inc(sm, 1)

                def step(t):
                    a, b, o, d, e = (t.plus(-k) for k in range(5))
                    if a.within():
                        dve.wait_ge(o_filled, a.n + 1)
                        dve.wait_ge(bias_added, a.n + 1)
                        if a.before(2):
                            dve.wait_ge(normed_done, TT * (a.n - 1))
                        nc.vector.tensor_tensor(total[a.slot][:, :, :], ps_o[:, :, :], biased[a.slot][:, :, :], ALU.add).then_inc(o_read, 1)
                        dve.wait_ge(o_read, a.n + 1)
                        statistics(total[a.slot], stats[a.slot], mv[a.slot], a.n, step1, 0)
                    if b.within():
                        dve.wait_ge(rstd_done, b.n + 1)
                        if b.before(2):
                            dve.wait_ge(affine, AFFINE_STEPS * (b.n - 1))
                        for k in range(TT):
                            nc.vector.tensor_scalar(normed[b.slot][:, k, :], total[b.slot][:, k, :], mv[b.slot][:, k, 0:1],
                                                    rstd[b.slot][:, k:k + 1], ALU.subtract, ALU.mult).then_inc(normed_done, 1)
                    if o.within():
                        dve.wait_ge(affine, AFFINE_STEPS * (o.n + 1))
                        if o.before(2):
                            dve.wait_ge(res_n_done, TT * (o.n - 1))
                        statistics(res[o.slot], stats_o[o.slot], mv_o[o.slot], o.n, step2, 0)
                    if d.within():
                        dve.wait_ge(rstd_o_done, d.n + 1)
                        if d.before(2):
                            dve.wait_ge(res_n_stored[d.slot], 16 * d.turn)
                            dve.wait_ge(r_turned, d.n - 1)
                        for k in range(TT):
                            nc.vector.tensor_scalar(res_n[d.slot][:, k, :], res[d.slot][:, k, :], mv_o[d.slot][:, k, 0:1],
                                                    rstd_o[d.slot][:, k:k + 1], ALU.subtract, ALU.mult).then_inc(res_n_done, 1)
                    if e.within():
                        dve.wait_ge(g_filled, e.n + 1)
                        nc.vector.tensor_copy(logits[:, bass.ds(e.n * TT, TT), :], ps_ge).then_inc(g_copied, 1)

                pipeline(dve, step, 0, 4)

            @block.gpsimd
            def _(pool):
                pool.wait_ge(params_loaded, 16 * 7)

                def root(m, v, r, t, k, done):
                    if t.before(1):
                        pool.wait_ge(done, t.n)
                    nc.gpsimd.tensor_tensor(v[:, :], m[:, :, 1], c.eps[:, :], ALU.add).then_inc(var_done, 1)
                    pool.wait_ge(var_done, k)
                    nc.gpsimd.tensor_tensor(r[:, :], v[:, :], c.minus_half[:, :], ALU.pow).then_inc(done, 1)

                def roots_before(t, k):
                    def some(m):
                        return min(max(m, 0), BATCHES) if isinstance(m, int) else m
                    return some(t.n + k) + some(t.n - 2)

                def step(t):
                    new, old, older = t.plus(1), t.plus(-1), t.plus(-2)
                    if new.within():
                        pool.wait_ge(x2_loaded[new.slot], 16 * (new.turn + 1))
                        if new.before(2):
                            pool.wait_ge(o_read, new.n - 1)
                        nc.gpsimd.tensor_tensor(biased[new.slot][:, :, :], x2_in[new.slot][:, :, :],
                                                b2_sb[:, :].unsqueeze(1).to_broadcast([P, TT, D]), ALU.add).then_inc(bias_added, 1)
                    if t.within():
                        pool.wait_ge(step1, LN_STEPS * (t.n + 1))
                        root(mv[t.slot], var, rstd[t.slot], t, roots_before(t, 0) + 1, rstd_done)
                    if old.within():
                        pool.wait_ge(normed_done, TT * (old.n + 1))
                        if old.before(2):
                            pool.wait_ge(res_n_done, TT * (old.n - 1))
                            pool.wait_ge(res_stored[old.slot], 16 * old.turn)
                        to = res[old.slot][:, :, :]
                        nc.gpsimd.tensor_tensor(to, normed[old.slot][:, :, :], g[:, :].unsqueeze(1).to_broadcast([P, TT, D]),
                                                ALU.mult).then_inc(affine, 1)
                        pool.wait_ge(affine, AFFINE_STEPS * old.n + 1)
                        nc.gpsimd.tensor_tensor(to, to, be[:, :].unsqueeze(1).to_broadcast([P, TT, D]), ALU.add).then_inc(affine, 1)
                        pool.wait_ge(affine, AFFINE_STEPS * old.n + 2)
                        pool.wait_ge(x_loaded[old.slot], 16 * (old.turn + 1))
                        nc.gpsimd.tensor_tensor(to, to, x_in[old.slot][:, :, :], ALU.add).then_inc(affine, 1)
                    if older.within():
                        pool.wait_ge(step2, LN_STEPS * (older.n + 1))
                        root(mv_o[older.slot], var_o, rstd_o[older.slot], older,
                             roots_before(t, 1) + 1, rstd_o_done)

                pipeline(pool, step, 1, 2)


def route(nc, c, logits, normed, xs, weights, slots, tile_expert, zeroed):
    with ExitStack() as ctx:
        def sb(nm, shape, dt=F32):
            return ctx.enter_context(nc.sbuf_tensor(f"route_{nm}", shape, dt))

        def sem(nm):
            return semaphore(nc, c, ctx, f"route_{nm}")

        NT, E = logits.shape[1], logits.shape[2]
        tiles = tile_expert.shape[1]
        top, top_at = sb("top", [P, NT, E]), sb("top_at", [P, NT, E], U32)
        chosen_at = sb("chosen_at", [P, NT, 2])
        chosen = [sb(f"chosen{k}", [P, NT, E]) for k in range(2)]
        either = sb("either", [P, NT, E])
        triangle, ones = sb("triangle", [P, P]), sb("ones", [P, P])
        numbers, bounds, tile_numbers = sb("numbers", [P, E]), sb("bounds", [P, SEQ * BATCHES // SEQ]), sb("tile_numbers", [1, tiles])
        total, sums = sb("total", [P, NT, E]), [sb(f"sums{k}", [P, NT, E]) for k in range(2)]
        above, used = sb("above", [P, E, BATCHES]), sb("used", [P, E])
        ends = [sb(f"ends{k}", [P, E]) for k in range(2)]
        start = sb("start", [P, E])
        place, picked, slot = sb("place", [P, NT, E]), sb("picked", [P, NT, E]), sb("slot", [P, NT])
        ended, owner = sb("ended", [1, tiles, E]), sb("owner", [1, tiles])
        gap, exped, both = sb("gap", [P, NT]), sb("exped", [P, NT]), sb("both", [P, NT])
        rows = sb("rows", [P, NT, D])
        ps_p = ctx.enter_context(nc.psum_tensor("route_ps_p", [P, BANK], F32))
        ps_t = ctx.enter_context(nc.psum_tensor("route_ps_t", [P, BANK], F32))

        made, exps, chose, counted, stepped = sem("made"), sem("exps"), sem("chose"), sem("counted"), sem("stepped")
        gap_done, slots_done, rows_loaded, scattered = sem("gap_done"), sem("slots_done"), sem("rows_loaded"), sem("scattered")

        with nc.Block() as block:
            @block.sync
            def _(sp):
                for b in range(BATCHES):
                    sp.dma_start(rows[:, b * TT:(b + 1) * TT, :], normed[b]).then_inc(rows_loaded, 16)

            @block.tensor
            def _(pe):
                pe.wait_ge(made, 6)
                pe.wait_ge(chose, 1)
                a = either[:, :, :].rearrange("p t e -> p (t e)")
                nc.tensor.matmul(ps_p[:, 0:NT * E], triangle[:, :], a, start=True, stop=True).then_inc(counted, 1)
                nc.tensor.matmul(ps_t[:, 0:NT * E], ones[:, :], a, start=True, stop=True).then_inc(counted, 1)

            @block.scalar
            def _(act):
                act.wait_ge(gap_done, 1)
                nc.scalar.activation(exped[:, :], gap[:, :], ACT.Exp).then_inc(exps, 1)

            @block.vector
            def _(dve):
                step = iter(range(1, 100))
                for t in range(NT):
                    ins = nc.vector.max(top[:, t, :], logits[:, t, :])
                ins.then_inc(stepped, 1)
                dve.wait_ge(stepped, next(step))
                for t in range(NT):
                    ins = nc.vector.max_index(top_at[:, t, :], top[:, t, :], logits[:, t, :])
                ins.then_inc(stepped, 1)
                nc.vector.tensor_tensor(gap[:, :], top[:, :, 1], top[:, :, 0], ALU.subtract).then_inc(gap_done, 1)
                dve.wait_ge(stepped, next(step))
                nc.vector.tensor_copy(chosen_at[:, :, :], top_at[:, :, 0:2]).then_inc(stepped, 1)
                dve.wait_ge(stepped, next(step))
                dve.wait_ge(made, 6)
                for k in range(2):
                    ins = nc.vector.tensor_tensor(chosen[k][:, :, :], numbers[:, :].unsqueeze(1).to_broadcast([P, NT, E]),
                                                  chosen_at[:, :, k:k + 1].to_broadcast([P, NT, E]), ALU.is_equal)
                ins.then_inc(stepped, 1)
                dve.wait_ge(stepped, next(step))
                nc.vector.tensor_tensor(either[:, :, :], chosen[0][:, :, :], chosen[1][:, :, :], ALU.add).then_inc(chose, 1)

                dve.wait_ge(exps, 1)
                nc.vector.tensor_scalar(both[:, :], exped[:, :], 1.0, None, ALU.add).then_inc(stepped, 1)
                dve.wait_ge(stepped, next(step))
                nc.vector.reciprocal(weights[:, 0, :], both[:, :]).then_inc(stepped, 1)
                dve.wait_ge(stepped, next(step))
                nc.vector.tensor_tensor(weights[:, 1, :], exped[:, :], weights[:, 0, :], ALU.mult)

                dve.wait_ge(counted, 2)
                nc.vector.tensor_copy(total[:, :, :], ps_t[:, 0:NT * E].rearrange("p (t e) -> p t e", e=E)).then_inc(stepped, 1)
                dve.wait_ge(stepped, next(step))
                frm, shift = total, 1
                while shift < NT:
                    to = sums[shift.bit_length() % 2]
                    nc.vector.tensor_tensor(to[:, shift:, :], frm[:, shift:, :], frm[:, 0:NT - shift, :], ALU.add)
                    nc.vector.tensor_copy(to[:, 0:shift, :], frm[:, 0:shift, :]).then_inc(stepped, 1)
                    dve.wait_ge(stepped, next(step))
                    frm, shift = to, 2 * shift
                summed = frm

                nc.vector.tensor_tensor(above[:, :, :], summed[:, NT - 1, :].unsqueeze(2).to_broadcast([P, E, BATCHES]),
                                        bounds[:, :].unsqueeze(1).to_broadcast([P, E, BATCHES]), ALU.is_gt).then_inc(stepped, 1)
                dve.wait_ge(stepped, next(step))
                nc.vector.tensor_reduce(used[:, :], above[:, :, :], AX.X, ALU.add).then_inc(stepped, 1)
                dve.wait_ge(stepped, next(step))
                frm, shift = used, 1
                while shift < E:
                    to = ends[shift.bit_length() % 2]
                    nc.vector.tensor_tensor(to[:, shift:], frm[:, shift:], frm[:, 0:E - shift], ALU.add)
                    nc.vector.tensor_copy(to[:, 0:shift], frm[:, 0:shift]).then_inc(stepped, 1)
                    dve.wait_ge(stepped, next(step))
                    frm, shift = to, 2 * shift
                end = frm
                nc.vector.tensor_tensor(start[:, :], end[:, :], used[:, :], ALU.subtract).then_inc(stepped, 1)
                dve.wait_ge(stepped, next(step))
                nc.vector.tensor_scalar(start[:, :], start[:, :], float(SEQ), None, ALU.mult).then_inc(stepped, 1)

                nc.vector.tensor_tensor(place[:, :, :], summed[:, :, :], total[:, :, :], ALU.subtract).then_inc(stepped, 1)
                next(step)
                dve.wait_ge(stepped, next(step))
                nc.vector.tensor_tensor(place[:, :, :], place[:, :, :], ps_p[:, 0:NT * E].rearrange("p (t e) -> p t e", e=E),
                                        ALU.add).then_inc(stepped, 1)
                dve.wait_ge(stepped, next(step))
                nc.vector.tensor_tensor(place[:, :, :], place[:, :, :], start[:, :].unsqueeze(1).to_broadcast([P, NT, E]),
                                        ALU.add).then_inc(stepped, 1)
                dve.wait_ge(stepped, next(step))
                for k in range(2):
                    nc.vector.tensor_tensor(picked[:, :, :], place[:, :, :], chosen[k][:, :, :], ALU.mult).then_inc(stepped, 1)
                    dve.wait_ge(stepped, next(step))
                    nc.vector.tensor_reduce(slot[:, :], picked[:, :, :], AX.X, ALU.add).then_inc(stepped, 1)
                    dve.wait_ge(stepped, next(step))
                    nc.vector.tensor_copy(slots[:, k, :], slot[:, :]).then_inc(slots_done, 1)
                    dve.wait_ge(slots_done, k + 1)

                nc.vector.tensor_tensor(ended[:, :, :], end[0:1, :].unsqueeze(1).to_broadcast([1, tiles, E]),
                                        tile_numbers[:, :].unsqueeze(2).to_broadcast([1, tiles, E]), ALU.is_le).then_inc(stepped, 1)
                dve.wait_ge(stepped, next(step))
                nc.vector.tensor_reduce(owner[:, :], ended[:, :, :], AX.X, ALU.add).then_inc(stepped, 1)
                dve.wait_ge(stepped, next(step))
                nc.vector.tensor_scalar(tile_expert[:, :], owner[:, :], float(E - 1), None, ALU.min)

            @block.gpsimd
            def _(pool):
                nc.gpsimd.memset(triangle[:, :], 1.0).then_inc(made, 1)
                nc.gpsimd.memset(ones[:, :], 1.0).then_inc(made, 1)
                nc.gpsimd.iota(numbers[:, :], [[1, E]], 0, 0, allow_small_or_imprecise_dtypes=True).then_inc(made, 1)
                nc.gpsimd.iota(bounds[:, :], [[SEQ, BATCHES]], 0, 0, allow_small_or_imprecise_dtypes=True).then_inc(made, 1)
                nc.gpsimd.iota(tile_numbers[:, :], [[1, tiles]], 0, 0, allow_small_or_imprecise_dtypes=True).then_inc(made, 1)
                pool.wait_ge(made, 5)
                nc.gpsimd.affine_select(out=triangle[:, :], in_=triangle[:, :], compare_op=ALU.is_gt, fill=0.0, base=0,
                                        pattern=[[1, P]], channel_multiplier=-1).then_inc(made, 1)
                pool.wait_ge(rows_loaded, 16 * BATCHES)
                pool.wait_ge(zeroed, 16)
                for k in range(2):
                    pool.wait_ge(slots_done, k + 1)
                    for t in range(NT):
                        nc.gpsimd.indirect_dma_start(xs[:, :], bass.IndirectOffsetOnAxis(ap=slots[:, k, t:t + 1], axis=0),
                                                     rows[:, t, :], None).then_inc(scattered, 16)
                pool.wait_ge(scattered, 16 * 2 * NT)


def experts(nc, c, xs, w13, w2, tile_expert, ys):
    with ExitStack() as ctx:
        def sb(nm, shape, dt=F32):
            return ctx.enter_context(nc.sbuf_tensor(f"moe_{nm}", shape, dt))

        def ps(nm, shape, dt=F32):
            return ctx.enter_context(nc.psum_tensor(f"moe_{nm}", shape, dt))

        def sem(nm):
            return semaphore(nc, c, ctx, f"moe_{nm}")

        def ring(make, nm, *args, n=2):
            return [make(f"{nm}{k}", *args) for k in range(n)]

        tiles = tile_expert.shape[1]
        E, HC = w2.shape[0], w2.shape[2]
        x_in, x_t = ring(sb, "x_in", [P, TT, D]), ring(sb, "x_t", [P, DC, SEQ])
        up_sb, down_sb = ring(sb, "up", [P, 2, DC, HC * P]), ring(sb, "down", [P, HC, D])
        mid = ring(sb, "mid", [P, HC, SEQ])
        y = ring(sb, "y", [P, TT, D])
        ps_x = ps("ps_x", [P, DC, SEQ])
        ps_u = ring(ps, "ps_u", [P, 2, SEQ])
        ps_y = ring(ps, "ps_y", [P, TT, D])
        x_loaded, up_loaded, down_loaded = ring(sem, "x_loaded"), ring(sem, "up_loaded"), ring(sem, "down_loaded")
        turned, x_copied, u_filled, silu_done, mid_done = sem("turned"), sem("x_copied"), sem("u_filled"), sem("silu_done"), sem("mid_done")
        y_filled, y_copied, y_stored = sem("y_filled"), sem("y_copied"), ring(sem, "y_stored")
        xs_t = xs.rearrange("(n t p) d -> n p t d", n=tiles, p=P)
        ys_t = ys.rearrange("(n t p) d -> n p t d", n=tiles, p=P)

        with nc.Block() as block:
            @block.sync
            def _(sp):
                def step(t):
                    new, old = t.plus(3), t.plus(-1)
                    if new.within():
                        e = sp.value_load(tile_expert[0:1, bass.ds(new.n, 1)], min_val=0, max_val=E - 1)
                        if new.before(2):
                            sp.wait_ge(turned, new.n - 1)
                        sp.dma_start(x_in[new.slot][:, :, :], xs_t[new.n]).then_inc(x_loaded[new.slot], 16)
                        if new.before(2):
                            sp.wait_ge(u_filled, HC * (new.n - 1))
                        sp.dma_start(up_sb[new.slot][:, :, :, :].rearrange("p m c h -> p (m c h)"), w13[e]).then_inc(up_loaded[new.slot], 16)
                        if new.before(2):
                            sp.wait_ge(y_filled, new.n - 1)
                        sp.dma_start(down_sb[new.slot][:, :, :], w2[e]).then_inc(down_loaded[new.slot], 16)
                    if old.within():
                        sp.wait_ge(y_copied, old.n + 1)
                        sp.dma_start(ys_t[old.n], y[old.slot][:, :, :]).then_inc(y_stored[old.slot], 16)

                pipeline(sp, step, 3, 1, tiles)
                for k in range(2):
                    sp.wait_ge(y_stored[k], 16 * ((tiles - k + 1) // 2))

            @block.tensor
            def _(pe):
                def turn_rows(t):
                    pe.wait_ge(x_loaded[t.slot], 16 * (t.turn + 1))
                    if t.before(1):
                        pe.wait_ge(x_copied, t.n)
                    for k in range(TT):
                        for dc in range(DC):
                            mm = nc.tensor.transpose(ps_x[:, dc, k * P:(k + 1) * P], x_in[t.slot][:, k, dc * P:(dc + 1) * P], c.ident[:, :])
                    mm.then_inc(turned, 1)

                def go_up(t):
                    pe.wait_ge(up_loaded[t.slot], 16 * (t.turn + 1))
                    pe.wait_ge(x_copied, t.n + 1)
                    for f in range(HC):
                        if f >= 2 or t.before(1):
                            pe.wait_ge(mid_done, HC * t.n + f - 1)
                        bank = ps_u[(HC * t.slot + f) % 2]
                        for m in range(2):
                            for dc in range(DC):
                                mm = nc.tensor.matmul(bank[:, m, :], up_sb[t.slot][:, m, dc, f * P:(f + 1) * P], x_t[t.slot][:, dc, :],
                                                      start=(dc == 0), stop=(dc == DC - 1))
                        mm.then_inc(u_filled, 1)

                def go_down(t):
                    pe.wait_ge(down_loaded[t.slot], 16 * (t.turn + 1))
                    pe.wait_ge(mid_done, HC * (t.n + 1))
                    if t.before(2):
                        pe.wait_ge(y_copied, t.n - 1)
                    for k in range(TT):
                        for f in range(HC):
                            mm = nc.tensor.matmul(ps_y[t.slot][:, k, :], mid[t.slot][:, f, k * P:(k + 1) * P], down_sb[t.slot][:, f, :],
                                                  start=(f == 0), stop=(f == HC - 1))
                    mm.then_inc(y_filled, 1)

                def step(t):
                    nxt, new = t.plus(1), t.plus(2)
                    if nxt.within():
                        go_up(nxt)
                    if new.within():
                        turn_rows(new)
                    if t.within():
                        go_down(t)

                pipeline(pe, step, 2, 0, tiles)

            @block.scalar
            def _(act):
                def step(t):
                    nxt, new = t.plus(1), t.plus(2)
                    if nxt.within():
                        for f in range(HC):
                            act.wait_ge(u_filled, HC * nxt.n + f + 1)
                            if f == 0 and nxt.before(2):
                                act.wait_ge(y_filled, nxt.n - 1)
                            nc.scalar.activation(mid[nxt.slot][:, f, :], ps_u[(HC * nxt.slot + f) % 2][:, 0, :], ACT.Silu).then_inc(silu_done, 1)
                    if new.within():
                        act.wait_ge(turned, new.n + 1)
                        nc.scalar.copy(x_t[new.slot][:, :, :], ps_x[:, :, :]).then_inc(x_copied, 1)
                    if t.within():
                        act.wait_ge(y_filled, t.n + 1)
                        if t.before(2):
                            act.wait_ge(y_stored[t.slot], 16 * t.turn)
                        nc.scalar.copy(y[t.slot][:, :, :], ps_y[t.slot][:, :, :]).then_inc(y_copied, 1)

                pipeline(act, step, 2, 0, tiles)

            @block.vector
            def _(dve):
                def step(t):
                    for f in range(HC):
                        dve.wait_ge(silu_done, HC * t.n + f + 1)
                        nc.vector.tensor_tensor(mid[t.slot][:, f, :], mid[t.slot][:, f, :], ps_u[(HC * t.slot + f) % 2][:, 1, :],
                                                ALU.mult).then_inc(mid_done, 1)

                pipeline(dve, step, 0, 0, tiles)


def combine(nc, c, x, ys, weights, slots, out, out_normed):
    with ExitStack() as ctx:
        def sb(nm, shape, dt=F32):
            return ctx.enter_context(nc.sbuf_tensor(f"comb_{nm}", shape, dt))

        def sem(nm):
            return semaphore(nc, c, ctx, f"comb_{nm}")

        def ring(make, nm, *args, n=2):
            return [make(f"{nm}{k}", *args) for k in range(n)]

        x_in, res, res_n = ring(sb, "x_in", [P, TT, D]), ring(sb, "res", [P, TT, D]), ring(sb, "res_n", [P, TT, D])
        y = ring(sb, "y", [P, 2, TT, D])
        part = sb("part", [P, TT, D])
        index, share = ring(sb, "index", [P, 2, TT], I32), ring(sb, "share", [P, 2, TT])
        stats, mv = ring(sb, "stats", [P, TT, 6]), ring(sb, "mv", [P, TT, 2])
        var, rstd = sb("var", [P, TT]), ring(sb, "rstd", [P, TT])
        x_loaded, y_loaded = ring(sem, "x_loaded"), ring(sem, "y_loaded")
        indexed, parted, summed, stepped = sem("indexed"), sem("parted"), sem("summed"), sem("stepped")
        var_done, rstd_done, normed_done = sem("var_done"), sem("rstd_done"), sem("normed_done")
        res_stored, res_n_stored = ring(sem, "res_stored"), ring(sem, "res_n_stored")
        ordered, aggregating = sem("ordered"), sem("aggregating")

        with nc.Block() as block:
            @block.sync
            def _(sp):
                def step(t):
                    new, old = t.plus(1), t.plus(-1)
                    if new.within():
                        if new.before(2):
                            sp.wait_ge(parted, TT * (new.n - 1))
                        sp.dma_start(x_in[new.slot][:, :, :], x[new.n]).then_inc(x_loaded[new.slot], 16)
                    if t.within():
                        sp.wait_ge(summed, TT * (t.n + 1))
                        sp.dma_start(out[t.n], res[t.slot][:, :, :]).then_inc(res_stored[t.slot], 16)
                    if old.within():
                        sp.wait_ge(normed_done, TT * (old.n + 1))
                        sp.dma_start(out_normed[old.n], res_n[old.slot][:, :, :]).then_inc(res_n_stored[old.slot], 16)

                pipeline(sp, step, 1, 1)
                for k in range(2):
                    sp.wait_ge(res_stored[k], 16 * (BATCHES // 2))
                    sp.wait_ge(res_n_stored[k], 16 * (BATCHES // 2))

            @block.gpsimd
            def _(pool):
                def step(t):
                    new = t.plus(1)
                    if new.within():
                        if new.before(2):
                            pool.wait_ge(summed, TT * (new.n - 1))
                        pool.wait_ge(indexed, new.n + 1)
                        pool.sem_inc(ordered, 1)
                        for k in range(2):
                            for j in range(TT):
                                nc.gpsimd.indirect_dma_start(y[new.slot][:, k, j, :], None, ys[:, :], bass.IndirectOffsetOnAxis(
                                    ap=index[new.slot][:, k, j:j + 1], axis=0)).then_inc(y_loaded[new.slot], 16)
                    if t.within():
                        pool.wait_ge(stepped, 2 * (t.n + 1))
                        if t.before(1):
                            pool.wait_ge(rstd_done, t.n)
                        nc.gpsimd.tensor_tensor(var[:, :], mv[t.slot][:, :, 1], c.eps[:, :], ALU.add).then_inc(var_done, 1)
                        pool.wait_ge(var_done, t.n + 1)
                        nc.gpsimd.tensor_tensor(rstd[t.slot][:, :], var[:, :], c.minus_half[:, :], ALU.pow).then_inc(rstd_done, 1)

                pipeline(pool, step, 1, 0)

            @block.vector
            def _(dve):
                def step(t):
                    new, old = t.plus(1), t.plus(-1)
                    if new.within():
                        if new.before(2):
                            dve.wait_ge(summed, TT * (new.n - 1))
                            dve.wait_ge(y_loaded[new.slot], 16 * 2 * TT * new.turn)
                        nc.vector.tensor_copy(index[new.slot][:, :, :], slots[:, :, bass.ds(new.n * TT, TT)])
                        nc.vector.tensor_copy(share[new.slot][:, :, :], weights[:, :, bass.ds(new.n * TT, TT)]).then_inc(indexed, 1)
                    if t.within():
                        dve.wait_ge(indexed, t.n + 1)
                        dve.wait_ge(x_loaded[t.slot], 16 * (t.turn + 1))
                        dve.wait_ge(y_loaded[t.slot], 16 * 2 * TT * (t.turn + 1))
                        if t.before(1):
                            dve.wait_ge(summed, TT * t.n)
                        for j in range(TT):
                            nc.vector.scalar_tensor_tensor(part[:, j, :], y[t.slot][:, 0, j, :], share[t.slot][:, 0, j:j + 1],
                                                           x_in[t.slot][:, j, :], ALU.mult, ALU.add).then_inc(parted, 1)
                        dve.wait_ge(parted, TT * (t.n + 1))
                        if t.before(2):
                            dve.wait_ge(res_stored[t.slot], 16 * t.turn)
                            dve.wait_ge(normed_done, TT * (t.n - 1))
                        for j in range(TT):
                            nc.vector.scalar_tensor_tensor(res[t.slot][:, j, :], y[t.slot][:, 1, j, :], share[t.slot][:, 1, j:j + 1],
                                                           part[:, j, :], ALU.mult, ALU.add).then_inc(summed, 1)
                        dve.wait_ge(summed, TT * (t.n + 1))
                        for j in range(TT):
                            ins = nc.vector.bn_stats(stats[t.slot][:, j, :], res[t.slot][:, j, :])
                        ins.then_inc(stepped, 1)
                        dve.wait_ge(stepped, 2 * t.n + 1)
                        dve.sem_inc(aggregating, 1)
                        for j in range(TT):
                            ins = nc.vector.bn_aggr(mv[t.slot][:, j, :], stats[t.slot][:, j, :])
                        ins.then_inc(stepped, 1)
                    if old.within():
                        dve.wait_ge(rstd_done, old.n + 1)
                        if old.before(2):
                            dve.wait_ge(res_n_stored[old.slot], 16 * old.turn)
                        for j in range(TT):
                            nc.vector.tensor_scalar(res_n[old.slot][:, j, :], res[old.slot][:, j, :], mv[old.slot][:, j, 0:1],
                                                    rstd[old.slot][:, j:j + 1], ALU.subtract, ALU.mult).then_inc(normed_done, 1)

                pipeline(dve, step, 1, 1)


def memory_table(nc, c, ctx_t, wkv, table):
    with ExitStack() as ctx:
        def sb(nm, shape, dt=F32):
            return ctx.enter_context(nc.sbuf_tensor(f"table_{nm}", shape, dt))

        def sem(nm):
            return semaphore(nc, c, ctx, f"table_{nm}")

        NT = BATCHES * TT
        rows_t, w = sb("rows_t", [P, DC, TOKENS]), sb("w", [P, DC, 2 * HD])
        rows = sb("rows", [P, NT, MEM_WORDS])
        halves = rows[:, :, 0:KEY_WORDS].bitcast(F16)
        ps_kv = ctx.enter_context(nc.psum_tensor("table_ps_kv", [P, NT, 2 * HD], F32))
        loaded, cleared, filled, done, stored = sem("loaded"), sem("cleared"), sem("filled"), sem("done"), sem("stored")

        with nc.Block() as block:
            @block.sync
            def _(sp):
                sp.dma_start(w[:, :, :], wkv.rearrange("(c p) f -> p c f", p=P)).then_inc(loaded, 16)
                sp.dma_start(rows_t[:, :, :], ctx_t.rearrange("(c p) s -> p c s", p=P)).then_inc(loaded, 16)
                sp.wait_ge(done, 5)
                sp.dma_start(table.rearrange("(t p) w -> p t w", p=P), rows[:, :, :]).then_inc(stored, 16)
                sp.wait_ge(stored, 16)

            @block.tensor
            def _(pe):
                pe.wait_ge(loaded, 32)
                for t in range(NT):
                    for dc in range(DC):
                        mm = nc.tensor.matmul(ps_kv[:, t, :], rows_t[:, dc, t * P:(t + 1) * P], w[:, dc, :],
                                              start=(dc == 0), stop=(dc == DC - 1))
                mm.then_inc(filled, 1)

            @block.vector
            def _(dve):
                nc.vector.memset(rows[:, :, :], 0.0).then_inc(cleared, 1)
                dve.wait_ge(cleared, 1)
                nc.vector.memset(rows[:, :, KEY_WORDS + HD], 1.0)
                nc.vector.memset(halves[:, :, STACK], 1.0).then_inc(done, 1)
                dve.wait_ge(filled, 1)
                for part in range(2):
                    nc.vector.tensor_copy(halves[:, :, part * HD:(part + 1) * HD], ps_kv[:, :, 0:HD]).then_inc(done, 1)
                dve.wait_ge(done, 3)
                nc.vector.tensor_tensor(halves[:, :, 2 * HD:STACK], ps_kv[:, :, 0:HD], halves[:, :, 0:HD],
                                        ALU.subtract).then_inc(done, 1)
                nc.vector.tensor_copy(rows[:, :, KEY_WORDS:KEY_WORDS + HD], ps_kv[:, :, HD:2 * HD]).then_inc(done, 1)


def mixture(nc, c, att, wc, xb, centroids, biases, wr, br, ws, bs, out):
    with ExitStack() as ctx:
        def sb(nm, shape, dt=F32):
            return ctx.enter_context(nc.sbuf_tensor(f"mix_{nm}", shape, dt))

        def ps(nm, shape, dt=F32):
            return ctx.enter_context(nc.psum_tensor(f"mix_{nm}", shape, dt))

        def sem(nm):
            return semaphore(nc, c, ctx, f"mix_{nm}")

        def ring(make, nm, *args, n=2):
            return [make(f"{nm}{k}", *args) for k in range(n)]

        E = centroids.shape[1]
        SHARED = ws.shape[0]
        G = E + 1
        QUADS = E // 2
        FILLS = QUADS * TT
        ADDS = 2 * FILLS
        RING = 4
        wc_sb, cent_sb = sb("wc", [P, DC, D]), sb("centroids", [P, DC, E])
        wr_sb = sb("wr", [P, DC, E, D])
        ws_sb = [sb(f"ws{k}", [P, DC, D]) for k in range(SHARED)]
        b_sb, bs_sb = sb("b", [G, D]), [sb(f"bs{k}", [1, D]) for k in range(SHARED)]
        eb_sb, numbers = sb("biases", [P, E]), sb("numbers", [P, E])
        att_in, xb_in = ring(sb, "att_in", [P, TT, D]), ring(sb, "xb_in", [P, TT, D])
        att_t, u_t = ring(sb, "att_t", [P, DC, SEQ]), ring(sb, "u_t", [P, DC, SEQ])
        xc, u, base = ring(sb, "xc", [P, TT, D]), ring(sb, "u", [P, TT, D]), ring(sb, "base", [P, TT, D])
        stats, mv = sb("stats", [P, TT, 6]), sb("mv", [P, TT, 2])
        var, rstd = sb("var", [P, TT]), sb("rstd", [P, TT])
        score, top, top_at = sb("score", [P, TT, E]), sb("top", [P, TT, 8]), sb("top_at", [P, TT, 8], U32)
        chosen_at, neg_top = sb("chosen_at", [P, TT, 2]), sb("neg_top", [P, TT])
        chosen = [sb(f"chosen{k}", [P, TT, E]) for k in range(2)]
        exps, exp_sum, recip = sb("exps", [P, TT, E]), sb("exp_sum", [P, TT]), sb("recip", [P, TT])
        probs = ring(sb, "probs", [P, TT, G])
        probs_t = ring(sb, "probs_t", [G, SEQ])
        acc = ring(sb, "acc", [P, TT, D])

        ps_t, ps_c = ps("ps_t", [P, DC, SEQ]), ps("ps_c", [P, TT, D])
        ps_s, ps_b = ps("ps_s", [P, BANK]), ps("ps_b", [P, TT, D])
        ps_e = ring(ps, "ps_e", [P, 2, D], n=RING)
        ps_scores = ps_s[:, 0:TT * E].rearrange("p (t e) -> p t e", t=TT)
        ps_probs = ps_s[0:G, 0:SEQ]

        params_loaded, set_up = sem("params_loaded"), sem("set_up")
        att_loaded, xb_loaded = ring(sem, "att_loaded"), ring(sem, "xb_loaded")
        t_filled, t_emptied, c_filled, xc_done = sem("t_filled"), sem("t_emptied"), sem("c_filled"), sem("xc_done")
        s_filled, s_emptied, b_filled, b_emptied = sem("s_filled"), sem("s_emptied"), sem("b_filled"), sem("b_emptied")
        stepped, var_done, rstd_done, u_done = sem("stepped"), sem("var_done"), sem("rstd_done"), sem("u_done")
        based, exps_done, probs_done = sem("based"), sem("exps_done"), sem("probs_done")
        e_filled, added, ordered = sem("e_filled"), sem("added"), sem("ordered")
        out_stored = ring(sem, "out_stored")
        PARAMS = 6 + 2 * SHARED - 1
        STEPS = 10
        XC_AT, U_AT, CHOOSE_AT = 1, 3, 5

        with nc.Block() as block:
            @block.sync
            def _(sp):
                sp.dma_start(wc_sb[:, :, :], wc.rearrange("(c p) f -> p c f", p=P)).then_inc(params_loaded, 16)
                sp.dma_start(cent_sb[:, :, :], centroids.rearrange("(c p) f -> p c f", p=P)).then_inc(params_loaded, 16)
                sp.dma_start(wr_sb[:, :, :, :].rearrange("p c e o -> p c (e o)"),
                             wr.rearrange("(c p) f -> p c f", p=P)).then_inc(params_loaded, 16)
                sp.dma_start(eb_sb[:, :], biases.partition_broadcast(P)).then_inc(params_loaded, 16)
                sp.dma_start(b_sb[1:G, :], br).then_inc(params_loaded, 16)
                for k in range(SHARED):
                    sp.dma_start(ws_sb[k][:, :, :], ws[k].rearrange("(c p) f -> p c f", p=P)).then_inc(params_loaded, 16)
                    sp.dma_start(bs_sb[k][:, :], bs[k:k + 1, :]).then_inc(params_loaded, 16)

                def step(t):
                    new, old = t.plus(2), t.plus(-1)
                    if new.within():
                        if new.before(2):
                            sp.wait_ge(t_filled, 2 * (new.n - 2) + 1)
                        sp.dma_start(att_in[new.slot][:, :, :], att[new.n]).then_inc(att_loaded[new.slot], 16)
                        if new.before(2):
                            sp.wait_ge(xc_done, new.n - 1)
                        sp.dma_start(xb_in[new.slot][:, :, :], xb[new.n]).then_inc(xb_loaded[new.slot], 16)
                    if old.within():
                        sp.wait_ge(added, ADDS * (old.n + 1))
                        sp.dma_start(out[old.n], acc[old.slot][:, :, :]).then_inc(out_stored[old.slot], 16)

                pipeline(sp, step, 2, 1)
                for k in range(2):
                    sp.wait_ge(out_stored[k], 16 * (BATCHES // 2))

            @block.tensor
            def _(pe):
                pe.wait_ge(params_loaded, 16 * PARAMS)
                pe.wait_ge(set_up, 3)
                pe.wait_ge(ordered, 3)

                def turn(src):
                    for k in range(TT):
                        for dc in range(DC):
                            mm = nc.tensor.transpose(ps_t[:, dc, k * P:(k + 1) * P], src[:, k, dc * P:(dc + 1) * P], c.ident[:, :])
                    mm.then_inc(t_filled, 1)

                def product(to, lhs_t, rhs, stop=True):
                    for k in range(TT):
                        for dc in range(DC):
                            mm = nc.tensor.matmul(to[:, k, :], lhs_t[:, dc, k * P:(k + 1) * P], rhs[:, dc, :],
                                                  start=(dc == 0), stop=(dc == DC - 1))
                    return mm

                def pair_of_experts(t, q, k):
                    fill = TT * q + k
                    if fill >= RING or t.before(1):
                        pe.wait_ge(added, ADDS * t.n + 2 * TT * ((fill - RING) // TT + 1))
                    for dc in range(DC):
                        mm = nc.tensor.matmul(ps_e[fill % RING][:, :, :], u_t[t.slot][:, dc, k * P:(k + 1) * P],
                                              wr_sb[:, dc, 2 * q:2 * q + 2, :], start=(dc == 0), stop=(dc == DC - 1))
                    mm.then_inc(e_filled, 1)

                def shared(t):
                    pe.wait_ge(s_emptied, 2 * (t.n + 1))
                    if t.before(1):
                        pe.wait_ge(b_emptied, t.n)
                    for k in range(TT):
                        nc.tensor.matmul(ps_b[:, k, :], probs_t[t.slot][:, k * P:(k + 1) * P], b_sb[:, :], start=True, stop=False)
                        for dc in range(DC):
                            mm = nc.tensor.matmul(ps_b[:, k, :], u_t[t.slot][:, dc, k * P:(k + 1) * P], ws_sb[0][:, dc, :],
                                                  start=False, stop=(dc == DC - 1))
                    mm.then_inc(b_filled, 1)

                def front(t, q):
                    if q == 0:
                        pe.wait_ge(att_loaded[t.slot], 16 * (t.turn + 1))
                        if t.before(1):
                            pe.wait_ge(t_emptied, 2 * t.n)
                        turn(att_in[t.slot])
                    if q == XC_AT:
                        pe.wait_ge(t_emptied, 2 * t.n + 1)
                        if t.before(1):
                            pe.wait_ge(xc_done, t.n)
                        product(ps_c, att_t[t.slot], wc_sb).then_inc(c_filled, 1)
                    if q == U_AT + 1:
                        pe.wait_ge(u_done, TT * (t.n + 1))
                        pe.wait_ge(t_emptied, 2 * t.n + 1)
                        turn(u[t.slot])
                    if q == CHOOSE_AT:
                        pe.wait_ge(t_emptied, 2 * t.n + 2)
                        if t.before(1):
                            pe.wait_ge(s_emptied, 2 * t.n)
                        product(ps_scores, u_t[t.slot], cent_sb).then_inc(s_filled, 1)
                    if q == QUADS - 1:
                        pe.wait_ge(probs_done, t.n + 1)
                        pe.wait_ge(s_emptied, 2 * t.n + 1)
                        for k in range(TT):
                            mm = nc.tensor.transpose(ps_probs[:, k * P:(k + 1) * P], probs[t.slot][:, k, :], c.ident[:, :])
                        mm.then_inc(s_filled, 1)

                def step(t):
                    nxt = t.plus(1)
                    for q in range(QUADS):
                        if t.within():
                            if q == 0:
                                shared(t)
                            for k in range(TT):
                                pair_of_experts(t, q, k)
                        if nxt.within():
                            front(nxt, q)

                pipeline(pe, step, 1, 0)

            @block.scalar
            def _(act):
                def step(t):
                    nxt = t.plus(1)
                    if not nxt.within():
                        return
                    t = nxt
                    for k, to in enumerate((att_t, u_t)):
                        act.wait_ge(t_filled, 2 * t.n + k + 1)
                        if k == 0 and t.before(2):
                            act.wait_ge(c_filled, t.n - 1)
                        if k == 1 and t.before(2):
                            act.wait_ge(e_filled, FILLS * (t.n - 1))
                        nc.scalar.copy(to[t.slot][:, :, :], ps_t[:, :, :]).then_inc(t_emptied, 1)
                    act.wait_ge(stepped, STEPS * t.n + 6)
                    if t.before(1):
                        act.wait_ge(probs_done, t.n)
                    for k in range(TT):
                        ins = nc.scalar.activation(exps[:, k, :], score[:, k, :], ACT.Exp, bias=neg_top[:, k:k + 1])
                    ins.then_inc(exps_done, 1)
                    act.wait_ge(s_filled, 2 * t.n + 2)
                    if t.before(2):
                        act.wait_ge(b_filled, t.n - 1)
                    nc.scalar.copy(probs_t[t.slot][:, :], ps_probs).then_inc(s_emptied, 1)

                pipeline(act, step, 1, 0)

            @block.vector
            def _(dve):
                dve.wait_ge(params_loaded, 16 * PARAMS)
                nc.vector.tensor_tensor(ws_sb[0][:, :, :], ws_sb[0][:, :, :], ws_sb[1][:, :, :], ALU.add).then_inc(set_up, 1)
                nc.vector.tensor_tensor(bs_sb[0][:, :], bs_sb[0][:, :], bs_sb[1][:, :], ALU.add).then_inc(set_up, 1)
                dve.wait_ge(set_up, 3)
                nc.vector.tensor_scalar(ws_sb[0][:, :, :], ws_sb[0][:, :, :], 1.0 / SHARED, None, ALU.mult).then_inc(ordered, 1)
                nc.vector.tensor_scalar(b_sb[0:1, :], bs_sb[0][:, :], 1.0 / SHARED, None, ALU.mult).then_inc(ordered, 1)
                for k in range(2):
                    ins = nc.vector.memset(probs[k][:, :, 0], 1.0)
                ins.then_inc(ordered, 1)

                def add_pair(t, q):
                    for j in range(2):
                        for k in range(TT):
                            if j == 0:
                                dve.wait_ge(e_filled, FILLS * t.n + TT * q + k + 1)
                            at = TT * (2 * q + j) + k
                            if at >= TT:
                                dve.wait_ge(added, ADDS * t.n + at - TT + 1)
                            elif k == 0:
                                dve.wait_ge(b_emptied, t.n + 1)
                            nc.vector.scalar_tensor_tensor(acc[t.slot][:, k, :], ps_e[(TT * q + k) % RING][:, j, :],
                                                           probs[t.slot][:, k, 1 + 2 * q + j:2 + 2 * q + j], acc[t.slot][:, k, :],
                                                           ALU.mult, ALU.add).then_inc(added, 1)

                def front(t, q):
                    if q == XC_AT:
                        dve.wait_ge(c_filled, t.n + 1)
                        dve.wait_ge(xb_loaded[t.slot], 16 * (t.turn + 1))
                        if t.before(2):
                            dve.wait_ge(based, t.n - 1)
                        nc.vector.tensor_tensor(xc[t.slot][:, :, :], ps_c[:, :, :], xb_in[t.slot][:, :, :], ALU.add).then_inc(xc_done, 1)
                        dve.wait_ge(xc_done, t.n + 1)
                        for k in range(TT):
                            ins = nc.vector.bn_stats(stats[:, k, :], xc[t.slot][:, k, :])
                        ins.then_inc(stepped, 1)
                        dve.wait_ge(stepped, STEPS * t.n + 1)
                        dve.sem_inc(stepped, 1)
                        for k in range(TT):
                            ins = nc.vector.bn_aggr(mv[:, k, :], stats[:, k, :])
                        ins.then_inc(stepped, 1)
                    if q == U_AT:
                        dve.wait_ge(rstd_done, t.n + 1)
                        if t.before(2):
                            dve.wait_ge(t_filled, 2 * (t.n - 1))
                        for k in range(TT):
                            nc.vector.tensor_scalar(u[t.slot][:, k, :], xc[t.slot][:, k, :], mv[:, k, 0:1], rstd[:, k:k + 1],
                                                    ALU.subtract, ALU.mult).then_inc(u_done, 1)
                    if q == CHOOSE_AT:
                        dve.wait_ge(s_filled, 2 * t.n + 1)
                        if t.before(1):
                            dve.wait_ge(exps_done, t.n)
                        nc.vector.tensor_tensor(score[:, :, :], ps_scores, eb_sb[:, :].unsqueeze(1).to_broadcast([P, TT, E]),
                                                ALU.add).then_inc(s_emptied, 1)
                        dve.wait_ge(s_emptied, 2 * t.n + 1)
                        dve.sem_inc(stepped, 1)
                        for k in range(TT):
                            ins = nc.vector.max(top[:, k, :], score[:, k, :])
                        ins.then_inc(stepped, 1)
                        dve.wait_ge(stepped, STEPS * t.n + 5)
                        nc.vector.tensor_scalar(neg_top[:, :], top[:, :, 0], -1.0, None, ALU.mult).then_inc(stepped, 1)
                        for k in range(TT):
                            ins = nc.vector.max_index(top_at[:, k, :], top[:, k, :], score[:, k, :])
                        ins.then_inc(stepped, 1)
                        dve.wait_ge(stepped, STEPS * t.n + 7)
                        nc.vector.tensor_copy(chosen_at[:, :, :], top_at[:, :, 0:2]).then_inc(stepped, 1)
                        dve.wait_ge(stepped, STEPS * t.n + 8)
                        for k in range(2):
                            ins = nc.vector.tensor_tensor(chosen[k][:, :, :], numbers[:, :].unsqueeze(1).to_broadcast([P, TT, E]),
                                                          chosen_at[:, :, k:k + 1].to_broadcast([P, TT, E]), ALU.is_equal)
                        ins.then_inc(stepped, 1)
                        dve.wait_ge(stepped, STEPS * t.n + 9)
                        nc.vector.tensor_tensor(chosen[0][:, :, :], chosen[0][:, :, :], chosen[1][:, :, :], ALU.add).then_inc(stepped, 1)
                    if q == CHOOSE_AT + 1:
                        dve.wait_ge(exps_done, t.n + 1)
                        nc.vector.tensor_reduce(exp_sum[:, :], exps[:, :, :], AX.X, ALU.add).then_inc(ordered, 1)
                        dve.wait_ge(ordered, 3 * t.n + 4)
                        nc.vector.reciprocal(recip[:, :], exp_sum[:, :]).then_inc(ordered, 1)
                        dve.wait_ge(stepped, STEPS * (t.n + 1))
                        nc.vector.tensor_tensor(chosen[0][:, :, :], chosen[0][:, :, :], exps[:, :, :], ALU.mult).then_inc(ordered, 1)
                        dve.wait_ge(ordered, 3 * t.n + 6)
                        if t.before(2):
                            dve.wait_ge(added, ADDS * (t.n - 1))
                        nc.vector.tensor_tensor(probs[t.slot][:, :, 1:G], chosen[0][:, :, :],
                                                recip[:, :].unsqueeze(2).to_broadcast([P, TT, E]), ALU.mult).then_inc(probs_done, 1)

                def step(t):
                    nxt = t.plus(1)
                    if t.within():
                        dve.wait_ge(b_filled, t.n + 1)
                        dve.wait_ge(based, t.n + 1)
                        if t.before(2):
                            dve.wait_ge(out_stored[t.slot], 16 * t.turn)
                        nc.vector.tensor_tensor(acc[t.slot][:, :, :], ps_b[:, :, :], base[t.slot][:, :, :], ALU.add).then_inc(b_emptied, 1)
                    for q in range(QUADS):
                        if t.within():
                            add_pair(t, q)
                        if nxt.within():
                            front(nxt, q)

                dve.wait_ge(set_up, 3)
                pipeline(dve, step, 1, 0)

            @block.gpsimd
            def _(pool):
                nc.gpsimd.iota(numbers[:, :], [[1, E]], 0, 0, allow_small_or_imprecise_dtypes=True).then_inc(set_up, 1)

                def step(t):
                    if t.before(1):
                        pool.wait_ge(rstd_done, t.n)
                    pool.wait_ge(stepped, STEPS * t.n + 3)
                    nc.gpsimd.tensor_tensor(var[:, :], mv[:, :, 1], c.eps[:, :], ALU.add).then_inc(var_done, 1)
                    pool.wait_ge(var_done, t.n + 1)
                    nc.gpsimd.tensor_tensor(rstd[:, :], var[:, :], c.minus_half[:, :], ALU.pow).then_inc(rstd_done, 1)
                    pool.wait_ge(u_done, TT * (t.n + 1))
                    if t.before(2):
                        pool.wait_ge(b_emptied, t.n - 1)
                    nc.gpsimd.tensor_tensor(base[t.slot][:, :, :], xc[t.slot][:, :, :], u[t.slot][:, :, :], ALU.add).then_inc(based, 1)

                pipeline(pool, step, 0, 0)


def program(nc, i, out):
    ctx = ExitStack()
    with ctx:
        def sb(name, shape, dt=F32):
            return ctx.enter_context(nc.sbuf_tensor(name, shape, dt))

        def dram(name, shape, dt=F32):
            return nc.dram_tensor(name, shape, dt, kind="Internal").ap()

        c = Constants(sb)
        E = i["gate"].shape[1]
        tiles = (2 * TOKENS + E * (SEQ - 1)) // SEQ
        xs, ys = dram("xs", [tiles * SEQ, D]), dram("ys", [tiles * SEQ, D])
        zeroed = ctx.enter_context(nc.semaphore("zeroed"))
        constants(nc, c, ctx.enter_context(nc.semaphore("constants_done")), xs, zeroed)
        rows = [BATCHES, P, TT, D]
        h0 = dram("h0", rows)
        normalize_input(nc, c, i["x"], h0)
        table = dram("table", [TOKENS, MEM_WORDS])
        memory_table(nc, c, i["ctx_t"], i["mem_wkv"], table)
        x1 = dram("x1", rows)
        attention(nc, c, "self", True, h0, (i["L0_xattn_Wq1"], i["L0_xattn_Wk1"], i["L0_xattn_Wv1"]), x1, None,
                  i["L0_xattn_bv1"], i["L0_xattn_g1"], i["L0_xattn_be1"])
        x2 = dram("x2", rows)
        attention(nc, c, "cross", False, x1, (i["L0_xattn_Wq2"], i["L0_xattn_Wk2"], i["L0_xattn_Wv2"]), x2, i["ctx_t"],
                  i["L0_xattn_bv2"], i["L0_xattn_g2"], i["L0_xattn_be2"])
        xa, hm = dram("xa", rows), dram("hm", rows)
        logits = sb("logits", [P, BATCHES * TT, E])
        feed_forward(nc, c, x2, i["x"], i["L0_xattn_Wf1"], i["bf1"], i["L0_xattn_Wf2"], i["L0_xattn_bf2"], i["L0_xattn_g3"], i["L0_xattn_be3"],
                     i["gate"], xa, hm, logits)
        clear_counted(nc, c)
        shares, slots = sb("shares", [P, 2, BATCHES * TT]), sb("slots", [P, 2, BATCHES * TT], I32)
        tile_expert = sb("tile_expert", [1, tiles], I32)
        route(nc, c, logits, hm, xs, shares, slots, tile_expert, zeroed)
        experts(nc, c, xs, i["moe_w13"], i["moe_w2"], tile_expert, ys)
        xb, h2 = dram("xb", rows), dram("h2", rows)
        combine(nc, c, xa, ys, shares, slots, xb, h2)
        att = dram("att", rows)
        attention(nc, c, "memory", False, h2, (i["mem_wq"],), att, i["ctx_t"], memory=table)
        mixture(nc, c, att, i["mem_wc"], xb, i["centroids"], i["L1_ffn_expert_biases"], i["mix_wr"], i["L1_ffn_br"], i["mix_ws"], i["L1_ffn_bs"],
                out.rearrange("b (t p) d -> b p t d", p=P))


def kernel(**inputs):
    import numpy as np
    import concourse.bacc as bacc
    from concourse.bass_utils import run_bass_kernel_spmd

    a = {k: np.asarray(x) for k, x in inputs.items()}

    def heads_last(w):
        return np.ascontiguousarray(w.transpose(1, 0, 2).reshape(D, D))

    laid = {"x": a["x"].reshape(TOKENS, D), "ctx_t": np.ascontiguousarray(a["ctx_1024"].reshape(TOKENS, D).T)}
    for n in "12":
        for w in "qkv":
            laid[f"L0_xattn_W{w}{n}"] = heads_last(a[f"L0_xattn_W{w}{n}"])
        laid[f"L0_xattn_bv{n}"] = a[f"L0_xattn_bv{n}"].reshape(D)
    for n in "123":
        laid[f"L0_xattn_g{n}"] = a[f"L0_xattn_g{n}"]
        laid[f"L0_xattn_be{n}"] = a[f"L0_xattn_be{n}"]
    for n in ("Wf1", "Wf2", "bf2"):
        laid[f"L0_xattn_{n}"] = a[f"L0_xattn_{n}"]
    laid["bf1"] = a["L0_xattn_bf1"].reshape(-1, P).T
    laid["gate"] = a["L0_ffn_gate_w"].T

    def by_partition(w):
        e, o, n = w.shape
        return w.transpose(0, 2, 1).reshape(e, n // P, P, o).transpose(0, 2, 1, 3)

    E = a["L0_ffn_W1"].shape[0]
    laid["moe_w13"] = np.stack([by_partition(a["L0_ffn_W1"]), by_partition(a["L0_ffn_W3"])], axis=2).reshape(E, P, -1)
    laid["moe_w2"] = by_partition(a["L0_ffn_W2"])

    laid["mem_wq"], laid["mem_wkv"], laid["mem_wc"] = (a[f"L1_xattn_{n}"].T for n in ("Wq", "Wkv", "Wc"))
    laid["centroids"] = a["L1_ffn_centroids"].T
    laid["mix_wr"] = a["L1_ffn_Wr"].transpose(2, 0, 1).reshape(D, -1)
    laid["mix_ws"] = a["L1_ffn_Ws"].transpose(0, 2, 1)
    for n in ("expert_biases", "br", "bs"):
        laid[f"L1_ffn_{n}"] = a[f"L1_ffn_{n}"]

    nc = bacc.Bacc("TRN2", target_bir_lowering=False, num_devices=1)
    arrays = {f"in_{k}": np.ascontiguousarray(x) for k, x in laid.items()}
    i = {k: nc.dram_tensor(f"in_{k}", x.shape, mybir.dt.from_np(x.dtype), kind="ExternalInput").ap()
         for k, x in laid.items()}
    out = nc.dram_tensor("out", (BATCHES, SEQ, D), F32, kind="ExternalOutput").ap()
    program(nc, i, out)
    r = run_bass_kernel_spmd(nc, [arrays], core_ids=[0])
    return r.results[0]["out"]
```

```python
import concourse.bass as bass
from concourse import mybir
from contextlib import ExitStack

F32 = mybir.dt.float32
F16 = mybir.dt.float16
BF16 = mybir.dt.bfloat16
U32 = mybir.dt.uint32
I32 = mybir.dt.int32
ALU = mybir.AluOpType
ACT = mybir.ActivationFunctionType
AX = mybir.AxisListType

P = 128
BATCHES = 8
SEQ = 256
TOKENS = BATCHES * SEQ
D = 256
TT = SEQ // P
DC = D // P
HEADS = 16
HD = D // HEADS
VW = 32
PAIRS = HEADS // 2
GROUP = P // VW
GROUPS = HEADS // GROUP
KEY_WORDS = 32
MEM_WORDS = KEY_WORDS + VW
HALF = HEADS // 2
SCALE = HD ** -0.5
EPS = 1e-5
LIFT = 64.0
HI, LO = 0, 1
PRODUCTS = ((HI, HI), (HI, LO), (LO, HI))
MASKED = -1e30
BANK = 512
STACK = 3 * HD
ROWS = STACK + 1


class Turn:

    def __init__(self, pairs, offset, count=BATCHES):
        self.pairs, self.offset, self.count = pairs, offset, count
        self.n = pairs * 2 + offset
        self.slot = offset % 2
        self.turn = pairs + offset // 2

    def plus(self, k):
        return Turn(self.pairs, self.offset + k, self.count)

    def within(self):
        return not isinstance(self.n, int) or 0 <= self.n < self.count

    def before(self, k):
        return not isinstance(self.n, int) or self.n >= k


def pipeline(eng, step, lead, tail, count=BATCHES):
    first, last = max((tail + 1) // 2, 1), (count - lead) // 2
    if last - first < 2:
        last = first
    for n in range(-lead, 2 * first):
        step(Turn(0, n, count))
    if last > first:
        with eng.Fori(first, last) as pairs:
            for k in range(2):
                step(Turn(pairs, k, count))
    for n in range(2 * last, count + tail):
        step(Turn(last, n - 2 * last, count))


class Constants:

    def __init__(self, sb):
        self.ident, self.ident_bf, self.ident_h = sb("ident", [P, P]), sb("ident_bf", [P, P], BF16), sb("ident_h", [P, P], F16)
        self.mask_st, self.mask_ts = sb("mask_st", [P, P], BF16), sb("mask_ts", [P, P], BF16)
        self.minus_half, self.eps = sb("minus_half", [P, TT]), sb("eps", [P, TT])
        self.zeros = sb("zeros", [P, D])
        self.counted = []


def semaphore(nc, c, ctx, name):
    sem = ctx.enter_context(nc.semaphore(name))
    c.counted.append(sem.num)
    return sem


def clear_counted(nc, c):
    nums = sorted(c.counted)
    starts = [n for n in nums if n - 1 not in nums]
    with nc.Block() as block:
        @block.gpsimd
        def _(pool):
            for first in starts:
                end = first
                while end in nums:
                    end += 1
                pool.sem_clear(range(first, end))
    c.counted.clear()


def constants(nc, c, done):
    with nc.Block() as block:
        @block.gpsimd
        def _(pool):
            nc.gpsimd.memset(c.ident[:, :], 0.0).then_inc(done, 1)
            nc.gpsimd.memset(c.ident_bf[:, :], 0.0).then_inc(done, 1)
            nc.gpsimd.memset(c.mask_st[:, :], 0.0).then_inc(done, 1)
            nc.gpsimd.memset(c.mask_ts[:, :], 0.0).then_inc(done, 1)
            nc.gpsimd.memset(c.minus_half[:, :], -0.5).then_inc(done, 1)
            nc.gpsimd.memset(c.eps[:, :], EPS).then_inc(done, 1)
            nc.gpsimd.memset(c.zeros[:, :], 0.0).then_inc(done, 1)
            nc.gpsimd.memset(c.ident_h[:, :], 0.0).then_inc(done, 1)
            pool.wait_ge(done, 8)
            for m in (c.ident, c.ident_bf, c.ident_h):
                nc.gpsimd.affine_select(out=m[:, :], in_=m[:, :], compare_op=ALU.not_equal, fill=1.0, base=0,
                                        pattern=[[-1, P]], channel_multiplier=1).then_inc(done, 1)
            nc.gpsimd.affine_select(out=c.mask_st[:, :], in_=c.mask_st[:, :], compare_op=ALU.is_ge, fill=MASKED,
                                    base=0, pattern=[[-1, P]], channel_multiplier=1).then_inc(done, 1)
            nc.gpsimd.affine_select(out=c.mask_ts[:, :], in_=c.mask_ts[:, :], compare_op=ALU.is_ge, fill=MASKED,
                                    base=0, pattern=[[1, P]], channel_multiplier=-1).then_inc(done, 1)
            pool.wait_ge(done, 13)


def prepare(nc, c, x, normed, ctx_t, ctx_hl, wkv, table, matrices, shared, shared_hl):
    with ExitStack() as ctx:
        def sb(nm, shape, dt=F32):
            return ctx.enter_context(nc.sbuf_tensor(f"prep_{nm}", shape, dt))

        def sem(nm):
            return semaphore(nc, c, ctx, f"prep_{nm}")

        def ring(make, nm, *args, n=2):
            return [make(f"{nm}{k}", *args) for k in range(n)]

        NT = BATCHES * TT
        PIECE = 2048
        pieces = [(src[:, at:min(at + PIECE, src.shape[1])], hl[:, :, at:min(at + PIECE, src.shape[1])]) for src, hl in matrices
                  for at in range(0, src.shape[1], PIECE)]
        POOL_FROM = len(matrices) + 1
        raw = [sb(f"raw{n}", [P, frm.shape[1]]) for n, (frm, _) in enumerate(pieces)]
        mean = [sb(f"mean{k}", [P, shared.shape[2]]) for k in range(2)]
        xt = ring(sb, "x", [P, TT, D], n=BATCHES)
        stats, mv = ring(sb, "stats", [P, TT, 6]), ring(sb, "mv", [P, TT, 2])
        var, rstd = ring(sb, "var", [P, TT]), ring(sb, "rstd", [P, TT])
        rows_t, w = sb("rows_t", [P, DC, TOKENS]), sb("w", [P, DC, 2 * HD])
        rows_hl = sb("rows_hl", [P, 2, DC, TOKENS], F16)
        rows = sb("rows", [P, NT, MEM_WORDS])
        halves = rows[:, :, 0:KEY_WORDS].bitcast(F16)
        ps_kv = ctx.enter_context(nc.psum_tensor("prep_ps_kv", [P, NT, 2 * HD], F32))

        x_loaded, x_stored = ring(sem, "x_loaded", n=BATCHES), sem("x_stored")
        stats_done, aggregated, var_done = sem("stats_done"), sem("aggregated"), sem("var_done")
        rstd_done, applied = sem("rstd_done"), sem("applied")
        rows_loaded, cleared, filled, table_done, table_stored = (sem(n) for n in (
            "rows_loaded", "cleared", "filled", "table_done", "table_stored"))
        raw_loaded, hi_done = ring(sem, "raw_loaded", n=len(pieces)), sem("hi_done")
        mean_loaded, summed = sem("mean_loaded"), sem("summed")
        lifted = sem("lifted")
        rows_hi, rows_split, rows_stored = sem("rows_hi"), sem("rows_split"), sem("rows_stored")
        src = x.rearrange("(b t p) d -> b p t d", b=BATCHES, p=P)

        with nc.Block() as block:
            @block.sync
            def _(sp):
                for n in range(BATCHES):
                    sp.dma_start(xt[n][:, :, :], src[n]).then_inc(x_loaded[n], 16)
                for n in range(BATCHES):
                    sp.wait_ge(applied, TT * (n + 1))
                    sp.dma_start(normed[n], xt[n][:, :, :]).then_inc(x_stored, 16)
                sp.wait_ge(table_done, 5)
                sp.dma_start(table.rearrange("(t p) w -> p t w", p=P), rows[:, :, :]).then_inc(table_stored, 16)
                sp.wait_ge(rows_split, DC)
                sp.dma_start(ctx_hl.rearrange("l (c p) s -> p (l c) s", p=P),
                             rows_hl[:, :, :, :].rearrange("p l c s -> p (l c) s")).then_inc(rows_stored, 16)
                sp.wait_ge(table_stored, 16)
                sp.wait_ge(rows_stored, 16)
                sp.wait_ge(x_stored, 16 * BATCHES)

            @block.tensor
            def _(pe):
                pe.wait_ge(rows_loaded, 32)
                for t in range(NT):
                    for dc in range(DC):
                        mm = nc.tensor.matmul(ps_kv[:, t, :], rows_t[:, dc, t * P:(t + 1) * P], w[:, dc, :],
                                              start=(dc == 0), stop=(dc == DC - 1))
                mm.then_inc(filled, 1)

            @block.scalar
            def _(act):
                def load(n):
                    act.dma_start(raw[n][:, :], pieces[n][0]).then_inc(raw_loaded[n], 16)

                for n in range(3):
                    load(n)
                act.dma_start(w[:, :, :], wkv.rearrange("(c p) f -> p c f", p=P)).then_inc(rows_loaded, 16)
                act.dma_start(rows_t[:, :, :], ctx_t.rearrange("(c p) s -> p c s", p=P)).then_inc(rows_loaded, 16)
                for n in range(3, len(pieces)):
                    load(n)
                for k in range(2):
                    act.dma_start(mean[k][:, :], shared[k]).then_inc(mean_loaded, 16)
                for n, (_, hl) in enumerate(pieces):
                    if n == POOL_FROM // 2:
                        act.wait_ge(rows_loaded, 32)
                        for dc in range(DC):
                            nc.scalar.copy(rows_hl[:, HI, dc, :], rows_t[:, dc, :]).then_inc(rows_hi, 1)
                    act.wait_ge(raw_loaded[n], 16)
                    if n < POOL_FROM:
                        nc.scalar.activation(hl[:, HI, :], raw[n][:, :], ACT.Copy, scale=LIFT).then_inc(hi_done, 1)
                    else:
                        nc.scalar.activation(raw[n][:, :], raw[n][:, :], ACT.Copy, scale=LIFT).then_inc(lifted, 1)
                        act.wait_ge(lifted, n - POOL_FROM + 1)
                        nc.scalar.copy(hl[:, HI, :], raw[n][:, :]).then_inc(hi_done, 1)
                act.wait_ge(summed, 1)
                nc.scalar.activation(shared_hl[:, 0, :], mean[0][:, :], ACT.Copy, scale=LIFT / 2).then_inc(hi_done, 1)

            @block.vector
            def _(dve):
                def low_part(n):
                    dve.wait_ge(hi_done, n + 1)
                    hl = pieces[n][1]
                    nc.vector.scalar_tensor_tensor(hl[:, LO, :], raw[n][:, :], LIFT, hl[:, HI, :], ALU.mult, ALU.subtract)

                nc.vector.memset(rows[:, :, :], 0.0).then_inc(cleared, 1)
                for n in range(BATCHES + 1):
                    t, old = Turn(0, n), Turn(0, n - 1)
                    if t.within():
                        dve.wait_ge(x_loaded[n], 16)
                        for k in range(TT):
                            nc.vector.bn_stats(stats[t.slot][:, k, :], xt[n][:, k, :]).then_inc(stats_done, 1)
                        dve.wait_ge(stats_done, TT * (t.n + 1))
                        for k in range(TT):
                            nc.vector.bn_aggr(mv[t.slot][:, k, :], stats[t.slot][:, k, :]).then_inc(aggregated, 1)
                    if old.within():
                        dve.wait_ge(rstd_done, old.n + 1)
                        for k in range(TT):
                            nc.vector.tensor_scalar(xt[n - 1][:, k, :], xt[n - 1][:, k, :], mv[old.slot][:, k, 0:1],
                                                    rstd[old.slot][:, k:k + 1], ALU.subtract, ALU.mult).then_inc(applied, 1)
                dve.wait_ge(cleared, 1)
                nc.vector.memset(rows[:, :, KEY_WORDS + HD], 1.0)
                nc.vector.memset(halves[:, :, STACK], 1.0).then_inc(table_done, 1)
                dve.wait_ge(filled, 1)
                for part in range(2):
                    nc.vector.tensor_copy(halves[:, :, part * HD:(part + 1) * HD], ps_kv[:, :, 0:HD]).then_inc(table_done, 1)
                dve.wait_ge(table_done, 3)
                nc.vector.tensor_tensor(halves[:, :, 2 * HD:STACK], ps_kv[:, :, 0:HD], halves[:, :, 0:HD],
                                        ALU.subtract).then_inc(table_done, 1)
                nc.vector.tensor_copy(rows[:, :, KEY_WORDS:KEY_WORDS + HD], ps_kv[:, :, HD:2 * HD]).then_inc(table_done, 1)
                for dc in range(DC):
                    dve.wait_ge(rows_hi, dc + 1)
                    nc.vector.tensor_tensor(rows_hl[:, LO, dc, :], rows_t[:, dc, :], rows_hl[:, HI, dc, :], ALU.subtract).then_inc(rows_split, 1)
                dve.wait_ge(mean_loaded, 32)
                nc.vector.tensor_tensor(mean[0][:, :], mean[0][:, :], mean[1][:, :], ALU.add).then_inc(summed, 1)
                for n in range(POOL_FROM):
                    low_part(n)

                dve.wait_ge(hi_done, len(pieces) + 1)
                dve.wait_ge(summed, 1)
                nc.vector.scalar_tensor_tensor(shared_hl[:, 1, :], mean[0][:, :], LIFT / 2, shared_hl[:, 0, :],
                                               ALU.mult, ALU.subtract)

            @block.gpsimd
            def _(pool):
                for n in range(BATCHES):
                    t = Turn(0, n)
                    pool.wait_ge(aggregated, TT * (n + 1))
                    nc.gpsimd.tensor_tensor(var[t.slot][:, :], mv[t.slot][:, :, 1], c.eps[:, :], ALU.add).then_inc(var_done, 1)
                    pool.wait_ge(var_done, n + 1)
                    nc.gpsimd.tensor_tensor(rstd[t.slot][:, :], var[t.slot][:, :], c.minus_half[:, :],
                                            ALU.pow).then_inc(rstd_done, 1)
                for n in range(POOL_FROM, len(pieces)):
                    pool.wait_ge(hi_done, n + 1)
                    hl = pieces[n][1]
                    nc.gpsimd.tensor_tensor(hl[:, LO, :], raw[n][:, :], hl[:, HI, :], ALU.subtract)


def attention(nc, c, name, causal, hin, weights, out, ctx_hl=None, bias_v=None, gain=None, shift=None, memory=None):
    with ExitStack() as ctx:
        def sb(nm, shape, dt=F32):
            return ctx.enter_context(nc.sbuf_tensor(f"{name}_{nm}", shape, dt))

        def ps(nm, shape, dt=F32):
            return ctx.enter_context(nc.psum_tensor(f"{name}_{nm}", shape, dt))

        def sem(nm):
            return semaphore(nc, c, ctx, f"{name}_{nm}")

        def ring(make, nm, *args, n=2):
            return [make(f"{nm}{k}", *args) for k in range(n)]

        def dram(nm, shape, dt):
            return nc.dram_tensor(f"{name}_{nm}", shape, dt, kind="Internal").ap()

        mem = memory is not None
        cross = ctx_hl is not None and not mem
        normed_out = gain is not None
        kv_heads = 1 if mem else HEADS
        keys_of = [P, SEQ] if causal else [SEQ, SEQ]
        width = sum(keys_of)
        q_of = [(0, SEQ), (P if causal else 0, SEQ)]

        h_in = ring(sb, "h_in", [P, TT, D])
        h_hl = ring(sb, "h_hl", [P, 2, DC, SEQ], F16)
        src_hl = ring(sb, "src_hl", [P, 2, DC, SEQ], F16) if ctx_hl is not None else h_hl
        q_hl = ring(sb, "q_hl", [P, 2, DC, SEQ], F16)
        q_st = ring(sb, "q_st", [64, HEADS, SEQ], F16)
        k_st = ring(sb, "k_st", [64, kv_heads, SEQ], F16)
        v = ring(sb, "v", [P, TT, kv_heads, VW])
        if mem:
            best = sb("best", [P, TT, 8])
            best_at = sb("best_at", [P, TT, 8], U32)
            best_row = ring(sb, "best_row", [P, TT], I32)
            first_row = sb("first_row", [P, TT])
            rows = ring(sb, "rows", [P, TT, MEM_WORDS])
        else:
            k_hl = ring(sb, "k_hl", [P, 2, DC, SEQ], F16)
            bv = sb("bv", [P, D])
        if normed_out:
            g, be = sb("gain", [P, D]), sb("shift", [P, D])
            h_res = ring(sb, "h_res", [P, TT, D])
            total = sb("total", [P, TT, D])
            stats, mv = sb("stats", [P, TT, 6]), sb("mv", [P, TT, 2])
            var, rstd = sb("var", [P, TT]), sb("rstd", [P, TT])
            normed = sb("normed", [P, TT, D])
        neg_m = ring(sb, "neg_m", [P, TT, HEADS])
        m_row = [ring(sb, f"m_row{half}", [HALF, SEQ], F16) for half in range(2)]
        probs = ring(sb, "probs", [P, 2, width], n=4)
        o_t = ring(sb, "o_t", [P, GROUPS, SEQ])
        recip = sb("recip", [P, HEADS])
        att = ring(sb, "att", [P, TT, HEADS, HD])
        result = ring(sb, "result", [P, TT, D]) if normed_out else [x[:, :, :, :].rearrange("p t h e -> p t (h e)") for x in att]

        ps_s = ring(ps, "ps_s", [P, TT, SEQ])
        ps_t = ps("ps_t", [P, 2, BANK])
        ps_o = ring(ps, "ps_o", [P, BANK])
        ps_f = ps("ps_f", [P, 2, SEQ])
        ps_x = ps("ps_x", [P, HEADS, VW])

        q_dram = dram("q_dram", [BATCHES, 2, D, SEQ], F16)
        k_dram = None if mem else dram("k_dram", [BATCHES, 2, D, SEQ], F16)

        params_loaded, ones_set = sem("params_loaded"), sem("ones_set")
        h_in_loaded, src_loaded = ring(sem, "h_in_loaded"), ring(sem, "src_loaded")
        f_filled, f_emptied = sem("f_filled"), sem("f_emptied")
        x_filled, x_emptied = sem("x_filled"), sem("x_emptied")
        h_hi, hi_done, lo_done = sem("h_hi"), sem("hi_done"), sem("lo_done")
        q_stored, k_stored = ring(sem, "q_stored"), ring(sem, "k_stored")
        stack_loaded, m_loaded = ([ring(sem, f"{nm}{half}") for half in range(2)] for nm in ("stack_loaded", "m_loaded"))
        s_filled, s_emptied = sem("s_filled"), sem("s_emptied")
        m_row_done = ring(sem, "m_row_done")
        t_filled, t_emptied = sem("t_filled"), sem("t_emptied")
        v_done, pv_done, o_copied, keys_done = sem("v_done"), sem("pv_done"), sem("o_copied"), sem("keys_done")
        recip_done, divided = sem("recip_done"), sem("divided")
        h_res_loaded, h_res_free = ring(sem, "h_res_loaded"), sem("h_res_free")
        tail_step, var_done, rstd_done = sem("tail_step"), sem("var_done"), sem("rstd_done")
        normed_free, affine_done = sem("normed_free"), sem("affine_done")
        result_stored = ring(sem, "result_stored")
        best_step, row_done, rows_loaded = sem("best_step"), sem("row_done"), ring(sem, "rows_loaded")
        ordered, gathering, turning = sem("ordered"), sem("gathering"), sem("turning")
        KV = 1 if mem else 2
        STACK_DMAS, TAIL_STEPS, BEST_STEPS = 3 * KV, 6, 3
        params = (0 if mem else 1) + (2 if normed_out else 0)

        F_FILLS = (2, 2, 2) if mem else (2, 2, 2, 1)
        F_TURN, F_Q, F_K, F_V = range(4)
        F_BEST = F_K
        X_FILLS = (0, -1, 1, -1, 2) if mem else (0, -1, 1, -1)
        X_OUT, X_MAX, X_KEYS = (1, 3), (2, 0), 4

        def fills(kinds, t, k):
            n = 0
            for j, off in enumerate(kinds):
                m = t.n + off + (1 if j < k else 0)
                n += min(max(m, 0), BATCHES) if isinstance(m, int) else m
            return n

        with nc.Block() as block:
            @block.sync
            def _(sp):
                for dst, src in (() if mem else ((bv, bias_v),)) + (((g, gain), (be, shift)) if normed_out else ()):
                    sp.dma_start(dst[:, :], src.partition_broadcast(P)).then_inc(params_loaded, 16)

                def load_h(t):
                    if t.before(2):
                        sp.wait_ge(f_filled, fills(F_FILLS, t.plus(-4), F_TURN) + 1)
                    sp.dma_start(h_in[t.slot][:, :, :], hin[t.n]).then_inc(h_in_loaded[t.slot], 16)

                def load_src(t):
                    if t.before(2):
                        sp.wait_ge(f_filled, fills(F_FILLS, t.plus(-4 if mem else -3), F_BEST if mem else F_V) + 1)
                    sp.dma_start(src_hl[t.slot][:, :, :, :].rearrange("p l c s -> p (l c) s"),
                                 ctx_hl[:, :, bass.ds(t.n * SEQ, SEQ)].rearrange("l (c p) s -> p (l c) s", p=P)).then_inc(src_loaded[t.slot], 16)

                def store(t, hl, to, stored, k):
                    sp.wait_ge(lo_done, KV * t.n + k + 1)
                    sp.dma_start(to[t.n].rearrange("l (c p) s -> p (l c) s", p=P),
                                 hl[t.slot][:, :, :, :].rearrange("p l c s -> p (l c) s")).then_inc(stored[t.slot], 16)

                def load_stacks(t, half):
                    if t.before(2):
                        sp.wait_ge(t_filled, PAIRS * (t.n - 2) + PAIRS // 2 * (half + 1))
                    if not mem and isinstance(t.n, int) and t.n < 2:
                        sp.wait_ge(ones_set, t.n + 1 + 2)
                    for frm, stored, to, parts in ((q_dram, q_stored, q_st, (0, 1, 0)), (k_dram, k_stored, k_st, (0, 0, 1)))[:KV]:
                        sp.wait_ge(stored[t.slot], 16 * (t.turn + 1))
                        for row, part in enumerate(parts):
                            sp.dma_start(to[t.slot][row * HD:(row + 1) * HD, half * HALF:(half + 1) * HALF, :],
                                         frm[t.n, part].rearrange("(h e) s -> e h s", e=HD)[:, half * HALF:(half + 1) * HALF, :]
                                         ).then_inc(stack_loaded[half][t.slot], 16)

                def load_m(t, half):
                    sp.wait_ge(m_row_done[half], t.n + 1)
                    sp.dma_start(q_st[t.slot][STACK:ROWS, half * HALF:(half + 1) * HALF, :],
                                 m_row[half][t.slot][:, :]).then_inc(m_loaded[half][t.slot], 16)

                def step(t):
                    nxt, new, ahead, older = t.plus(1), t.plus(2), t.plus(3), t.plus(-2)
                    if cross and new.within():
                        load_src(new)
                    if nxt.within():
                        load_stacks(nxt, 1)
                    if t.within():
                        load_m(t, 1)
                    if mem and ahead.within():
                        load_src(ahead)
                    if ahead.within():
                        load_h(ahead)
                    if normed_out and t.within():
                        if t.before(2):
                            sp.wait_ge(h_res_free, t.n - 1)
                        sp.dma_start(h_res[t.slot][:, :, :], hin[t.n]).then_inc(h_res_loaded[t.slot], 16)
                    if new.within():
                        store(new, q_hl, q_dram, q_stored, 0)
                        if not mem:
                            store(new, k_hl, k_dram, k_stored, 1)
                    if nxt.within():
                        load_m(nxt, 0)
                    if new.within():
                        load_stacks(new, 0)
                    if older.within():
                        if normed_out:
                            sp.wait_ge(affine_done, 2 * (older.n + 1))
                        else:
                            sp.wait_ge(divided, TT * (older.n + 1))
                        sp.dma_start(out[older.n], result[older.slot][:, :, :] if normed_out else result[older.slot]).then_inc(result_stored[older.slot], 16)

                pipeline(sp, step, 3, 2)
                for k in range(2):
                    sp.wait_ge(result_stored[k], 16 * (BATCHES // 2))

            @block.tensor
            def _(pe):
                pe.sem_inc(pv_done, 2)
                if params:
                    pe.wait_ge(params_loaded, 16 * params)

                def turn_rows(t, new):
                    pe.wait_ge(f_emptied, fills(F_FILLS, t, F_TURN))
                    pe.wait_ge(h_in_loaded[new.slot], 16 * (new.turn + 1))
                    for k in range(TT):
                        for dc in range(DC):
                            mm = nc.tensor.transpose(ps_f[:, dc, k * P:(k + 1) * P],
                                                     h_in[new.slot][:, k, dc * P:(dc + 1) * P], c.ident[:, :])
                    mm.then_inc(f_filled, 1)

                def project(t, k, src, wt):
                    pe.wait_ge(f_emptied, fills(F_FILLS, t, k))
                    for fc in range(DC):
                        for dc in range(DC):
                            for m, r in PRODUCTS:
                                mm = nc.tensor.matmul(ps_f[:, fc, :], wt[:, m, dc, fc * P:(fc + 1) * P], src[:, r, dc, :],
                                                      start=(dc == 0 and m == r), stop=(dc == DC - 1 and m == LO))
                    mm.then_inc(f_filled, 1)

                def project_values(t, nxt):
                    pe.wait_ge(f_emptied, fills(F_FILLS, t, F_V))
                    for k in range(TT):
                        for dc in range(DC):
                            for r, m in PRODUCTS:
                                mm = nc.tensor.matmul(ps_f[:, k, :], src_hl[nxt.slot][:, r, dc, k * P:(k + 1) * P], weights[2][:, m, dc, :],
                                                      start=(dc == 0 and m == r), stop=(dc == DC - 1 and r == LO))
                    mm.then_inc(f_filled, 1)

                def score_rows(t, new):
                    pe.wait_ge(f_emptied, fills(F_FILLS, t, F_BEST))
                    pe.wait_ge(src_loaded[new.slot], 16 * (new.turn + 1))
                    for k in range(TT):
                        for dc in range(DC):
                            for q, r in PRODUCTS:
                                mm = nc.tensor.matmul(ps_f[:, k, :], q_hl[new.slot][:, q, dc, k * P:(k + 1) * P], src_hl[new.slot][:, r, dc, :],
                                                      start=(dc == 0 and q == r), stop=(dc == DC - 1 and q == LO))
                    mm.then_inc(f_filled, 1)

                def turn_keys(t, nxt):
                    pe.wait_ge(x_emptied, fills(X_FILLS, t, X_KEYS))
                    pe.wait_ge(rows_loaded[nxt.slot], 16 * TT * (nxt.turn + 1))
                    pe.sem_inc(turning, 1)
                    to = ps_x[0:64, 0:8, :].rearrange("p a b -> p (a b)").bitcast(F16)
                    for k in range(TT):
                        mm = nc.tensor.transpose(to[:, k * P:(k + 1) * P], rows[nxt.slot][:, k, 0:KEY_WORDS].bitcast(F16), c.ident_h[:, :])
                    mm.then_inc(x_filled, 1)

                def scores(nxt, h):
                    pe.wait_ge(s_emptied, HEADS * nxt.n + h + 1)
                    q, kk, to = q_st[nxt.slot], k_st[nxt.slot][:, h % kv_heads, :], ps_s[h % 2]
                    for k in range(TT):
                        mm = nc.tensor.matmul(to[:, k, 0:keys_of[k]], q[0:STACK, h, k * P:(k + 1) * P],
                                              kk[0:STACK, 0:keys_of[k]], start=True, stop=not causal)
                        if causal:
                            mm = nc.tensor.matmul(to[:, k, k * P:(k + 1) * P], c.ident_bf[:, :], c.mask_st[:, :],
                                                  start=False, stop=True)
                    mm.then_inc(s_filled, 1)

                def turn_maxima(t, of, half):
                    pe.wait_ge(x_emptied, fills(X_FILLS, t, X_MAX[half]))
                    pe.wait_ge(s_emptied, 2 + HEADS * of.n + HALF * (half + 1))
                    to = ps_x[0:HALF, 0:8, :].rearrange("p a b -> p (a b)")
                    for k in range(TT):
                        mm = nc.tensor.transpose(to[:, k * P:(k + 1) * P], neg_m[of.slot][:, k, half * HALF:(half + 1) * HALF], c.ident[:, :])
                    mm.then_inc(x_filled, 1)

                def shifted_scores(t, p):
                    if p % (PAIRS // 2) == 0:
                        pe.wait_ge(m_loaded[2 * p // PAIRS][t.slot], 16 * (t.turn + 1))
                    pe.wait_ge(t_emptied, PAIRS * t.n + p + 1)
                    for j in range(2):
                        h, at = 2 * p + j, 0
                        for k in range(TT):
                            a, b = q_of[k]
                            mm = nc.tensor.matmul(ps_t[:, j, at:at + b - a], k_st[t.slot][0:ROWS, h % kv_heads, k * P:(k + 1) * P],
                                                  q_st[t.slot][0:ROWS, h, a:b], start=True, stop=not causal)
                            if causal:
                                mm = nc.tensor.matmul(ps_t[:, j, at:at + P], c.ident_bf[:, :], c.mask_ts[:, :],
                                                      start=False, stop=True)
                            at += b - a
                    mm.then_inc(t_filled, 1)

                def values(t, gr):
                    pe.wait_ge(t_emptied, 1 + PAIRS * t.n + 2 * gr + 2)
                    if gr == 0:
                        pe.wait_ge(v_done, t.n + 1)
                    pe.wait_ge(o_copied, GROUPS * t.n + gr + 1)
                    at = 0
                    for k in range(TT):
                        a, b = q_of[k]
                        for j in range(GROUP):
                            h = GROUP * gr + j
                            vals = v[t.slot][:, k, h % kv_heads, :]
                            mm = nc.tensor.matmul(ps_o[gr % 2][j * VW:(j + 1) * VW, a:b], vals,
                                                  probs[h // 2 % 4][:, h % 2, at:at + b - a], start=(k == 0), stop=(k == TT - 1),
                                                  tile_position=(0, j * VW))
                        at += b - a
                    mm.then_inc(pv_done, 1)

                def turn_outputs(t, old, k):
                    pe.wait_ge(x_emptied, fills(X_FILLS, t, X_OUT[k]))
                    if k == 0:
                        pe.wait_ge(o_copied, 2 + GROUPS * (old.n + 1))
                    to = ps_x[:, :, :].rearrange("p (g h) e -> p g (h e)", g=GROUPS)
                    for gr in range(GROUPS):
                        mm = nc.tensor.transpose(to[:, gr, :], o_t[old.slot][:, gr, k * P:(k + 1) * P], c.ident[:, :])
                    mm.then_inc(x_filled, 1)

                def step(t):
                    nxt, new, old = t.plus(1), t.plus(2), t.plus(-1)
                    for p in range(PAIRS):
                        if t.within():
                            shifted_scores(t, p)
                        if nxt.within():
                            if p % (PAIRS // 2) == 0:
                                pe.wait_ge(stack_loaded[2 * p // PAIRS][nxt.slot], 16 * STACK_DMAS * (nxt.turn + 1))
                            if p == 0 and mem:
                                pe.wait_ge(keys_done, nxt.n + 1)
                            scores(nxt, 2 * p)
                        if p == 0 and old.within():
                            values(old, GROUPS - 1)
                        if p == 1 and t.within():
                            turn_maxima(t, t, 1)
                        if p in (2, 5) and old.within():
                            turn_outputs(t, old, p // 3)
                        if t.within() and p in (3, 5, 7):
                            values(t, (p - 3) // 2)
                        if p == 0 and new.within():
                            turn_rows(t, new)
                        if p == 1 and new.within():
                            project(t, F_Q, h_hl[new.slot], weights[0])
                        if p == 7 and new.within() and mem:
                            turn_keys(t, new)
                        if nxt.within():
                            scores(nxt, 2 * p + 1)
                        if p == 2 and new.within() and not mem:
                            if cross:
                                pe.wait_ge(src_loaded[new.slot], 16 * (new.turn + 1))
                            project(t, F_K, src_hl[new.slot], weights[1])
                        if p == 2 and new.within() and mem:
                            score_rows(t, new)
                        if p == 4 and nxt.within():
                            turn_maxima(t, nxt, 0)
                        if p == 5 and nxt.within() and not mem:
                            project_values(t, nxt)

                pipeline(pe, step, 2, 1)

            @block.scalar
            def _(act):
                act.sem_inc(t_emptied, 1)
                act.sem_inc(o_copied, 2)

                def copy_outputs(t, gr):
                    act.wait_ge(pv_done, 2 + GROUPS * t.n + gr + 1)
                    if gr == 0 and t.before(2):
                        act.wait_ge(x_filled, fills(X_FILLS, t.plus(-1), X_OUT[1]) + 1)
                    nc.scalar.copy(o_t[t.slot][:, gr, :], ps_o[gr % 2][:, 0:SEQ]).then_inc(o_copied, 1)

                def copy_maxima(t, of, half):
                    act.wait_ge(x_filled, fills(X_FILLS, t, X_MAX[half]) + 1)
                    if of.before(2):
                        act.wait_ge(m_loaded[half][of.slot], 16 * of.turn)
                    nc.scalar.copy(m_row[half][of.slot][:, :],
                                   ps_x[0:HALF, 0:8, :].rearrange("p a b -> p (a b)")).then_inc(x_emptied, 1)
                    act.wait_ge(x_emptied, fills(X_FILLS, t, X_MAX[half]) + 1)
                    act.sem_inc(m_row_done[half], 1)

                def step(t):
                    nxt, new, old = t.plus(1), t.plus(2), t.plus(-1)
                    for p in range(PAIRS):
                        if t.within():
                            act.wait_ge(t_filled, PAIRS * t.n + p + 1)
                            act.wait_ge(pv_done, GROUPS * t.n + p // 2 + 1)
                            nc.scalar.activation(probs[p % 4][:, :, :], ps_t[:, :, 0:width], ACT.Exp,
                                                 scale=SCALE).then_inc(t_emptied, 1)
                        if p == 0 and old.within():
                            copy_outputs(old, GROUPS - 1)
                        if p in (3, 5, 7) and t.within():
                            copy_outputs(t, (p - 3) // 2)
                        if p == 0 and new.within():
                            act.wait_ge(f_filled, fills(F_FILLS, t, F_TURN) + 1)
                            nc.scalar.copy(h_hl[new.slot][:, HI, :, :], ps_f[:, :, :]).then_inc(h_hi, 1)
                        if p in (1, 2)[:KV] and new.within():
                            hl, stored = (q_hl, q_stored) if p == 1 else (k_hl, k_stored)
                            act.wait_ge(f_filled, fills(F_FILLS, t, F_Q if p == 1 else F_K) + 1)
                            if new.before(2):
                                act.wait_ge(stored[new.slot], 16 * new.turn)
                            nc.scalar.activation(hl[new.slot][:, HI, :, :], ps_f[:, :, :], ACT.Copy, scale=1 / LIFT).then_inc(hi_done, 1)
                        if p == 1 and t.within():
                            copy_maxima(t, t, 1)
                        if p == 4 and nxt.within():
                            copy_maxima(t, nxt, 0)
                        if p == 7 and new.within() and mem:
                            act.wait_ge(x_filled, fills(X_FILLS, t, X_KEYS) + 1)
                            if new.before(2):
                                act.wait_ge(t_filled, PAIRS * (new.n - 1))
                            nc.scalar.copy(k_st[new.slot][:, 0, :],
                                           ps_x[0:64, 0:8, :].rearrange("p a b -> p (a b)").bitcast(F16)[:, 0:SEQ]).then_inc(x_emptied, 1)
                            act.wait_ge(x_emptied, fills(X_FILLS, t, X_KEYS) + 1)
                            act.sem_inc(keys_done, 1)

                pipeline(act, step, 2, 1)

            @block.vector
            def _(dve):
                dve.sem_inc(s_emptied, 2)
                if mem:
                    nc.vector.memset(first_row[:, :], 0.0).then_inc(row_done, 1)
                else:
                    for k in range(2):
                        nc.vector.memset(v[k][:, :, :, HD:VW], 0.0).then_inc(ones_set, 1)
                    dve.wait_ge(ones_set, 2)
                    for k in range(2):
                        nc.vector.memset(v[k][:, :, :, HD:HD + 1], 1.0)
                        nc.vector.memset(k_st[k][32:64, :, :], 1.0).then_inc(ones_set, 1)
                if params:
                    dve.wait_ge(params_loaded, 16 * params)

                def low_part(t, new, k, hl):
                    dve.wait_ge(hi_done, KV * new.n + k)
                    nc.vector.scalar_tensor_tensor(hl[new.slot][:, LO, :, :], ps_f[:, :, :], 1 / LIFT, hl[new.slot][:, HI, :, :],
                                                   ALU.mult, ALU.subtract).then_inc(f_emptied, 1)
                    dve.wait_ge(f_emptied, fills(F_FILLS, t, k) + 1)
                    dve.sem_inc(lo_done, 1)

                def rows_low(t, new):
                    dve.wait_ge(h_hi, new.n + 1)
                    nc.vector.tensor_tensor(h_hl[new.slot][:, LO, :, :], ps_f[:, :, :], h_hl[new.slot][:, HI, :, :],
                                            ALU.subtract).then_inc(f_emptied, 1)

                def copy_values(t, nxt):
                    dve.wait_ge(f_filled, fills(F_FILLS, t, F_V) + 1)
                    if nxt.before(1):
                        dve.wait_ge(pv_done, 2 + GROUPS * (nxt.n - 1))
                    for k in range(TT):
                        ins = nc.vector.scalar_tensor_tensor(
                            v[nxt.slot][:, k, :, 0:HD], ps_f[:, k, :].rearrange("p (h e) -> p h e", e=HD), 1 / LIFT,
                            bv[:, :].rearrange("p (h e) -> p h e", e=HD), ALU.mult, ALU.add)
                    ins.then_inc(f_emptied, 1)
                    dve.wait_ge(f_emptied, fills(F_FILLS, t, F_V) + 1)
                    dve.sem_inc(v_done, 1)

                def best_value(t, new):
                    dve.wait_ge(f_filled, fills(F_FILLS, t, F_BEST) + 1)
                    dve.sem_inc(ordered, 1)
                    for k in range(TT):
                        ins = nc.vector.max(best[:, k, :], ps_f[:, k, :])
                    ins.then_inc(best_step, 1)

                def best_place(t, new):
                    dve.wait_ge(best_step, BEST_STEPS * new.n + 1)
                    dve.sem_inc(ordered, 1)
                    for k in range(TT):
                        ins = nc.vector.max_index(best_at[:, k, :], best[:, k, :], ps_f[:, k, :])
                    ins.then_inc(f_emptied, 1)

                def table_row(t, new):
                    dve.wait_ge(f_emptied, fills(F_FILLS, t, F_BEST) + 1)
                    nc.vector.tensor_copy(best[:, :, 0], best_at[:, :, 0]).then_inc(best_step, 1)
                    dve.wait_ge(best_step, BEST_STEPS * new.n + 2)
                    dve.wait_ge(row_done, new.n + 1)
                    if new.before(2):
                        dve.wait_ge(rows_loaded[new.slot], 16 * TT * new.turn)
                    nc.vector.tensor_tensor(best_row[new.slot][:, :], best[:, :, 0], first_row[:, :], ALU.add).then_inc(best_step, 1)
                    dve.wait_ge(best_step, BEST_STEPS * new.n + 3)
                    nc.vector.tensor_scalar(first_row[:, :], first_row[:, :], float(SEQ), None, ALU.add).then_inc(row_done, 1)

                def maximum(nxt, h):
                    dve.wait_ge(s_filled, HEADS * nxt.n + h + 1)
                    if causal:
                        nc.vector.tensor_reduce(neg_m[nxt.slot][:, 0, h:h + 1], ps_s[h % 2][:, 0, 0:P], AX.X, ALU.max, negate=True)
                        nc.vector.tensor_reduce(neg_m[nxt.slot][:, 1, h:h + 1], ps_s[h % 2][:, 1, :], AX.X, ALU.max,
                                                negate=True).then_inc(s_emptied, 1)
                    else:
                        nc.vector.tensor_reduce(neg_m[nxt.slot][:, :, h:h + 1], ps_s[h % 2][:, :, :], AX.X, ALU.max,
                                                negate=True).then_inc(s_emptied, 1)

                def divide(t, old, k):
                    dve.wait_ge(x_filled, fills(X_FILLS, t, X_OUT[k]) + 1)
                    if k == 0 and not normed_out and old.before(2):
                        dve.wait_ge(result_stored[old.slot], 16 * old.turn)
                    nc.vector.reciprocal(recip[:, :], ps_x[:, :, HD]).then_inc(recip_done, 1)
                    dve.wait_ge(recip_done, TT * old.n + k + 1)
                    nc.vector.tensor_tensor(att[old.slot][:, k, :, :], ps_x[:, :, 0:HD],
                                            recip[:, :].unsqueeze(2).to_broadcast([P, HEADS, HD]),
                                            ALU.mult).then_inc(x_emptied, 1)
                    dve.wait_ge(x_emptied, fills(X_FILLS, t, X_OUT[k]) + 1)
                    dve.sem_inc(divided, 1)

                def sum_and_stats(t):
                    dve.wait_ge(h_res_loaded[t.slot], 16 * (t.turn + 1))
                    nc.vector.tensor_tensor(total[:, :, :], att[t.slot][:, :, :, :].rearrange("p t h e -> p t (h e)"),
                                            h_res[t.slot][:, :, :], ALU.add).then_inc(tail_step, 1)
                    dve.wait_ge(tail_step, TAIL_STEPS * t.n + 1)
                    for k in range(TT):
                        ins = nc.vector.bn_stats(stats[:, k, :], total[:, k, :])
                    ins.then_inc(tail_step, 1)
                    dve.wait_ge(tail_step, TAIL_STEPS * t.n + 2)
                    dve.sem_inc(h_res_free, 1)
                    for k in range(TT):
                        nc.vector.bn_aggr(mv[:, k, :], stats[:, k, :]).then_inc(tail_step, 1)

                def apply(t):
                    dve.wait_ge(rstd_done, t.n + 1)
                    if t.before(1):
                        dve.wait_ge(normed_free, t.n)
                    for k in range(TT):
                        nc.vector.tensor_scalar(normed[:, k, :], total[:, k, :], mv[:, k, 0:1], rstd[:, k:k + 1],
                                                ALU.subtract, ALU.mult).then_inc(tail_step, 1)

                def step(t):
                    nxt, new, old, older = t.plus(1), t.plus(2), t.plus(-1), t.plus(-2)
                    for p in range(PAIRS):
                        if p == 2 and new.within():
                            low_part(t, new, 1, q_hl)
                        if p in (3, 6) and old.within():
                            divide(t, old, p // 3 - 1)
                        if p == 4 and new.within() and mem:
                            table_row(t, new)
                        if p == 6 and nxt.within() and not mem:
                            copy_values(t, nxt)
                        if p == 7 and old.within() and normed_out:
                            sum_and_stats(old)
                        if p == 1 and older.within() and normed_out:
                            apply(older)
                        if nxt.within():
                            maximum(nxt, 2 * p)
                        if p == 0 and new.within():
                            rows_low(t, new)
                        if p == 3 and new.within() and not mem:
                            low_part(t, new, 2, k_hl)
                        if p == 3 and new.within() and mem:
                            best_value(t, new)
                        if nxt.within():
                            maximum(nxt, 2 * p + 1)
                        if p == 3 and new.within() and mem:
                            best_place(t, new)

                pipeline(dve, step, 2, 2)

            @block.gpsimd
            def _(pool):
                if params:
                    pool.wait_ge(params_loaded, 16 * params)

                def gather(t):
                    if t.before(2):
                        pool.wait_ge(v_done, t.n - 1)
                        pool.wait_ge(keys_done, t.n - 1)
                    pool.wait_ge(row_done, t.n + 2)
                    pool.sem_inc(gathering, 1)
                    for k in range(TT):
                        nc.gpsimd.indirect_dma_start(rows[t.slot][:, k, :], None, memory[:, :], bass.IndirectOffsetOnAxis(
                            ap=best_row[t.slot][:, k:k + 1], axis=0)).then_inc(rows_loaded[t.slot], 16)

                def take_values(t):
                    if t.before(2):
                        pool.wait_ge(pv_done, 2 + GROUPS * (t.n - 1))
                    pool.wait_ge(rows_loaded[t.slot], 16 * TT * (t.turn + 1))
                    pool.sem_inc(gathering, 1)
                    nc.gpsimd.tensor_copy(v[t.slot][:, :, 0, :], rows[t.slot][:, :, KEY_WORDS:MEM_WORDS]).then_inc(v_done, 1)

                def step(t):
                    nxt, new, t = t.plus(1), t.plus(2), t.plus(-1)
                    if mem and nxt.within():
                        take_values(nxt)
                    if mem and new.within():
                        gather(new)
                    if not t.within() or not normed_out:
                        return
                    pool.wait_ge(tail_step, TAIL_STEPS * t.n + 4)
                    nc.gpsimd.tensor_tensor(var[:, :], mv[:, :, 1], c.eps[:, :], ALU.add).then_inc(var_done, 1)
                    pool.wait_ge(var_done, t.n + 1)
                    nc.gpsimd.tensor_tensor(rstd[:, :], var[:, :], c.minus_half[:, :], ALU.pow).then_inc(rstd_done, 1)
                    pool.wait_ge(tail_step, TAIL_STEPS * (t.n + 1))
                    if t.before(2):
                        pool.wait_ge(result_stored[t.slot], 16 * t.turn)
                    nc.gpsimd.tensor_tensor(result[t.slot][:, :, :], normed[:, :, :],
                                            g[:, :].unsqueeze(1).to_broadcast([P, TT, D]), ALU.mult).then_inc(affine_done, 1)
                    pool.wait_ge(affine_done, 2 * t.n + 1)
                    pool.sem_inc(normed_free, 1)
                    nc.gpsimd.tensor_tensor(result[t.slot][:, :, :], result[t.slot][:, :, :],
                                            be[:, :].unsqueeze(1).to_broadcast([P, TT, D]), ALU.add).then_inc(affine_done, 1)

                pipeline(pool, step, 2, 1)


def feed_forward(nc, c, x2, x, w1_hl, b1, w2_hl, b2, gain, shift, gate, out, out_normed, logits, xs, zeroed):
    with ExitStack() as ctx:
        def sb(nm, shape, dt=F32):
            return ctx.enter_context(nc.sbuf_tensor(f"ff_{nm}", shape, dt))

        def ps(nm, shape, dt=F32):
            return ctx.enter_context(nc.psum_tensor(f"ff_{nm}", shape, dt))

        def sem(nm):
            return semaphore(nc, c, ctx, f"ff_{nm}")

        def ring(make, nm, *args, n=2):
            return [make(f"{nm}{k}", *args) for k in range(n)]

        FC = w1_hl.shape[3] // P
        E = gate.shape[1]
        b1_sb, b2_sb = sb("b1", [P, FC]), sb("b2", [P, D])
        g, be, gate_sb = sb("gain", [P, D]), sb("shift", [P, D]), sb("gate", [P, DC, E])
        x2_in = ring(sb, "x2_in", [P, TT, D])
        x2_hl = ring(sb, "x2_hl", [P, 2, DC, SEQ], F16)
        hidden = sb("hidden", [P, FC, SEQ])
        hidden_hl = ring(sb, "hidden_hl", [P, 2, FC, SEQ], F16)
        biased = ring(sb, "biased", [P, TT, D])
        total = ring(sb, "total", [P, TT, D])
        stats, mv = ring(sb, "stats", [P, TT, 6]), ring(sb, "mv", [P, TT, 2])
        stats_o, mv_o = ring(sb, "stats_o", [P, TT, 6]), ring(sb, "mv_o", [P, TT, 2])
        var, rstd = sb("var", [P, TT]), ring(sb, "rstd", [P, TT])
        var_o, rstd_o = sb("var_o", [P, TT]), ring(sb, "rstd_o", [P, TT])
        normed = ring(sb, "normed", [P, TT, D])
        x_in = ring(sb, "x_in", [P, TT, D])
        res = ring(sb, "res", [P, TT, D])
        res_n = ring(sb, "res_n", [P, TT, D])
        res_t = sb("res_t", [P, DC, SEQ])

        ps_x = ps("ps_x", [P, DC, SEQ])
        ps_h = ring(ps, "ps_h", [P, 2, SEQ])
        ps_o = ps("ps_o", [P, TT, D])
        ps_r = ps("ps_r", [P, DC, SEQ])
        ps_g = ps("ps_g", [P, BANK])
        ps_ge = ps_g[:, 0:TT * E].rearrange("p (t e) -> p t e", t=TT)

        params_loaded = sem("params_loaded")
        x2_loaded, x_loaded = ring(sem, "x2_loaded"), ring(sem, "x_loaded")
        x_turned, x_hi, x_split = sem("x_turned"), sem("x_hi"), sem("x_split")
        h_filled, h_done, h_split = sem("h_filled"), sem("h_done"), sem("h_split")
        o_filled, o_read, bias_added = sem("o_filled"), sem("o_read"), sem("bias_added")
        step1, step2 = sem("step1"), sem("step2")
        var_done, rstd_done, rstd_o_done = sem("var_done"), sem("rstd_done"), sem("rstd_o_done")
        normed_done, affine = sem("normed_done"), sem("affine")
        res_n_done = sem("res_n_done")
        r_turned, r_copied, g_filled, g_copied = sem("r_turned"), sem("r_copied"), sem("g_filled"), sem("g_copied")
        res_stored, res_n_stored = ring(sem, "res_stored"), ring(sem, "res_n_stored")
        AFFINE_STEPS, LN_STEPS = 3, 3
        x_rows = x.rearrange("(b t p) d -> b p t d", b=BATCHES, p=P)
        xs_share = xs.rearrange("(b p n) d -> b p n d", b=BATCHES, n=BATCHES)

        with nc.Block() as block:
            @block.sync
            def _(sp):
                sp.dma_start(gate_sb[:, :, :], gate.rearrange("(c p) f -> p c f", p=P)).then_inc(params_loaded, 16)
                sp.dma_start(b1_sb[:, :], b1).then_inc(params_loaded, 16)
                for dst, src in ((b2_sb, b2), (g, gain), (be, shift)):
                    sp.dma_start(dst[:, :], src.partition_broadcast(P)).then_inc(params_loaded, 16)

                def step(t):
                    new, old, older = t.plus(3), t.plus(-2), t.plus(-4)
                    if new.within():
                        if new.before(2):
                            sp.wait_ge(x_turned, new.n - 1)
                            sp.wait_ge(bias_added, new.n - 1)
                        sp.dma_start(x2_in[new.slot][:, :, :], x2[new.n]).then_inc(x2_loaded[new.slot], 16)
                    if t.within():
                        sp.dma_start(xs_share[t.n], c.zeros[0:xs_share.shape[1], :].unsqueeze(1).to_broadcast(
                            xs_share.shape[1:])).then_inc(zeroed, 16)
                        if t.before(2):
                            sp.wait_ge(affine, AFFINE_STEPS * (t.n - 1))
                        sp.dma_start(x_in[t.slot][:, :, :], x_rows[t.n]).then_inc(x_loaded[t.slot], 16)
                    if old.within():
                        sp.wait_ge(affine, AFFINE_STEPS * (old.n + 1))
                        sp.dma_start(out[old.n], res[old.slot][:, :, :]).then_inc(res_stored[old.slot], 16)
                    if older.within():
                        sp.wait_ge(res_n_done, TT * (older.n + 1))
                        sp.dma_start(out_normed[older.n], res_n[older.slot][:, :, :]).then_inc(res_n_stored[older.slot], 16)

                pipeline(sp, step, 3, 4)
                for k in range(2):
                    sp.wait_ge(res_stored[k], 16 * (BATCHES // 2))
                    sp.wait_ge(res_n_stored[k], 16 * (BATCHES // 2))

            @block.tensor
            def _(pe):
                pe.wait_ge(params_loaded, 16 * 5)

                def turn_rows(t):
                    pe.wait_ge(x2_loaded[t.slot], 16 * (t.turn + 1))
                    if t.before(1):
                        pe.wait_ge(x_split, t.n)
                    for k in range(TT):
                        for dc in range(DC):
                            mm = nc.tensor.transpose(ps_x[:, dc, k * P:(k + 1) * P], x2_in[t.slot][:, k, dc * P:(dc + 1) * P], c.ident[:, :])
                    mm.then_inc(x_turned, 1)

                def first_layer(t):
                    pe.wait_ge(x_split, t.n + 1)
                    for f in range(0, FC, 2):
                        if f >= 4 or t.before(1):
                            pe.wait_ge(h_done, FC * t.n + f - 2)
                        for j in range(2):
                            for dc in range(DC):
                                for w, x in PRODUCTS:
                                    mm = nc.tensor.matmul(ps_h[f // 2 % 2][:, j, :], w1_hl[:, w, dc, (f + j) * P:(f + j + 1) * P],
                                                          x2_hl[t.slot][:, x, dc, :], start=(dc == 0 and w == x), stop=(dc == DC - 1 and w == LO))
                        mm.then_inc(h_filled, 1)

                def second_layer(t):
                    pe.wait_ge(h_split, FC // 2 * (t.n + 1))
                    if t.before(1):
                        pe.wait_ge(o_read, t.n)
                    for k in range(TT):
                        for f in range(FC):
                            for h, w in PRODUCTS:
                                mm = nc.tensor.matmul(ps_o[:, k, :], hidden_hl[t.slot][:, h, f, k * P:(k + 1) * P], w2_hl[:, w, f, :],
                                                      start=(f == 0 and w == h), stop=(f == FC - 1 and h == LO))
                    mm.then_inc(o_filled, 1)

                def turn_result(t):
                    pe.wait_ge(res_n_done, TT * (t.n + 1))
                    if t.before(1):
                        pe.wait_ge(r_copied, t.n)
                    for k in range(TT):
                        for dc in range(DC):
                            mm = nc.tensor.transpose(ps_r[:, dc, k * P:(k + 1) * P], res_n[t.slot][:, k, dc * P:(dc + 1) * P], c.ident[:, :])
                    mm.then_inc(r_turned, 1)

                def gates(t):
                    pe.wait_ge(r_copied, t.n + 1)
                    if t.before(1):
                        pe.wait_ge(g_copied, t.n)
                    for k in range(TT):
                        for dc in range(DC):
                            mm = nc.tensor.matmul(ps_ge[:, k, :], res_t[:, dc, k * P:(k + 1) * P], gate_sb[:, dc, :],
                                                  start=(dc == 0), stop=(dc == DC - 1))
                    mm.then_inc(g_filled, 1)

                def step(t):
                    new, ahead, old = t.plus(1), t.plus(2), t.plus(-4)
                    if old.within():
                        turn_result(old)
                    if new.within():
                        first_layer(new)
                    if ahead.within():
                        turn_rows(ahead)
                    if old.within():
                        gates(old)
                    if t.within():
                        second_layer(t)

                pipeline(pe, step, 2, 4)

            @block.scalar
            def _(act):
                act.wait_ge(params_loaded, 16 * 5)

                def step(t):
                    new, ahead, old = t.plus(1), t.plus(2), t.plus(-4)
                    if old.within():
                        act.wait_ge(r_turned, old.n + 1)
                        if old.before(1):
                            act.wait_ge(g_filled, old.n)
                        nc.scalar.copy(res_t[:, :, :], ps_r[:, :, :]).then_inc(r_copied, 1)
                    if new.within():
                        for f in range(FC):
                            if f % 2 == 0:
                                act.wait_ge(h_filled, FC // 2 * new.n + f // 2 + 1)
                                if new.before(1):
                                    act.wait_ge(h_split, FC // 2 * (new.n - 1) + f // 2 + 1)
                            if f == 0 and new.before(2):
                                act.wait_ge(o_filled, new.n - 1)
                            for to in (hidden[:, f, :], hidden_hl[new.slot][:, HI, f, :]):
                                ins = nc.scalar.activation(to, ps_h[f // 2 % 2][:, f % 2, :], ACT.Relu, bias=b1_sb[:, f:f + 1], scale=1 / LIFT)
                            ins.then_inc(h_done, 1)
                    if ahead.within():
                        act.wait_ge(x_turned, ahead.n + 1)
                        if ahead.before(2):
                            act.wait_ge(h_filled, FC // 2 * (ahead.n - 1))
                        nc.scalar.copy(x2_hl[ahead.slot][:, HI, :, :], ps_x[:, :, :]).then_inc(x_hi, 1)

                pipeline(act, step, 2, 4)

            @block.vector
            def _(dve):
                def statistics(src, st, to, n, sm, base):
                    for k in range(TT):
                        ins = nc.vector.bn_stats(st[:, k, :], src[:, k, :])
                    ins.then_inc(sm, 1)
                    dve.wait_ge(sm, LN_STEPS * n + base + 1)
                    dve.sem_inc(sm, 1)
                    for k in range(TT):
                        ins = nc.vector.bn_aggr(to[:, k, :], st[:, k, :])
                    ins.then_inc(sm, 1)

                def step(t):
                    a, b, o, d, e = (t.plus(-k) for k in range(5))
                    new, ahead = t.plus(1), t.plus(2)
                    if b.within():
                        dve.wait_ge(rstd_done, b.n + 1)
                        if b.before(2):
                            dve.wait_ge(affine, AFFINE_STEPS * (b.n - 1))
                        for k in range(TT):
                            nc.vector.tensor_scalar(normed[b.slot][:, k, :], total[b.slot][:, k, :], mv[b.slot][:, k, 0:1],
                                                    rstd[b.slot][:, k:k + 1], ALU.subtract, ALU.mult).then_inc(normed_done, 1)
                    if o.within():
                        dve.wait_ge(affine, AFFINE_STEPS * (o.n + 1))
                        if o.before(2):
                            dve.wait_ge(res_n_done, TT * (o.n - 1))
                        statistics(res[o.slot], stats_o[o.slot], mv_o[o.slot], o.n, step2, 0)
                    if d.within():
                        dve.wait_ge(rstd_o_done, d.n + 1)
                        if d.before(2):
                            dve.wait_ge(res_n_stored[d.slot], 16 * d.turn)
                            dve.wait_ge(r_turned, d.n - 1)
                        for k in range(TT):
                            nc.vector.tensor_scalar(res_n[d.slot][:, k, :], res[d.slot][:, k, :], mv_o[d.slot][:, k, 0:1],
                                                    rstd_o[d.slot][:, k:k + 1], ALU.subtract, ALU.mult).then_inc(res_n_done, 1)
                    if new.within():
                        for f in range(FC // 2):
                            dve.wait_ge(h_done, FC * new.n + 2 * f + 2)
                            nc.vector.tensor_tensor(hidden_hl[new.slot][:, LO, 2 * f:2 * f + 2, :], hidden[:, 2 * f:2 * f + 2, :],
                                                    hidden_hl[new.slot][:, HI, 2 * f:2 * f + 2, :], ALU.subtract).then_inc(h_split, 1)
                    if ahead.within():
                        dve.wait_ge(x_hi, ahead.n + 1)
                        nc.vector.tensor_tensor(x2_hl[ahead.slot][:, LO, :, :], ps_x[:, :, :], x2_hl[ahead.slot][:, HI, :, :],
                                                ALU.subtract).then_inc(x_split, 1)
                    if e.within():
                        dve.wait_ge(g_filled, e.n + 1)
                        nc.vector.tensor_copy(logits[:, bass.ds(e.n * TT, TT), :], ps_ge).then_inc(g_copied, 1)
                    if a.within():
                        dve.wait_ge(o_filled, a.n + 1)
                        dve.wait_ge(bias_added, a.n + 1)
                        if a.before(2):
                            dve.wait_ge(normed_done, TT * (a.n - 1))
                        nc.vector.scalar_tensor_tensor(total[a.slot][:, :, :], ps_o[:, :, :], 1 / LIFT, biased[a.slot][:, :, :],
                                                       ALU.mult, ALU.add).then_inc(o_read, 1)
                        dve.wait_ge(o_read, a.n + 1)
                        statistics(total[a.slot], stats[a.slot], mv[a.slot], a.n, step1, 0)

                pipeline(dve, step, 2, 4)

            @block.gpsimd
            def _(pool):
                pool.wait_ge(params_loaded, 16 * 5)

                def root(m, v, r, t, k, done):
                    if t.before(1):
                        pool.wait_ge(done, t.n)
                    nc.gpsimd.tensor_tensor(v[:, :], m[:, :, 1], c.eps[:, :], ALU.add).then_inc(var_done, 1)
                    pool.wait_ge(var_done, k)
                    nc.gpsimd.tensor_tensor(r[:, :], v[:, :], c.minus_half[:, :], ALU.pow).then_inc(done, 1)

                def roots_before(t, k):
                    def some(m):
                        return min(max(m, 0), BATCHES) if isinstance(m, int) else m
                    return some(t.n) + some(t.n - 2 + k)

                def step(t):
                    new, old, older = t.plus(1), t.plus(-1), t.plus(-2)
                    if old.within():
                        pool.wait_ge(normed_done, TT * (old.n + 1))
                        if old.before(2):
                            pool.wait_ge(res_n_done, TT * (old.n - 1))
                            pool.wait_ge(res_stored[old.slot], 16 * old.turn)
                        to = res[old.slot][:, :, :]
                        nc.gpsimd.tensor_tensor(to, normed[old.slot][:, :, :], g[:, :].unsqueeze(1).to_broadcast([P, TT, D]),
                                                ALU.mult).then_inc(affine, 1)
                        pool.wait_ge(affine, AFFINE_STEPS * old.n + 1)
                        nc.gpsimd.tensor_tensor(to, to, be[:, :].unsqueeze(1).to_broadcast([P, TT, D]), ALU.add).then_inc(affine, 1)
                        pool.wait_ge(affine, AFFINE_STEPS * old.n + 2)
                        pool.wait_ge(x_loaded[old.slot], 16 * (old.turn + 1))
                        nc.gpsimd.tensor_tensor(to, to, x_in[old.slot][:, :, :], ALU.add).then_inc(affine, 1)
                    if older.within():
                        pool.wait_ge(step2, LN_STEPS * (older.n + 1))
                        root(mv_o[older.slot], var_o, rstd_o[older.slot], older,
                             roots_before(t, 0) + 1, rstd_o_done)
                    if new.within():
                        pool.wait_ge(x2_loaded[new.slot], 16 * (new.turn + 1))
                        if new.before(2):
                            pool.wait_ge(o_read, new.n - 1)
                        nc.gpsimd.tensor_tensor(biased[new.slot][:, :, :], x2_in[new.slot][:, :, :],
                                                b2_sb[:, :].unsqueeze(1).to_broadcast([P, TT, D]), ALU.add).then_inc(bias_added, 1)
                    if t.within():
                        pool.wait_ge(step1, LN_STEPS * (t.n + 1))
                        root(mv[t.slot], var, rstd[t.slot], t, roots_before(t, 1) + 1, rstd_done)

                pipeline(pool, step, 1, 2)


def route(nc, c, logits, normed, xs, weights, slots, tile_expert, zeroed):
    with ExitStack() as ctx:
        def sb(nm, shape, dt=F32):
            return ctx.enter_context(nc.sbuf_tensor(f"route_{nm}", shape, dt))

        def sem(nm):
            return semaphore(nc, c, ctx, f"route_{nm}")

        NT, E = logits.shape[1], logits.shape[2]
        tiles = tile_expert.shape[1]
        top, top_at = sb("top", [P, NT, E]), sb("top_at", [P, NT, E], U32)
        chosen_at = sb("chosen_at", [P, NT, 2])
        chosen = [sb(f"chosen{k}", [P, NT, E]) for k in range(2)]
        either = sb("either", [P, NT, E])
        triangle, ones = sb("triangle", [P, P]), sb("ones", [P, P])
        numbers, bounds, tile_numbers = sb("numbers", [P, E]), sb("bounds", [P, BATCHES]), sb("tile_numbers", [1, tiles])
        total, sums = sb("total", [P, NT, E]), [sb(f"sums{k}", [P, NT, E]) for k in range(2)]
        above, used = sb("above", [P, E, BATCHES]), sb("used", [P, E])
        ends = [sb(f"ends{k}", [P, E]) for k in range(2)]
        start = sb("start", [P, E])
        place, picked, slot = sb("place", [P, NT, E]), sb("picked", [P, NT, E]), sb("slot", [P, NT])
        ended, owner = sb("ended", [1, tiles, E]), sb("owner", [1, tiles])
        gap, exped, both = sb("gap", [P, NT]), sb("exped", [P, NT]), sb("both", [P, NT])
        rows = sb("rows", [P, NT, D])
        ps_p = ctx.enter_context(nc.psum_tensor("route_ps_p", [P, BANK], F32))
        ps_t = ctx.enter_context(nc.psum_tensor("route_ps_t", [P, BANK], F32))

        made, exps, chose, counted, stepped = sem("made"), sem("exps"), sem("chose"), sem("counted"), sem("stepped")
        gap_done, slots_done, rows_loaded, scattered = sem("gap_done"), sem("slots_done"), sem("rows_loaded"), sem("scattered")

        with nc.Block() as block:
            @block.sync
            def _(sp):
                for b in range(BATCHES):
                    sp.dma_start(rows[:, b * TT:(b + 1) * TT, :], normed[b]).then_inc(rows_loaded, 16)

            @block.tensor
            def _(pe):
                pe.wait_ge(made, 6)
                pe.wait_ge(chose, 1)
                a = either[:, :, :].rearrange("p t e -> p (t e)")
                nc.tensor.matmul(ps_p[:, 0:NT * E], triangle[:, :], a, start=True, stop=True).then_inc(counted, 1)
                nc.tensor.matmul(ps_t[:, 0:NT * E], ones[:, :], a, start=True, stop=True).then_inc(counted, 1)

            @block.scalar
            def _(act):
                act.wait_ge(gap_done, 1)
                nc.scalar.activation(exped[:, :], gap[:, :], ACT.Exp).then_inc(exps, 1)

            @block.vector
            def _(dve):
                step = iter(range(1, 100))
                for t in range(NT):
                    ins = nc.vector.max(top[:, t, :], logits[:, t, :])
                ins.then_inc(stepped, 1)
                dve.wait_ge(stepped, next(step))
                for t in range(NT):
                    ins = nc.vector.max_index(top_at[:, t, :], top[:, t, :], logits[:, t, :])
                ins.then_inc(stepped, 1)
                nc.vector.tensor_tensor(gap[:, :], top[:, :, 1], top[:, :, 0], ALU.subtract).then_inc(gap_done, 1)
                dve.wait_ge(stepped, next(step))
                nc.vector.tensor_copy(chosen_at[:, :, :], top_at[:, :, 0:2]).then_inc(stepped, 1)
                dve.wait_ge(stepped, next(step))
                dve.wait_ge(made, 6)
                for k in range(2):
                    ins = nc.vector.tensor_tensor(chosen[k][:, :, :], numbers[:, :].unsqueeze(1).to_broadcast([P, NT, E]),
                                                  chosen_at[:, :, k:k + 1].to_broadcast([P, NT, E]), ALU.is_equal)
                ins.then_inc(stepped, 1)
                dve.wait_ge(stepped, next(step))
                nc.vector.tensor_tensor(either[:, :, :], chosen[0][:, :, :], chosen[1][:, :, :], ALU.add).then_inc(chose, 1)

                dve.wait_ge(exps, 1)
                nc.vector.tensor_scalar(both[:, :], exped[:, :], 1.0, None, ALU.add).then_inc(stepped, 1)
                dve.wait_ge(stepped, next(step))
                nc.vector.reciprocal(weights[:, 0, :], both[:, :]).then_inc(stepped, 1)
                dve.wait_ge(stepped, next(step))
                nc.vector.tensor_tensor(weights[:, 1, :], exped[:, :], weights[:, 0, :], ALU.mult)

                dve.wait_ge(counted, 2)
                nc.vector.tensor_copy(total[:, :, :], ps_t[:, 0:NT * E].rearrange("p (t e) -> p t e", e=E)).then_inc(stepped, 1)
                dve.wait_ge(stepped, next(step))
                frm, shift = total, 1
                while shift < NT:
                    to = sums[shift.bit_length() % 2]
                    nc.vector.tensor_tensor(to[:, shift:, :], frm[:, shift:, :], frm[:, 0:NT - shift, :], ALU.add)
                    nc.vector.tensor_copy(to[:, 0:shift, :], frm[:, 0:shift, :]).then_inc(stepped, 1)
                    dve.wait_ge(stepped, next(step))
                    frm, shift = to, 2 * shift
                summed = frm

                nc.vector.tensor_tensor(above[:, :, :], summed[:, NT - 1, :].unsqueeze(2).to_broadcast([P, E, BATCHES]),
                                        bounds[:, :].unsqueeze(1).to_broadcast([P, E, BATCHES]), ALU.is_gt).then_inc(stepped, 1)
                dve.wait_ge(stepped, next(step))
                nc.vector.tensor_reduce(used[:, :], above[:, :, :], AX.X, ALU.add).then_inc(stepped, 1)
                dve.wait_ge(stepped, next(step))
                frm, shift = used, 1
                while shift < E:
                    to = ends[shift.bit_length() % 2]
                    nc.vector.tensor_tensor(to[:, shift:], frm[:, shift:], frm[:, 0:E - shift], ALU.add)
                    nc.vector.tensor_copy(to[:, 0:shift], frm[:, 0:shift]).then_inc(stepped, 1)
                    dve.wait_ge(stepped, next(step))
                    frm, shift = to, 2 * shift
                end = frm
                nc.vector.tensor_tensor(start[:, :], end[:, :], used[:, :], ALU.subtract).then_inc(stepped, 1)
                dve.wait_ge(stepped, next(step))
                nc.vector.tensor_scalar(start[:, :], start[:, :], float(SEQ), None, ALU.mult).then_inc(stepped, 1)

                nc.vector.tensor_tensor(place[:, :, :], summed[:, :, :], total[:, :, :], ALU.subtract).then_inc(stepped, 1)
                next(step)
                dve.wait_ge(stepped, next(step))
                nc.vector.tensor_tensor(place[:, :, :], place[:, :, :], ps_p[:, 0:NT * E].rearrange("p (t e) -> p t e", e=E),
                                        ALU.add).then_inc(stepped, 1)
                dve.wait_ge(stepped, next(step))
                nc.vector.tensor_tensor(place[:, :, :], place[:, :, :], start[:, :].unsqueeze(1).to_broadcast([P, NT, E]),
                                        ALU.add).then_inc(stepped, 1)
                dve.wait_ge(stepped, next(step))
                for k in range(2):
                    nc.vector.tensor_tensor(picked[:, :, :], place[:, :, :], chosen[k][:, :, :], ALU.mult).then_inc(stepped, 1)
                    dve.wait_ge(stepped, next(step))
                    nc.vector.tensor_reduce(slot[:, :], picked[:, :, :], AX.X, ALU.add).then_inc(stepped, 1)
                    dve.wait_ge(stepped, next(step))
                    nc.vector.tensor_copy(slots[:, k, :], slot[:, :]).then_inc(slots_done, 1)
                    dve.wait_ge(slots_done, k + 1)

                nc.vector.tensor_tensor(ended[:, :, :], end[0:1, :].unsqueeze(1).to_broadcast([1, tiles, E]),
                                        tile_numbers[:, :].unsqueeze(2).to_broadcast([1, tiles, E]), ALU.is_le).then_inc(stepped, 1)
                dve.wait_ge(stepped, next(step))
                nc.vector.tensor_reduce(owner[:, :], ended[:, :, :], AX.X, ALU.add).then_inc(stepped, 1)
                dve.wait_ge(stepped, next(step))
                nc.vector.tensor_scalar(tile_expert[:, :], owner[:, :], float(E - 1), None, ALU.min)

            @block.gpsimd
            def _(pool):
                nc.gpsimd.memset(triangle[:, :], 1.0).then_inc(made, 1)
                nc.gpsimd.memset(ones[:, :], 1.0).then_inc(made, 1)
                nc.gpsimd.iota(numbers[:, :], [[1, E]], 0, 0, allow_small_or_imprecise_dtypes=True).then_inc(made, 1)
                nc.gpsimd.iota(bounds[:, :], [[SEQ, BATCHES]], 0, 0, allow_small_or_imprecise_dtypes=True).then_inc(made, 1)
                nc.gpsimd.iota(tile_numbers[:, :], [[1, tiles]], 0, 0, allow_small_or_imprecise_dtypes=True).then_inc(made, 1)
                pool.wait_ge(made, 5)
                nc.gpsimd.affine_select(out=triangle[:, :], in_=triangle[:, :], compare_op=ALU.is_gt, fill=0.0, base=0,
                                        pattern=[[1, P]], channel_multiplier=-1).then_inc(made, 1)
                pool.wait_ge(rows_loaded, 16 * BATCHES)
                pool.wait_ge(zeroed, 16 * BATCHES)
                for k in range(2):
                    pool.wait_ge(slots_done, k + 1)
                    for t in range(NT):
                        nc.gpsimd.indirect_dma_start(xs[:, :], bass.IndirectOffsetOnAxis(ap=slots[:, k, t:t + 1], axis=0),
                                                     rows[:, t, :], None).then_inc(scattered, 16)
                pool.wait_ge(scattered, 16 * 2 * NT)


def experts(nc, c, xs, w13, w2, tile_expert, ys):
    with ExitStack() as ctx:
        def sb(nm, shape, dt=F32):
            return ctx.enter_context(nc.sbuf_tensor(f"moe_{nm}", shape, dt))

        def ps(nm, shape, dt=F32):
            return ctx.enter_context(nc.psum_tensor(f"moe_{nm}", shape, dt))

        def sem(nm):
            return semaphore(nc, c, ctx, f"moe_{nm}")

        def ring(make, nm, *args, n=2):
            return [make(f"{nm}{k}", *args) for k in range(n)]

        tiles = tile_expert.shape[1]
        E, HC = w2.shape[0], w2.shape[2]
        x_in, x_hl = ring(sb, "x_in", [P, TT, D]), ring(sb, "x_hl", [P, 2, DC, SEQ], F16)
        up_in, down_in = ring(sb, "up_in", [P, 2, DC, HC * P]), ring(sb, "down_in", [P, HC, D])
        up_hl, down_hl = ring(sb, "up_hl", [P, 2, 2, DC, HC * P], F16), ring(sb, "down_hl", [P, 2, HC, D], F16)
        mid, mid_hl = sb("mid", [P, HC, SEQ]), ring(sb, "mid_hl", [P, 2, HC, SEQ], F16)
        y = ring(sb, "y", [P, TT, D])
        ps_x = ps("ps_x", [P, DC, SEQ])
        ps_u = ring(ps, "ps_u", [P, 2, SEQ])
        ps_y = ring(ps, "ps_y", [P, TT, D])
        x_loaded, up_loaded, down_loaded = ring(sem, "x_loaded"), ring(sem, "up_loaded"), ring(sem, "down_loaded")
        up_hi, up_split, down_hi, down_split = sem("up_hi"), sem("up_split"), sem("down_hi"), sem("down_split")
        turned, x_hi, x_split = sem("turned"), sem("x_hi"), sem("x_split")
        u_filled, silu_done, mid_done, mid_hi, mid_split = sem("u_filled"), sem("silu_done"), sem("mid_done"), sem("mid_hi"), sem("mid_split")
        y_filled, y_copied, y_stored, ordered = sem("y_filled"), sem("y_copied"), ring(sem, "y_stored"), sem("ordered")
        xs_t = xs.rearrange("(n t p) d -> n p t d", n=tiles, p=P)
        ys_t = ys.rearrange("(n t p) d -> n p t d", n=tiles, p=P)

        with nc.Block() as block:
            @block.sync
            def _(sp):
                def step(t):
                    new, ahead, old = t.plus(2), t.plus(3), t.plus(-1)
                    if new.within():
                        e = sp.value_load(tile_expert[0:1, bass.ds(new.n, 1)], min_val=0, max_val=E - 1)
                        if new.before(2):
                            sp.wait_ge(down_split, HC * (new.n - 1))
                        sp.dma_start(down_in[new.slot][:, :, :], w2[e]).then_inc(down_loaded[new.slot], 16)
                    if ahead.within():
                        e = sp.value_load(tile_expert[0:1, bass.ds(ahead.n, 1)], min_val=0, max_val=E - 1)
                        if ahead.before(2):
                            sp.wait_ge(turned, ahead.n - 1)
                        sp.dma_start(x_in[ahead.slot][:, :, :], xs_t[ahead.n]).then_inc(x_loaded[ahead.slot], 16)
                        if ahead.before(2):
                            sp.wait_ge(up_split, HC * (ahead.n - 1))
                        sp.dma_start(up_in[ahead.slot][:, :, :, :].rearrange("p m c h -> p (m c h)"), w13[e]).then_inc(up_loaded[ahead.slot], 16)
                    if old.within():
                        sp.wait_ge(y_copied, old.n + 1)
                        sp.dma_start(ys_t[old.n], y[old.slot][:, :, :]).then_inc(y_stored[old.slot], 16)

                pipeline(sp, step, 3, 1, tiles)
                for k in range(2):
                    sp.wait_ge(y_stored[k], 16 * ((tiles - k + 1) // 2))

            @block.tensor
            def _(pe):
                def turn_rows(t):
                    pe.wait_ge(x_loaded[t.slot], 16 * (t.turn + 1))
                    if t.before(1):
                        pe.wait_ge(x_split, t.n)
                    for k in range(TT):
                        for dc in range(DC):
                            mm = nc.tensor.transpose(ps_x[:, dc, k * P:(k + 1) * P], x_in[t.slot][:, k, dc * P:(dc + 1) * P], c.ident[:, :])
                    mm.then_inc(turned, 1)

                def go_up(t):
                    pe.wait_ge(up_split, HC * (t.n + 1))
                    pe.wait_ge(x_split, t.n + 1)
                    for f in range(HC):
                        if f >= 2 or t.before(1):
                            pe.wait_ge(mid_done, HC * t.n + f - 1)
                        bank = ps_u[(HC * t.slot + f) % 2]
                        for m in range(2):
                            for dc in range(DC):
                                for w, x in PRODUCTS:
                                    mm = nc.tensor.matmul(bank[:, m, :], up_hl[t.slot][:, w, m, dc, f * P:(f + 1) * P], x_hl[t.slot][:, x, dc, :],
                                                          start=(dc == 0 and w == x), stop=(dc == DC - 1 and w == LO))
                        mm.then_inc(u_filled, 1)

                def go_down(t):
                    pe.wait_ge(down_split, HC * (t.n + 1))
                    pe.wait_ge(mid_split, HC * (t.n + 1))
                    if t.before(2):
                        pe.wait_ge(y_copied, t.n - 1)
                    for k in range(TT):
                        for f in range(HC):
                            for m, w in PRODUCTS:
                                mm = nc.tensor.matmul(ps_y[t.slot][:, k, :], mid_hl[t.slot][:, m, f, k * P:(k + 1) * P], down_hl[t.slot][:, w, f, :],
                                                      start=(f == 0 and w == m), stop=(f == HC - 1 and m == LO))
                    mm.then_inc(y_filled, 1)

                def step(t):
                    nxt, new = t.plus(1), t.plus(2)
                    if nxt.within():
                        go_up(nxt)
                    if new.within():
                        turn_rows(new)
                    if t.within():
                        go_down(t)

                pipeline(pe, step, 2, 0, tiles)

            @block.scalar
            def _(act):
                def step(t):
                    nxt, new = t.plus(1), t.plus(2)
                    if nxt.within():
                        act.wait_ge(down_loaded[nxt.slot], 16 * (nxt.turn + 1))
                        if nxt.before(2):
                            act.wait_ge(y_filled, nxt.n - 1)
                    if new.within():
                        act.wait_ge(up_loaded[new.slot], 16 * (new.turn + 1))
                        if new.before(2):
                            act.wait_ge(u_filled, HC * (new.n - 1))
                    for f in range(HC):
                        if nxt.within():
                            act.wait_ge(u_filled, HC * nxt.n + f + 1)
                            if nxt.before(1):
                                act.wait_ge(mid_split, HC * (nxt.n - 1) + f + 1)
                            nc.scalar.activation(mid[:, f, :], ps_u[(HC * nxt.slot + f) % 2][:, 0, :], ACT.Silu,
                                                 scale=1 / LIFT).then_inc(silu_done, 1)
                            nc.scalar.activation(down_hl[nxt.slot][:, HI, f, :], down_in[nxt.slot][:, f, :], ACT.Copy,
                                                 scale=LIFT).then_inc(down_hi, 1)
                        if new.within():
                            nc.scalar.activation(up_hl[new.slot][:, HI, :, :, f * P:(f + 1) * P].rearrange("p m c h -> p (m c) h"),
                                                 up_in[new.slot][:, :, :, f * P:(f + 1) * P].rearrange("p m c h -> p (m c) h"), ACT.Copy,
                                                 scale=LIFT).then_inc(up_hi, 1)
                    if new.within():
                        act.wait_ge(turned, new.n + 1)
                        nc.scalar.copy(x_hl[new.slot][:, HI, :, :], ps_x[:, :, :]).then_inc(x_hi, 1)
                    if t.within():
                        act.wait_ge(y_filled, t.n + 1)
                        if t.before(2):
                            act.wait_ge(y_stored[t.slot], 16 * t.turn)
                        nc.scalar.activation(y[t.slot][:, :, :], ps_y[t.slot][:, :, :], ACT.Copy, scale=1 / LIFT).then_inc(y_copied, 1)

                pipeline(act, step, 2, 0, tiles)

            @block.vector
            def _(dve):
                def up_low(t, f):
                    dve.wait_ge(up_hi, HC * t.n + f + 1)
                    at = slice(f * P, (f + 1) * P)
                    nc.vector.scalar_tensor_tensor(up_hl[t.slot][:, LO, :, :, at].rearrange("p m c h -> p (m c) h"),
                                                   up_in[t.slot][:, :, :, at].rearrange("p m c h -> p (m c) h"), LIFT,
                                                   up_hl[t.slot][:, HI, :, :, at].rearrange("p m c h -> p (m c) h"),
                                                   ALU.mult, ALU.subtract).then_inc(up_split, 1)

                def mid_low(t, f):
                    dve.wait_ge(mid_hi, HC * t.n + f + 1)
                    nc.vector.tensor_tensor(mid_hl[t.slot][:, LO, f, :], mid[:, f, :], mid_hl[t.slot][:, HI, f, :],
                                            ALU.subtract).then_inc(mid_split, 1)

                def step(t):
                    nxt, new = t.plus(1), t.plus(2)
                    for f in range(HC):
                        if nxt.within():
                            dve.wait_ge(silu_done, HC * nxt.n + f + 1)
                            nc.vector.scalar_tensor_tensor(mid[:, f, :], ps_u[(HC * nxt.slot + f) % 2][:, 1, :], 1 / LIFT, mid[:, f, :],
                                                           ALU.mult, ALU.mult).then_inc(mid_done, 1)
                            dve.wait_ge(down_hi, HC * nxt.n + f + 1)
                            nc.vector.scalar_tensor_tensor(down_hl[nxt.slot][:, LO, f, :], down_in[nxt.slot][:, f, :], LIFT,
                                                           down_hl[nxt.slot][:, HI, f, :], ALU.mult, ALU.subtract).then_inc(down_split, 1)
                        if nxt.within() and f > 0:
                            mid_low(nxt, f - 1)
                        if new.within() and f % 2 == 1:
                            up_low(new, f)
                    if nxt.within():
                        mid_low(nxt, HC - 1)
                    if new.within():
                        dve.wait_ge(x_hi, new.n + 1)
                        nc.vector.tensor_tensor(x_hl[new.slot][:, LO, :, :], ps_x[:, :, :], x_hl[new.slot][:, HI, :, :],
                                                ALU.subtract).then_inc(x_split, 1)
                    for f in range(0, HC, 2):
                        if new.within():
                            up_low(new, f)

                pipeline(dve, step, 2, 0, tiles)

            @block.gpsimd
            def _(pool):
                def step(t):
                    for f in range(HC):
                        if f == 0 and t.before(2):
                            pool.wait_ge(y_filled, t.n - 1)
                        pool.wait_ge(mid_done, HC * t.n + f + 1)
                        pool.sem_inc(ordered, 1)
                        nc.gpsimd.tensor_copy(mid_hl[t.slot][:, HI, f, :], mid[:, f, :]).then_inc(mid_hi, 1)

                pipeline(pool, step, 0, 0, tiles)


def combine(nc, c, x, ys, weights, slots, out, out_normed):
    with ExitStack() as ctx:
        def sb(nm, shape, dt=F32):
            return ctx.enter_context(nc.sbuf_tensor(f"comb_{nm}", shape, dt))

        def sem(nm):
            return semaphore(nc, c, ctx, f"comb_{nm}")

        def ring(make, nm, *args, n=2):
            return [make(f"{nm}{k}", *args) for k in range(n)]

        x_in, res, res_n = ring(sb, "x_in", [P, TT, D]), ring(sb, "res", [P, TT, D]), ring(sb, "res_n", [P, TT, D])
        y = ring(sb, "y", [P, 2, TT, D])
        part = sb("part", [P, TT, D])
        index, share = ring(sb, "index", [P, 2, TT], I32), ring(sb, "share", [P, 2, TT])
        stats, mv = ring(sb, "stats", [P, TT, 6]), ring(sb, "mv", [P, TT, 2])
        var, rstd = sb("var", [P, TT]), ring(sb, "rstd", [P, TT])
        x_loaded, y_loaded = ring(sem, "x_loaded"), ring(sem, "y_loaded")
        indexed, parted, summed, stepped = sem("indexed"), sem("parted"), sem("summed"), sem("stepped")
        var_done, rstd_done, normed_done = sem("var_done"), sem("rstd_done"), sem("normed_done")
        res_stored, res_n_stored = ring(sem, "res_stored"), ring(sem, "res_n_stored")
        ordered, aggregating = sem("ordered"), sem("aggregating")

        with nc.Block() as block:
            @block.sync
            def _(sp):
                def step(t):
                    new, old = t.plus(1), t.plus(-1)
                    if new.within():
                        if new.before(2):
                            sp.wait_ge(parted, TT * (new.n - 1))
                        sp.dma_start(x_in[new.slot][:, :, :], x[new.n]).then_inc(x_loaded[new.slot], 16)
                    if t.within():
                        sp.wait_ge(summed, TT * (t.n + 1))
                        sp.dma_start(out[t.n], res[t.slot][:, :, :]).then_inc(res_stored[t.slot], 16)
                    if old.within():
                        sp.wait_ge(normed_done, TT * (old.n + 1))
                        sp.dma_start(out_normed[old.n], res_n[old.slot][:, :, :]).then_inc(res_n_stored[old.slot], 16)

                pipeline(sp, step, 1, 1)
                for k in range(2):
                    sp.wait_ge(res_stored[k], 16 * (BATCHES // 2))
                    sp.wait_ge(res_n_stored[k], 16 * (BATCHES // 2))

            @block.gpsimd
            def _(pool):
                def step(t):
                    new = t.plus(1)
                    if new.within():
                        if new.before(2):
                            pool.wait_ge(summed, TT * (new.n - 1))
                        pool.wait_ge(indexed, new.n + 1)
                        pool.sem_inc(ordered, 1)
                        for k in range(2):
                            for j in range(TT):
                                nc.gpsimd.indirect_dma_start(y[new.slot][:, k, j, :], None, ys[:, :], bass.IndirectOffsetOnAxis(
                                    ap=index[new.slot][:, k, j:j + 1], axis=0)).then_inc(y_loaded[new.slot], 16)
                    if t.within():
                        pool.wait_ge(stepped, 2 * (t.n + 1))
                        if t.before(1):
                            pool.wait_ge(rstd_done, t.n)
                        nc.gpsimd.tensor_tensor(var[:, :], mv[t.slot][:, :, 1], c.eps[:, :], ALU.add).then_inc(var_done, 1)
                        pool.wait_ge(var_done, t.n + 1)
                        nc.gpsimd.tensor_tensor(rstd[t.slot][:, :], var[:, :], c.minus_half[:, :], ALU.pow).then_inc(rstd_done, 1)

                pipeline(pool, step, 1, 0)

            @block.vector
            def _(dve):
                def step(t):
                    new, old = t.plus(1), t.plus(-1)
                    if new.within():
                        if new.before(2):
                            dve.wait_ge(summed, TT * (new.n - 1))
                            dve.wait_ge(y_loaded[new.slot], 16 * 2 * TT * new.turn)
                        nc.vector.tensor_copy(index[new.slot][:, :, :], slots[:, :, bass.ds(new.n * TT, TT)])
                        nc.vector.tensor_copy(share[new.slot][:, :, :], weights[:, :, bass.ds(new.n * TT, TT)]).then_inc(indexed, 1)
                    if t.within():
                        dve.wait_ge(indexed, t.n + 1)
                        dve.wait_ge(x_loaded[t.slot], 16 * (t.turn + 1))
                        dve.wait_ge(y_loaded[t.slot], 16 * 2 * TT * (t.turn + 1))
                        if t.before(1):
                            dve.wait_ge(summed, TT * t.n)
                        for j in range(TT):
                            nc.vector.scalar_tensor_tensor(part[:, j, :], y[t.slot][:, 0, j, :], share[t.slot][:, 0, j:j + 1],
                                                           x_in[t.slot][:, j, :], ALU.mult, ALU.add).then_inc(parted, 1)
                        dve.wait_ge(parted, TT * (t.n + 1))
                        if t.before(2):
                            dve.wait_ge(res_stored[t.slot], 16 * t.turn)
                            dve.wait_ge(normed_done, TT * (t.n - 1))
                        for j in range(TT):
                            nc.vector.scalar_tensor_tensor(res[t.slot][:, j, :], y[t.slot][:, 1, j, :], share[t.slot][:, 1, j:j + 1],
                                                           part[:, j, :], ALU.mult, ALU.add).then_inc(summed, 1)
                        dve.wait_ge(summed, TT * (t.n + 1))
                        for j in range(TT):
                            ins = nc.vector.bn_stats(stats[t.slot][:, j, :], res[t.slot][:, j, :])
                        ins.then_inc(stepped, 1)
                        dve.wait_ge(stepped, 2 * t.n + 1)
                        dve.sem_inc(aggregating, 1)
                        for j in range(TT):
                            ins = nc.vector.bn_aggr(mv[t.slot][:, j, :], stats[t.slot][:, j, :])
                        ins.then_inc(stepped, 1)
                    if old.within():
                        dve.wait_ge(rstd_done, old.n + 1)
                        if old.before(2):
                            dve.wait_ge(res_n_stored[old.slot], 16 * old.turn)
                        for j in range(TT):
                            nc.vector.tensor_scalar(res_n[old.slot][:, j, :], res[old.slot][:, j, :], mv[old.slot][:, j, 0:1],
                                                    rstd[old.slot][:, j:j + 1], ALU.subtract, ALU.mult).then_inc(normed_done, 1)

                pipeline(dve, step, 1, 1)


def mixture(nc, c, att, wc_hl, xb, cent_hl, biases, wr_hl, br, ws_hl, bs, out):
    with ExitStack() as ctx:
        def sb(nm, shape, dt=F32):
            return ctx.enter_context(nc.sbuf_tensor(f"mix_{nm}", shape, dt))

        def ps(nm, shape, dt=F32):
            return ctx.enter_context(nc.psum_tensor(f"mix_{nm}", shape, dt))

        def sem(nm):
            return semaphore(nc, c, ctx, f"mix_{nm}")

        def ring(make, nm, *args, n=2):
            return [make(f"{nm}{k}", *args) for k in range(n)]

        E = wr_hl.shape[3]
        SHARED = bs.shape[0]
        G = E + 1
        QUADS = E // 2
        FILLS = QUADS * TT
        ADDS = 2 * FILLS
        RING = 4
        b_sb, bs_sb = sb("b", [G, D]), [sb(f"bs{k}", [1, D]) for k in range(SHARED)]
        eb_sb, numbers = sb("biases", [P, E]), sb("numbers", [P, E])
        att_in, xb_in = ring(sb, "att_in", [P, TT, D]), ring(sb, "xb_in", [P, TT, D])
        att_hl, u_hl = (ring(sb, nm, [P, 2, DC, SEQ], F16) for nm in ("att_hl", "u_hl"))
        xc, u, base = ring(sb, "xc", [P, TT, D]), ring(sb, "u", [P, TT, D]), ring(sb, "base", [P, TT, D])
        stats, mv = sb("stats", [P, TT, 6]), sb("mv", [P, TT, 2])
        var, rstd = sb("var", [P, TT]), sb("rstd", [P, TT])
        score, top, top_at = sb("score", [P, TT, E]), sb("top", [P, TT, 8]), sb("top_at", [P, TT, 8], U32)
        chosen_at, neg_top = sb("chosen_at", [P, TT, 2]), sb("neg_top", [P, TT])
        chosen = [sb(f"chosen{k}", [P, TT, E]) for k in range(2)]
        exps, exp_sum, recip = sb("exps", [P, TT, E]), sb("exp_sum", [P, TT]), sb("recip", [P, TT])
        probs = ring(sb, "probs", [P, TT, G])
        shares = ring(sb, "shares", [P, TT, E])
        probs_t = ring(sb, "probs_t", [G, SEQ])
        acc = ring(sb, "acc", [P, TT, D])

        ps_t, ps_c = ps("ps_t", [P, DC, SEQ]), ps("ps_c", [P, TT, D])
        ps_s, ps_b = ps("ps_s", [P, BANK]), ps("ps_b", [P, TT, D])
        ps_e = ring(ps, "ps_e", [P, 2, D], n=RING)
        ps_scores = ps_s[:, 0:TT * E].rearrange("p (t e) -> p t e", t=TT)
        ps_probs = ps_s[0:G, 0:SEQ]

        params_loaded, set_up = sem("params_loaded"), sem("set_up")
        att_loaded, xb_loaded = ring(sem, "att_loaded"), ring(sem, "xb_loaded")
        t_hi, t_filled, t_emptied, c_filled, xc_done = sem("t_hi"), sem("t_filled"), sem("t_emptied"), sem("c_filled"), sem("xc_done")
        s_filled, s_emptied, b_filled, b_emptied = sem("s_filled"), sem("s_emptied"), sem("b_filled"), sem("b_emptied")
        stepped, var_done, rstd_done, u_done = sem("stepped"), sem("var_done"), sem("rstd_done"), sem("u_done")
        based, exps_done, probs_done = sem("based"), sem("exps_done"), sem("probs_done")
        e_filled, added, ordered, shared_out = sem("e_filled"), sem("added"), sem("ordered"), sem("shared_out")
        out_stored = ring(sem, "out_stored")
        PARAMS = 3 + SHARED
        STEPS = 10
        XC_AT, U_AT, CHOOSE_AT = 1, 3, 5

        with nc.Block() as block:
            @block.sync
            def _(sp):
                sp.dma_start(eb_sb[:, :], biases.partition_broadcast(P)).then_inc(params_loaded, 16)
                sp.dma_start(b_sb[1:G, :], br).then_inc(params_loaded, 16)
                sp.dma_start(b_sb[0:1, :], bs[0:1, :]).then_inc(params_loaded, 16)
                for k in range(SHARED):
                    sp.dma_start(bs_sb[k][:, :], bs[k:k + 1, :]).then_inc(params_loaded, 16)

                def step(t):
                    new, old = t.plus(2), t.plus(-1)
                    if new.within():
                        if new.before(2):
                            sp.wait_ge(t_filled, 2 * (new.n - 2) + 1)
                        sp.dma_start(att_in[new.slot][:, :, :], att[new.n]).then_inc(att_loaded[new.slot], 16)
                        if new.before(2):
                            sp.wait_ge(xc_done, new.n - 1)
                        sp.dma_start(xb_in[new.slot][:, :, :], xb[new.n]).then_inc(xb_loaded[new.slot], 16)
                    if old.within():
                        sp.wait_ge(added, ADDS * (old.n + 1))
                        sp.dma_start(out[old.n], acc[old.slot][:, :, :]).then_inc(out_stored[old.slot], 16)

                pipeline(sp, step, 2, 1)
                for k in range(2):
                    sp.wait_ge(out_stored[k], 16 * (BATCHES // 2))

            @block.tensor
            def _(pe):
                pe.wait_ge(params_loaded, 16 * PARAMS)
                pe.wait_ge(ordered, 2)

                def turn(src):
                    for k in range(TT):
                        for dc in range(DC):
                            mm = nc.tensor.transpose(ps_t[:, dc, k * P:(k + 1) * P], src[:, k, dc * P:(dc + 1) * P], c.ident[:, :])
                    mm.then_inc(t_filled, 1)

                def product(to, rows_t, matrix):
                    for k in range(TT):
                        for dc in range(DC):
                            for r, m in PRODUCTS:
                                mm = nc.tensor.matmul(to[:, k, :], rows_t[:, r, dc, k * P:(k + 1) * P], matrix[:, m, dc, :],
                                                      start=(dc == 0 and r == m), stop=(dc == DC - 1 and r == LO))
                    return mm

                def pair_of_experts(t, q, k):
                    fill = TT * q + k
                    if fill >= RING or t.before(1):
                        pe.wait_ge(added, ADDS * t.n + 2 * TT * ((fill - RING) // TT + 1))
                    for dc in range(DC):
                        for r, m in PRODUCTS:
                            mm = nc.tensor.matmul(ps_e[fill % RING][:, :, :], u_hl[t.slot][:, r, dc, k * P:(k + 1) * P],
                                                  wr_hl[:, m, dc, 2 * q:2 * q + 2, :], start=(dc == 0 and r == m), stop=(dc == DC - 1 and r == LO))
                    mm.then_inc(e_filled, 1)

                def shared(t):
                    pe.wait_ge(s_emptied, 2 * (t.n + 1))
                    if t.before(1):
                        pe.wait_ge(b_emptied, t.n)
                    for k in range(TT):
                        nc.tensor.matmul(ps_b[:, k, :], probs_t[t.slot][:, k * P:(k + 1) * P], b_sb[:, :], start=True, stop=False)
                        for dc in range(DC):
                            for r, m in PRODUCTS:
                                mm = nc.tensor.matmul(ps_b[:, k, :], u_hl[t.slot][:, r, dc, k * P:(k + 1) * P], ws_hl[:, m, dc, :],
                                                      start=False, stop=(dc == DC - 1 and r == LO))
                    mm.then_inc(b_filled, 1)

                def front(t, q):
                    if q == 0:
                        pe.wait_ge(att_loaded[t.slot], 16 * (t.turn + 1))
                        if t.before(1):
                            pe.wait_ge(t_emptied, 2 * t.n)
                        turn(att_in[t.slot])
                    if q == XC_AT:
                        pe.wait_ge(t_emptied, 2 * t.n + 1)
                        if t.before(1):
                            pe.wait_ge(xc_done, t.n)
                        product(ps_c, att_hl[t.slot], wc_hl).then_inc(c_filled, 1)
                    if q == U_AT + 1:
                        pe.wait_ge(u_done, TT * (t.n + 1))
                        pe.wait_ge(t_emptied, 2 * t.n + 1)
                        turn(u[t.slot])
                    if q == CHOOSE_AT:
                        pe.wait_ge(t_emptied, 2 * t.n + 2)
                        if t.before(1):
                            pe.wait_ge(s_emptied, 2 * t.n)
                        product(ps_scores, u_hl[t.slot], cent_hl).then_inc(s_filled, 1)
                    if q == QUADS - 1:
                        pe.wait_ge(probs_done, t.n + 1)
                        pe.wait_ge(s_emptied, 2 * t.n + 1)
                        for k in range(TT):
                            mm = nc.tensor.transpose(ps_probs[:, k * P:(k + 1) * P], probs[t.slot][:, k, :], c.ident[:, :])
                        mm.then_inc(s_filled, 1)

                def step(t):
                    nxt = t.plus(1)
                    for q in range(QUADS):
                        if t.within():
                            if q == 0:
                                shared(t)
                            for k in range(TT):
                                pair_of_experts(t, q, k)
                        if nxt.within():
                            front(nxt, q)

                pipeline(pe, step, 1, 0)

            @block.scalar
            def _(act):
                def step(t):
                    nxt = t.plus(1)
                    if not nxt.within():
                        return
                    t = nxt
                    for k, to in enumerate((att_hl, u_hl)):
                        act.wait_ge(t_filled, 2 * t.n + k + 1)
                        if k == 0 and t.before(2):
                            act.wait_ge(c_filled, t.n - 1)
                        if k == 1 and t.before(2):
                            act.wait_ge(e_filled, FILLS * (t.n - 1))
                        nc.scalar.copy(to[t.slot][:, HI, :, :], ps_t[:, :, :]).then_inc(t_hi, 1)
                    act.wait_ge(stepped, STEPS * t.n + 6)
                    if t.before(1):
                        act.wait_ge(probs_done, t.n)
                    for k in range(TT):
                        ins = nc.scalar.activation(exps[:, k, :], score[:, k, :], ACT.Exp, bias=neg_top[:, k:k + 1])
                    ins.then_inc(exps_done, 1)
                    act.wait_ge(s_filled, 2 * t.n + 2)
                    if t.before(2):
                        act.wait_ge(b_filled, t.n - 1)
                    nc.scalar.copy(probs_t[t.slot][:, :], ps_probs).then_inc(s_emptied, 1)

                pipeline(act, step, 1, 0)

            @block.vector
            def _(dve):
                dve.wait_ge(params_loaded, 16 * PARAMS)
                nc.vector.tensor_tensor(bs_sb[0][:, :], bs_sb[0][:, :], bs_sb[1][:, :], ALU.add).then_inc(set_up, 1)
                nc.vector.tensor_scalar(b_sb[:, :], b_sb[:, :], LIFT, None, ALU.mult).then_inc(ordered, 1)
                dve.wait_ge(set_up, 2)
                dve.wait_ge(ordered, 1)
                nc.vector.tensor_scalar(b_sb[0:1, :], bs_sb[0][:, :], LIFT / SHARED, None, ALU.mult).then_inc(ordered, 1)
                for k in range(2):
                    ins = nc.vector.memset(probs[k][:, :, 0], 1.0)
                ins.then_inc(ordered, 1)

                def low_part(t, k, to):
                    dve.wait_ge(t_hi, 2 * t.n + k + 1)
                    nc.vector.tensor_tensor(to[t.slot][:, LO, :, :], ps_t[:, :, :], to[t.slot][:, HI, :, :],
                                            ALU.subtract).then_inc(t_emptied, 1)

                def add_pair(t, q):
                    for j in range(2):
                        for k in range(TT):
                            if j == 0:
                                dve.wait_ge(e_filled, FILLS * t.n + TT * q + k + 1)
                            at = TT * (2 * q + j) + k
                            if at >= TT:
                                dve.wait_ge(added, ADDS * t.n + at - TT + 1)
                            elif k == 0:
                                dve.wait_ge(b_emptied, t.n + 1)
                            nc.vector.scalar_tensor_tensor(acc[t.slot][:, k, :], ps_e[(TT * q + k) % RING][:, j, :],
                                                           shares[t.slot][:, k, 2 * q + j:2 * q + j + 1], acc[t.slot][:, k, :],
                                                           ALU.mult, ALU.add).then_inc(added, 1)

                def front(t, q):
                    if q == 0:
                        low_part(t, 0, att_hl)
                    if q == U_AT + 1:
                        low_part(t, 1, u_hl)
                    if q == XC_AT:
                        dve.wait_ge(c_filled, t.n + 1)
                        dve.wait_ge(xb_loaded[t.slot], 16 * (t.turn + 1))
                        if t.before(2):
                            dve.wait_ge(based, t.n - 1)
                        nc.vector.scalar_tensor_tensor(xc[t.slot][:, :, :], ps_c[:, :, :], 1 / LIFT, xb_in[t.slot][:, :, :],
                                                       ALU.mult, ALU.add).then_inc(xc_done, 1)
                        dve.wait_ge(xc_done, t.n + 1)
                        for k in range(TT):
                            ins = nc.vector.bn_stats(stats[:, k, :], xc[t.slot][:, k, :])
                        ins.then_inc(stepped, 1)
                        dve.wait_ge(stepped, STEPS * t.n + 1)
                        dve.sem_inc(stepped, 1)
                        for k in range(TT):
                            ins = nc.vector.bn_aggr(mv[:, k, :], stats[:, k, :])
                        ins.then_inc(stepped, 1)
                    if q == U_AT:
                        dve.wait_ge(rstd_done, t.n + 1)
                        if t.before(2):
                            dve.wait_ge(t_filled, 2 * (t.n - 1))
                        for k in range(TT):
                            nc.vector.tensor_scalar(u[t.slot][:, k, :], xc[t.slot][:, k, :], mv[:, k, 0:1], rstd[:, k:k + 1],
                                                    ALU.subtract, ALU.mult).then_inc(u_done, 1)
                    if q == CHOOSE_AT:
                        dve.wait_ge(s_filled, 2 * t.n + 1)
                        if t.before(1):
                            dve.wait_ge(exps_done, t.n)
                        nc.vector.scalar_tensor_tensor(score[:, :, :], ps_scores, 1 / LIFT, eb_sb[:, :].unsqueeze(1).to_broadcast([P, TT, E]),
                                                       ALU.mult, ALU.add).then_inc(s_emptied, 1)
                        dve.wait_ge(s_emptied, 2 * t.n + 1)
                        dve.sem_inc(stepped, 1)
                        for k in range(TT):
                            ins = nc.vector.max(top[:, k, :], score[:, k, :])
                        ins.then_inc(stepped, 1)
                        dve.wait_ge(stepped, STEPS * t.n + 5)
                        nc.vector.tensor_scalar(neg_top[:, :], top[:, :, 0], -1.0, None, ALU.mult).then_inc(stepped, 1)
                        for k in range(TT):
                            ins = nc.vector.max_index(top_at[:, k, :], top[:, k, :], score[:, k, :])
                        ins.then_inc(stepped, 1)
                        dve.wait_ge(stepped, STEPS * t.n + 7)
                        nc.vector.tensor_copy(chosen_at[:, :, :], top_at[:, :, 0:2]).then_inc(stepped, 1)
                        dve.wait_ge(stepped, STEPS * t.n + 8)
                        for k in range(2):
                            ins = nc.vector.tensor_tensor(chosen[k][:, :, :], numbers[:, :].unsqueeze(1).to_broadcast([P, TT, E]),
                                                          chosen_at[:, :, k:k + 1].to_broadcast([P, TT, E]), ALU.is_equal)
                        ins.then_inc(stepped, 1)
                        dve.wait_ge(stepped, STEPS * t.n + 9)
                        nc.vector.tensor_tensor(chosen[0][:, :, :], chosen[0][:, :, :], chosen[1][:, :, :], ALU.add).then_inc(stepped, 1)
                    if q == CHOOSE_AT + 1:
                        dve.wait_ge(exps_done, t.n + 1)
                        nc.vector.tensor_reduce(exp_sum[:, :], exps[:, :, :], AX.X, ALU.add).then_inc(ordered, 1)
                        dve.wait_ge(ordered, 3 * t.n + 4)
                        nc.vector.reciprocal(recip[:, :], exp_sum[:, :]).then_inc(ordered, 1)
                        dve.wait_ge(stepped, STEPS * (t.n + 1))
                        nc.vector.tensor_tensor(chosen[0][:, :, :], chosen[0][:, :, :], exps[:, :, :], ALU.mult).then_inc(ordered, 1)
                        dve.wait_ge(ordered, 3 * t.n + 6)
                        if t.before(2):
                            dve.wait_ge(added, ADDS * (t.n - 1))
                            dve.wait_ge(s_filled, 2 * (t.n - 1))
                        nc.vector.tensor_tensor(probs[t.slot][:, :, 1:G], chosen[0][:, :, :],
                                                recip[:, :].unsqueeze(2).to_broadcast([P, TT, E]), ALU.mult).then_inc(probs_done, 1)
                        dve.wait_ge(probs_done, t.n + 1)
                        nc.vector.tensor_scalar(shares[t.slot][:, :, :], probs[t.slot][:, :, 1:G], 1 / LIFT, None,
                                                ALU.mult).then_inc(shared_out, 1)

                def step(t):
                    nxt = t.plus(1)
                    if t.within():
                        dve.wait_ge(b_filled, t.n + 1)
                        dve.wait_ge(based, t.n + 1)
                        if t.before(2):
                            dve.wait_ge(out_stored[t.slot], 16 * t.turn)
                        nc.vector.scalar_tensor_tensor(acc[t.slot][:, :, :], ps_b[:, :, :], 1 / LIFT, base[t.slot][:, :, :],
                                                       ALU.mult, ALU.add).then_inc(b_emptied, 1)
                        dve.wait_ge(shared_out, t.n + 1)
                    for q in range(QUADS):
                        if t.within():
                            add_pair(t, q)
                        if nxt.within():
                            front(nxt, q)

                pipeline(dve, step, 1, 0)

            @block.gpsimd
            def _(pool):
                nc.gpsimd.iota(numbers[:, :], [[1, E]], 0, 0, allow_small_or_imprecise_dtypes=True).then_inc(set_up, 1)

                def step(t):
                    if t.before(1):
                        pool.wait_ge(rstd_done, t.n)
                    pool.wait_ge(stepped, STEPS * t.n + 3)
                    nc.gpsimd.tensor_tensor(var[:, :], mv[:, :, 1], c.eps[:, :], ALU.add).then_inc(var_done, 1)
                    pool.wait_ge(var_done, t.n + 1)
                    nc.gpsimd.tensor_tensor(rstd[:, :], var[:, :], c.minus_half[:, :], ALU.pow).then_inc(rstd_done, 1)
                    pool.wait_ge(u_done, TT * (t.n + 1))
                    if t.before(2):
                        pool.wait_ge(b_emptied, t.n - 1)
                    nc.gpsimd.tensor_tensor(base[t.slot][:, :, :], xc[t.slot][:, :, :], u[t.slot][:, :, :], ALU.add).then_inc(based, 1)

                pipeline(pool, step, 0, 0)


def program(nc, i, out):
    ctx = ExitStack()
    with ctx:
        def sb(name, shape, dt=F32):
            return ctx.enter_context(nc.sbuf_tensor(name, shape, dt))

        def dram(name, shape, dt=F32):
            return nc.dram_tensor(name, shape, dt, kind="Internal").ap()

        c = Constants(sb)
        E = i["gate"].shape[1]
        tiles = (2 * TOKENS + E * (SEQ - 1)) // SEQ
        xs, ys = dram("xs", [tiles * SEQ, D]), dram("ys", [tiles * SEQ, D])
        zeroed = ctx.enter_context(nc.semaphore("zeroed"))
        constants(nc, c, ctx.enter_context(nc.semaphore("constants_done")))
        rows = [BATCHES, P, TT, D]
        h0 = dram("h0", rows)
        table = dram("table", [TOKENS, MEM_WORDS])

        def parts(name, cols, rows=D):
            return sb(name, [P, 2, rows // P] + cols, F16)

        width, routed = i["w1"].shape[1] // DC, i["br"].shape[0]
        w1_hl, w2_hl = parts("w1_hl", [width]), parts("w2_hl", [D], width)
        wc_hl, ws_hl, cent_hl = parts("wc_hl", [D]), parts("ws_hl", [D]), parts("cent_hl", [routed])
        wr_hl = parts("wr_hl", [routed, D])
        projections = {n: parts(n, [D]) for n in ("wq1", "wk1", "wv1", "wq2", "wk2", "wv2", "mem_wq")}
        ctx_hl = dram("ctx_hl", [2, D, TOKENS], F16)
        prepare(nc, c, i["x"], h0, i["ctx_t"], ctx_hl, i["mem_wkv"], table,
                tuple((i[n], hl[:, :, :, :].rearrange("p l c f -> p l (c f)")) for n, hl in projections.items()) +
                ((i["w1"], w1_hl[:, :, :, :].rearrange("p l c f -> p l (c f)")), (i["w2"], w2_hl[:, :, :, :].rearrange("p l c f -> p l (c f)")),
                 (i["mem_wc"], wc_hl[:, :, :, :].rearrange("p l c f -> p l (c f)")),
                 (i["centroids"], cent_hl[:, :, :, :].rearrange("p l c f -> p l (c f)")),
                 (i["mix_wr"], wr_hl[:, :, :, :, :].rearrange("p l c e f -> p l (c e f)"))),
                i["mix_ws"], ws_hl[:, :, :, :].rearrange("p l c f -> p l (c f)"))
        x1 = dram("x1", rows)
        attention(nc, c, "self", True, h0, [projections[n] for n in ("wq1", "wk1", "wv1")], x1, None,
                  i["L0_xattn_bv1"], i["L0_xattn_g1"], i["L0_xattn_be1"])
        x2 = dram("x2", rows)
        attention(nc, c, "cross", False, x1, [projections[n] for n in ("wq2", "wk2", "wv2")], x2, ctx_hl,
                  i["L0_xattn_bv2"], i["L0_xattn_g2"], i["L0_xattn_be2"])
        clear_counted(nc, c)
        xa, hm = dram("xa", rows), dram("hm", rows)
        logits = sb("logits", [P, BATCHES * TT, E])
        feed_forward(nc, c, x2, i["x"], w1_hl, i["bf1"], w2_hl, i["L0_xattn_bf2"], i["L0_xattn_g3"], i["L0_xattn_be3"],
    i["gate"], xa, hm, logits, xs, zeroed)
        shares, slots = sb("shares", [P, 2, BATCHES * TT]), sb("slots", [P, 2, BATCHES * TT], I32)
        tile_expert = sb("tile_expert", [1, tiles], I32)
        route(nc, c, logits, hm, xs, shares, slots, tile_expert, zeroed)
        experts(nc, c, xs, i["moe_w13"], i["moe_w2"], tile_expert, ys)
        xb, h2 = dram("xb", rows), dram("h2", rows)
        combine(nc, c, xa, ys, shares, slots, xb, h2)
        clear_counted(nc, c)
        att = dram("att", rows)
        attention(nc, c, "memory", False, h2, [projections["mem_wq"]], att, ctx_hl, memory=table)
        mixture(nc, c, att, wc_hl, xb, cent_hl, i["expert_biases"], wr_hl, i["br"], ws_hl, i["bs"],
                out.rearrange("b (t p) d -> b p t d", p=P))


def kernel(**inputs):
    import numpy as np
    import concourse.bacc as bacc
    from concourse.bass_utils import run_bass_kernel_spmd

    a = {k: np.asarray(x) for k, x in inputs.items()}

    def heads_last(w):
        return np.ascontiguousarray(w.transpose(1, 0, 2).reshape(D, D))

    def on_partitions(w):
        return w.reshape(w.shape[0] // P, P, -1).transpose(1, 0, 2).reshape(P, -1)

    laid = {"x": a["x"].reshape(TOKENS, D), "ctx_t": np.ascontiguousarray(a["ctx_1024"].reshape(TOKENS, D).T)}
    for n in "12":
        for w in "qkv":
            laid[f"w{w}{n}"] = on_partitions(heads_last(a[f"L0_xattn_W{w}{n}"]))
        laid[f"L0_xattn_bv{n}"] = a[f"L0_xattn_bv{n}"].reshape(D)
    for n in "123":
        laid[f"L0_xattn_g{n}"] = a[f"L0_xattn_g{n}"]
        laid[f"L0_xattn_be{n}"] = a[f"L0_xattn_be{n}"]
    laid["L0_xattn_bf2"] = a["L0_xattn_bf2"]

    laid["w1"], laid["w2"] = on_partitions(a["L0_xattn_Wf1"]), on_partitions(a["L0_xattn_Wf2"])
    laid["bf1"] = a["L0_xattn_bf1"].reshape(-1, P).T
    laid["gate"] = a["L0_ffn_gate_w"].T

    def by_partition(w):
        e, o, n = w.shape
        return w.transpose(0, 2, 1).reshape(e, n // P, P, o).transpose(0, 2, 1, 3)

    E = a["L0_ffn_W1"].shape[0]
    laid["moe_w13"] = np.stack([by_partition(a["L0_ffn_W1"]), by_partition(a["L0_ffn_W3"])], axis=2).reshape(E, P, -1)
    laid["moe_w2"] = by_partition(a["L0_ffn_W2"])

    laid["mem_wq"], laid["mem_wkv"] = on_partitions(a["L1_xattn_Wq"].T), a["L1_xattn_Wkv"].T
    laid["mem_wc"], laid["centroids"] = on_partitions(a["L1_xattn_Wc"].T), on_partitions(a["L1_ffn_centroids"].T)
    laid["mix_wr"] = on_partitions(a["L1_ffn_Wr"].transpose(2, 0, 1).reshape(D, -1))
    laid["mix_ws"] = np.stack([on_partitions(w.T) for w in a["L1_ffn_Ws"]])
    for n in ("expert_biases", "br", "bs"):
        laid[n] = a[f"L1_ffn_{n}"]

    nc = bacc.Bacc("TRN2", target_bir_lowering=False, num_devices=1)
    arrays = {f"in_{k}": np.ascontiguousarray(x) for k, x in laid.items()}
    i = {k: nc.dram_tensor(f"in_{k}", x.shape, mybir.dt.from_np(x.dtype), kind="ExternalInput").ap()
         for k, x in laid.items()}
    out = nc.dram_tensor("out", (BATCHES, SEQ, D), F32, kind="ExternalOutput").ap()
    program(nc, i, out)
    r = run_bass_kernel_spmd(nc, [arrays], core_ids=[0])
    return r.results[0]["out"]
```
